# Optimizing a Trainium2 kernel written in Bass

```python
import numpy as np
import jax
import jax.numpy as jnp

def _softmax(x, axis=-1):
    return jax.nn.softmax(x, axis=axis)

def _gelu(x):
    return jax.nn.gelu(x, approximate=True)

def _silu(x):
    return jax.nn.silu(x)

def _sigmoid(x):
    return jax.nn.sigmoid(x)

def _layernorm(x, axis=-1, eps=1e-05):
    m = jnp.mean(x, axis=axis, keepdims=True)
    v = jnp.var(x, axis=axis, keepdims=True)
    return (x - m) / jnp.sqrt(v + eps)

def _scatter_add(tgt, idx, src, axis=0):
    return tgt.at[idx].add(src)

def _segment_sum(src, seg, n):
    return jax.ops.segment_sum(src, seg, n)
kernel_name = 'mk_decoder_preln_d2_seqx_r8_193361'

def setup_inputs(seed: int=0):
    np.random.seed(seed)
    _w = jnp.asarray

    def _rec_inputs():
        import jax
        import jax.numpy as jnp
        _rk = jax.random.key(seed)
        x = -7.109e-05 + 0.9999 * jax.random.normal(jax.random.fold_in(_rk, 1), (4, 256, 256), jnp.float32)
        _lenS = 256 - jax.random.randint(jax.random.fold_in(_rk, 7), (4,), 0, max(1, 256 // 4) + 1, jnp.int32)
        _lenS2 = 256 - jax.random.randint(jax.random.fold_in(_rk, 8), (4,), 0, max(1, 256 // 4) + 1, jnp.int32)
        _ctx_512P = jax.random.normal(jax.random.fold_in(_rk, 11), (4, 16, 64), jnp.float32)
        _ctx_512c = jax.random.dirichlet(jax.random.fold_in(_rk, 511), 0.3 * jnp.ones((16,), jnp.float32), (4, 256))
        _ctx_512t = jnp.einsum('bsk,bkd->bsd', _ctx_512c, _ctx_512P)
        _ctx_512t = _ctx_512t * jax.lax.rsqrt(jnp.mean(jnp.square(_ctx_512t)) + 1e-12) * 0.953939
        ctx_512 = 2.81802e-05 + 1.00001 * (_ctx_512t + 0.3 * jax.random.normal(jax.random.fold_in(_rk, 611), (4, 256, 64), jnp.float32))
        return (x, ctx_512)
    x, ctx_512 = _rec_inputs()

    def _L0_attn_setup():
        import math
        import jax, jax.numpy as jnp
        import numpy as np
        B, S, HID = (2, 128, 256)
        H, D, R = (16, 128, 64)
        KVC, QC = (64, 192)
        MAX_POS = 512

        def _lin(x, w, b):
            return x @ w.T + b

        def _rotate_half(x):
            x1, x2 = (x[..., :x.shape[-1] // 2], x[..., x.shape[-1] // 2:])
            return jnp.concatenate([-x2, x1], axis=-1)

        def _rope_tables(dim, end, theta=10000.0):
            freqs = 1.0 / theta ** (jnp.arange(0, dim, 2)[:dim // 2].astype(jnp.float32) / dim)
            f = jnp.outer(jnp.arange(end, dtype=jnp.float32), freqs)
            cos, sin = (jnp.cos(f), jnp.sin(f))
            return (jnp.concatenate([cos, cos], -1), jnp.concatenate([sin, sin], -1))

        def _reference_tuple_inner(hidden_states, W_DKV_w, W_DKV_b, W_UK_w, W_UK_b, W_UV_w, W_UV_b, W_KR_w, W_KR_b, W_DQ_w, W_DQ_b, W_UQ_w, W_UQ_b, W_QR_w, W_QR_b, W_O_w, W_O_b):
            b, s = hidden_states.shape[:2]
            c_kv = _lin(hidden_states, W_DKV_w, W_DKV_b)
            k = _lin(c_kv, W_UK_w, W_UK_b).reshape(b, s, H, D)
            v = _lin(c_kv, W_UV_w, W_UV_b).reshape(b, s, H, D)
            c_q = _lin(hidden_states, W_DQ_w, W_DQ_b)
            q = _lin(c_q, W_UQ_w, W_UQ_b).reshape(b, s, H, D)
            k_r = _lin(k, W_KR_w, W_KR_b)
            q_r = _lin(q, W_QR_w, W_QR_b)
            cos, sin = _rope_tables(R, MAX_POS)
            cos_p = cos[:s][:, None, :]
            sin_p = sin[:s][:, None, :]
            q_r = q_r * cos_p + _rotate_half(q_r) * sin_p
            k_r = k_r * cos_p + _rotate_half(k_r) * sin_p
            scale = 1.0 / math.sqrt(D)
            scores = jnp.einsum('bqhd,bkhd->bhqk', q, k) * scale
            probs = jax.nn.softmax(scores, axis=-1)
            attn = jnp.einsum('bhqk,bkhd->bqhd', probs, v).reshape(b, s, H * D)
            output = _lin(attn, W_O_w, W_O_b)
            return (output, c_kv, k_r)
        key = jax.random.key(seed)
        ks = jax.random.split(key, 17)
        w = lambda k, shape: jax.random.normal(k, shape, jnp.float32) * 0.02
        return {'hidden_states': jax.random.normal(ks[0], (B, S, HID), jnp.float32), 'W_DKV_w': w(ks[1], (KVC, HID)), 'W_DKV_b': w(ks[2], (KVC,)), 'W_UK_w': w(ks[3], (H * D, KVC)), 'W_UK_b': w(ks[4], (H * D,)), 'W_UV_w': w(ks[5], (H * D, KVC)), 'W_UV_b': w(ks[6], (H * D,)), 'W_KR_w': w(ks[7], (R, D)), 'W_KR_b': w(ks[8], (R,)), 'W_DQ_w': w(ks[9], (QC, HID)), 'W_DQ_b': w(ks[10], (QC,)), 'W_UQ_w': w(ks[11], (H * D, QC)), 'W_UQ_b': w(ks[12], (H * D,)), 'W_QR_w': w(ks[13], (R, D)), 'W_QR_b': w(ks[14], (R,)), 'W_O_w': w(ks[15], (HID, H * D)), 'W_O_b': w(ks[16], (HID,))}
    _L0_attn_all = _L0_attn_setup()
    _L0_attn_in = {k: v for k, v in _L0_attn_all.items() if k in ('W_DKV_w', 'W_DKV_b', 'W_UK_w', 'W_UK_b', 'W_UV_w', 'W_UV_b', 'W_KR_w', 'W_KR_b', 'W_DQ_w', 'W_DQ_b', 'W_UQ_w', 'W_UQ_b', 'W_QR_w', 'W_QR_b', 'W_O_w', 'W_O_b')}
    del _L0_attn_all

    def _L0_xattn_setup():
        import jax, jax.numpy as jnp
        import numpy as np
        EPS = 1e-06
        IMAGE_DIMS = 256
        key = jax.random.key(seed)
        k1, k2, k3 = jax.random.split(key, 3)
        B, I, J, D = (16, 256, 256, 64)
        p = jax.random.normal(k1, (B, I, J), dtype=jnp.float32)
        k_v = jax.random.normal(k2, (B, J, D), dtype=jnp.float32)
        W_k = jax.random.normal(k3, (D, D), dtype=jnp.float32) * (1.0 / np.sqrt(D))
        b_k = jnp.zeros((D,), dtype=jnp.float32)
        ln_gamma = jnp.ones((J,), dtype=jnp.float32)
        ln_beta = jnp.zeros((J,), dtype=jnp.float32)
        return {'p': p, 'k_v': k_v, 'W_k': W_k, 'b_k': b_k, 'ln_gamma': ln_gamma, 'ln_beta': ln_beta}
    _L0_xattn_all = _L0_xattn_setup()
    _L0_xattn_in = {k: v for k, v in _L0_xattn_all.items() if k in ('W_k', 'b_k', 'ln_gamma', 'ln_beta')}
    del _L0_xattn_all

    def _L0_ffn_setup():
        import jax, jax.numpy as jnp
        import numpy as np
        CAPACITY = 0.125
        HEAD_DIM = 128
        N_HEADS = 16
        N_KV_HEADS = 8
        ROPE_THETA = 10000.0
        EPS = 1e-06

        def _rms_norm(x, w):
            return x * jax.lax.rsqrt(jnp.mean(x * x, axis=-1, keepdims=True) + EPS) * w

        def _rotate_half(t):
            h = t.shape[-1] // 2
            return jnp.concatenate([-t[..., h:], t[..., :h]], axis=-1)
        key = jax.random.key(seed)
        ks = jax.random.split(key, 12)
        B, T, D = (4, 512, 256)
        I = 1024
        s = 0.02
        return {'hidden_states': jax.random.normal(ks[0], (B, T, D), jnp.float32), 'w_router': jax.random.normal(ks[1], (D,), jnp.float32) * s, 'wq': jax.random.normal(ks[2], (D, N_HEADS * HEAD_DIM), jnp.float32) * s, 'bq': jnp.zeros((N_HEADS * HEAD_DIM,), jnp.float32), 'wk': jax.random.normal(ks[3], (D, N_KV_HEADS * HEAD_DIM), jnp.float32) * s, 'bk': jnp.zeros((N_KV_HEADS * HEAD_DIM,), jnp.float32), 'wv': jax.random.normal(ks[4], (D, N_KV_HEADS * HEAD_DIM), jnp.float32) * s, 'bv': jnp.zeros((N_KV_HEADS * HEAD_DIM,), jnp.float32), 'wo': jax.random.normal(ks[5], (N_HEADS * HEAD_DIM, D), jnp.float32) * s, 'w_gate': jax.random.normal(ks[6], (D, I), jnp.float32) * s, 'w_up': jax.random.normal(ks[7], (D, I), jnp.float32) * s, 'w_down': jax.random.normal(ks[8], (I, D), jnp.float32) * s, 'ln1_w': jnp.ones((D,), jnp.float32), 'ln2_w': jnp.ones((D,), jnp.float32)}
    _L0_ffn_all = _L0_ffn_setup()
    _L0_ffn_in = {k: v for k, v in _L0_ffn_all.items() if k in ('w_router', 'wq', 'bq', 'wk', 'bk', 'wv', 'bv', 'wo', 'w_gate', 'w_up', 'w_down', 'ln1_w', 'ln2_w')}
    del _L0_ffn_all

    def _L1_attn_setup():
        import jax, jax.numpy as jnp
        import numpy as np
        B, N, C, H = (4, 256, 256, 16)
        DH = C // H
        key = jax.random.key(seed)
        ks = jax.random.split(key, 5)
        s = 0.02
        return {'x': jax.random.normal(ks[0], (B, N, C), dtype=jnp.float32), 'w_qkv': jax.random.normal(ks[1], (3 * C, C), dtype=jnp.float32) * s, 'b_qkv': jax.random.normal(ks[2], (3 * C,), dtype=jnp.float32) * s, 'w_out': jax.random.normal(ks[3], (C, C), dtype=jnp.float32) * s, 'b_out': jax.random.normal(ks[4], (C,), dtype=jnp.float32) * s}
    _L1_attn_all = _L1_attn_setup()
    _L1_attn_in = {k: v for k, v in _L1_attn_all.items() if k in ('w_qkv', 'b_qkv', 'w_out', 'b_out')}
    del _L1_attn_all

    def _L1_xattn_setup():
        import jax, jax.numpy as jnp
        import numpy as np
        B, S, H, NH, L = (2, 256, 256, 16, 64)
        HD = H // NH
        key = jax.random.key(seed)
        k1, k2, k3, k4, k5 = jax.random.split(key, 5)
        scale = 0.02
        return {'q': jax.random.normal(k1, (B, S, H), dtype=jnp.float32), 'latent_kv': jax.random.normal(k2, (B, S, L), dtype=jnp.float32), 'Wq': jax.random.normal(k3, (H, H), dtype=jnp.float32) * scale, 'Wkv_expand': jax.random.normal(k4, (2 * H, L), dtype=jnp.float32) * scale, 'Wout': jax.random.normal(k5, (H, H), dtype=jnp.float32) * scale}
    _L1_xattn_all = _L1_xattn_setup()
    _L1_xattn_in = {k: v for k, v in _L1_xattn_all.items() if k in ('Wq', 'Wkv_expand', 'Wout')}
    del _L1_xattn_all

    def _L1_ffn_setup():
        import jax, jax.numpy as jnp
        import numpy as np
        TOP_K = 6
        key = jax.random.key(seed)
        k1, k2, k3, k4, k5 = jax.random.split(key, 5)
        B, S, H = (2, 256, 256)
        E, M = (28, 176)
        scale = 0.02
        return {'hidden_states': jax.random.normal(k1, (B, S, H), jnp.float32), 'gate_weight': jax.random.normal(k2, (E, H), jnp.float32) * scale, 'w_gate': jax.random.normal(k3, (E, H, M), jnp.float32) * scale, 'w_up': jax.random.normal(k4, (E, H, M), jnp.float32) * scale, 'w_down': jax.random.normal(k5, (E, M, H), jnp.float32) * scale}
    _L1_ffn_all = _L1_ffn_setup()
    _L1_ffn_in = {k: v for k, v in _L1_ffn_all.items() if k in ('gate_weight', 'w_gate', 'w_up', 'w_down')}
    del _L1_ffn_all
    return {'x': x, 'ctx_512': ctx_512, 'L0_attn_W_DKV_w': _L0_attn_in['W_DKV_w'], 'L0_attn_W_DKV_b': _L0_attn_in['W_DKV_b'], 'L0_attn_W_UK_w': _L0_attn_in['W_UK_w'], 'L0_attn_W_UK_b': _L0_attn_in['W_UK_b'], 'L0_attn_W_UV_w': _L0_attn_in['W_UV_w'], 'L0_attn_W_UV_b': _L0_attn_in['W_UV_b'], 'L0_attn_W_KR_w': _L0_attn_in['W_KR_w'], 'L0_attn_W_KR_b': _L0_attn_in['W_KR_b'], 'L0_attn_W_DQ_w': _L0_attn_in['W_DQ_w'], 'L0_attn_W_DQ_b': _L0_attn_in['W_DQ_b'], 'L0_attn_W_UQ_w': _L0_attn_in['W_UQ_w'], 'L0_attn_W_UQ_b': _L0_attn_in['W_UQ_b'], 'L0_attn_W_QR_w': _L0_attn_in['W_QR_w'], 'L0_attn_W_QR_b': _L0_attn_in['W_QR_b'], 'L0_attn_W_O_w': _L0_attn_in['W_O_w'], 'L0_attn_W_O_b': _L0_attn_in['W_O_b'], 'L0_xattn_W_k': _L0_xattn_in['W_k'], 'L0_xattn_b_k': _L0_xattn_in['b_k'], 'L0_xattn_ln_gamma': _L0_xattn_in['ln_gamma'], 'L0_xattn_ln_beta': _L0_xattn_in['ln_beta'], 'L0_ffn_w_router': _L0_ffn_in['w_router'], 'L0_ffn_wq': _L0_ffn_in['wq'], 'L0_ffn_bq': _L0_ffn_in['bq'], 'L0_ffn_wk': _L0_ffn_in['wk'], 'L0_ffn_bk': _L0_ffn_in['bk'], 'L0_ffn_wv': _L0_ffn_in['wv'], 'L0_ffn_bv': _L0_ffn_in['bv'], 'L0_ffn_wo': _L0_ffn_in['wo'], 'L0_ffn_w_gate': _L0_ffn_in['w_gate'], 'L0_ffn_w_up': _L0_ffn_in['w_up'], 'L0_ffn_w_down': _L0_ffn_in['w_down'], 'L0_ffn_ln1_w': _L0_ffn_in['ln1_w'], 'L0_ffn_ln2_w': _L0_ffn_in['ln2_w'], 'L1_attn_w_qkv': _L1_attn_in['w_qkv'], 'L1_attn_b_qkv': _L1_attn_in['b_qkv'], 'L1_attn_w_out': _L1_attn_in['w_out'], 'L1_attn_b_out': _L1_attn_in['b_out'], 'L1_xattn_Wq': _L1_xattn_in['Wq'], 'L1_xattn_Wkv_expand': _L1_xattn_in['Wkv_expand'], 'L1_xattn_Wout': _L1_xattn_in['Wout'], 'L1_ffn_gate_weight': _L1_ffn_in['gate_weight'], 'L1_ffn_w_gate': _L1_ffn_in['w_gate'], 'L1_ffn_w_up': _L1_ffn_in['w_up'], 'L1_ffn_w_down': _L1_ffn_in['w_down']}

def reference(x, ctx_512, L0_attn_W_DKV_w, L0_attn_W_DKV_b, L0_attn_W_UK_w, L0_attn_W_UK_b, L0_attn_W_UV_w, L0_attn_W_UV_b, L0_attn_W_KR_w, L0_attn_W_KR_b, L0_attn_W_DQ_w, L0_attn_W_DQ_b, L0_attn_W_UQ_w, L0_attn_W_UQ_b, L0_attn_W_QR_w, L0_attn_W_QR_b, L0_attn_W_O_w, L0_attn_W_O_b, L0_xattn_W_k, L0_xattn_b_k, L0_xattn_ln_gamma, L0_xattn_ln_beta, L0_ffn_w_router, L0_ffn_wq, L0_ffn_bq, L0_ffn_wk, L0_ffn_bk, L0_ffn_wv, L0_ffn_bv, L0_ffn_wo, L0_ffn_w_gate, L0_ffn_w_up, L0_ffn_w_down, L0_ffn_ln1_w, L0_ffn_ln2_w, L1_attn_w_qkv, L1_attn_b_qkv, L1_attn_w_out, L1_attn_b_out, L1_xattn_Wq, L1_xattn_Wkv_expand, L1_xattn_Wout, L1_ffn_gate_weight, L1_ffn_w_gate, L1_ffn_w_up, L1_ffn_w_down):
    import jax
    import jax.numpy as jnp

    def _L0_attn_ref(hidden_states, W_DKV_w, W_DKV_b, W_UK_w, W_UK_b, W_UV_w, W_UV_b, W_KR_w, W_KR_b, W_DQ_w, W_DQ_b, W_UQ_w, W_UQ_b, W_QR_w, W_QR_b, W_O_w, W_O_b):
        import math
        import jax, jax.numpy as jnp
        import numpy as np
        B, S, HID = (2, 128, 256)
        H, D, R = (16, 128, 64)
        KVC, QC = (64, 192)
        MAX_POS = 512

        def _lin(x, w, b):
            return x @ w.T + b

        def _rotate_half(x):
            x1, x2 = (x[..., :x.shape[-1] // 2], x[..., x.shape[-1] // 2:])
            return jnp.concatenate([-x2, x1], axis=-1)

        def _rope_tables(dim, end, theta=10000.0):
            freqs = 1.0 / theta ** (jnp.arange(0, dim, 2)[:dim // 2].astype(jnp.float32) / dim)
            f = jnp.outer(jnp.arange(end, dtype=jnp.float32), freqs)
            cos, sin = (jnp.cos(f), jnp.sin(f))
            return (jnp.concatenate([cos, cos], -1), jnp.concatenate([sin, sin], -1))

        def _reference_tuple_inner(hidden_states, W_DKV_w, W_DKV_b, W_UK_w, W_UK_b, W_UV_w, W_UV_b, W_KR_w, W_KR_b, W_DQ_w, W_DQ_b, W_UQ_w, W_UQ_b, W_QR_w, W_QR_b, W_O_w, W_O_b):
            b, s = hidden_states.shape[:2]
            c_kv = _lin(hidden_states, W_DKV_w, W_DKV_b)
            k = _lin(c_kv, W_UK_w, W_UK_b).reshape(b, s, H, D)
            v = _lin(c_kv, W_UV_w, W_UV_b).reshape(b, s, H, D)
            c_q = _lin(hidden_states, W_DQ_w, W_DQ_b)
            q = _lin(c_q, W_UQ_w, W_UQ_b).reshape(b, s, H, D)
            k_r = _lin(k, W_KR_w, W_KR_b)
            q_r = _lin(q, W_QR_w, W_QR_b)
            cos, sin = _rope_tables(R, MAX_POS)
            cos_p = cos[:s][:, None, :]
            sin_p = sin[:s][:, None, :]
            q_r = q_r * cos_p + _rotate_half(q_r) * sin_p
            k_r = k_r * cos_p + _rotate_half(k_r) * sin_p
            scale = 1.0 / math.sqrt(D)
            scores = jnp.einsum('bqhd,bkhd->bhqk', q, k) * scale
            probs = jax.nn.softmax(scores, axis=-1)
            attn = jnp.einsum('bhqk,bkhd->bqhd', probs, v).reshape(b, s, H * D)
            output = _lin(attn, W_O_w, W_O_b)
            return (output, c_kv, k_r)
        return _reference_tuple_inner(hidden_states, W_DKV_w, W_DKV_b, W_UK_w, W_UK_b, W_UV_w, W_UV_b, W_KR_w, W_KR_b, W_DQ_w, W_DQ_b, W_UQ_w, W_UQ_b, W_QR_w, W_QR_b, W_O_w, W_O_b)[0]

    def _L0_xattn_ref(p, k_v, W_k, b_k, ln_gamma, ln_beta):
        import jax, jax.numpy as jnp
        import numpy as np
        EPS = 1e-06
        IMAGE_DIMS = 256
        kv = k_v @ W_k.T + b_k
        out = jnp.einsum('bij,bjd->bid', p, kv)
        scale = IMAGE_DIMS ** (-0.5)
        sim = jnp.einsum('bid,bjd->bij', out, kv) * scale
        mu = jnp.mean(sim, axis=-1, keepdims=True)
        var = jnp.var(sim, axis=-1, keepdims=True)
        sim = (sim - mu) * jax.lax.rsqrt(var + EPS) * ln_gamma + ln_beta
        attn = jax.nn.softmax(sim, axis=-1)
        return attn

    def _L0_ffn_ref(hidden_states, w_router, wq, bq, wk, bk, wv, bv, wo, w_gate, w_up, w_down, ln1_w, ln2_w):
        import jax, jax.numpy as jnp
        import numpy as np
        CAPACITY = 0.125
        HEAD_DIM = 128
        N_HEADS = 16
        N_KV_HEADS = 8
        ROPE_THETA = 10000.0
        EPS = 1e-06

        def _rms_norm(x, w):
            return x * jax.lax.rsqrt(jnp.mean(x * x, axis=-1, keepdims=True) + EPS) * w

        def _rotate_half(t):
            h = t.shape[-1] // 2
            return jnp.concatenate([-t[..., h:], t[..., :h]], axis=-1)
        B, T, D = hidden_states.shape
        k = max(1, int(T * CAPACITY))
        scores = jnp.einsum('btd,d->bt', hidden_states, w_router)
        _, idx = jax.lax.top_k(scores, k)
        idx = jnp.sort(idx, axis=-1)
        b = jnp.arange(B)[:, None]
        sel = hidden_states[b, idx]
        sel_scores = scores[b, idx]
        S = B * k
        x = sel.reshape(S, D)
        pos = idx.reshape(S)
        inv_freq = 1.0 / ROPE_THETA ** (jnp.arange(0, HEAD_DIM, 2, dtype=jnp.float32) / HEAD_DIM)
        ang = pos.astype(jnp.float32)[:, None] * inv_freq
        cos = jnp.concatenate([jnp.cos(ang), jnp.cos(ang)], axis=-1)[:, None, :]
        sin = jnp.concatenate([jnp.sin(ang), jnp.sin(ang)], axis=-1)[:, None, :]
        h = _rms_norm(x, ln1_w)
        q = (h @ wq + bq).reshape(S, N_HEADS, HEAD_DIM)
        kk = (h @ wk + bk).reshape(S, N_KV_HEADS, HEAD_DIM)
        v = (h @ wv + bv).reshape(S, N_KV_HEADS, HEAD_DIM)
        q = q * cos + _rotate_half(q) * sin
        kk = kk * cos + _rotate_half(kk) * sin
        rep = N_HEADS // N_KV_HEADS
        kk = jnp.repeat(kk, rep, axis=1)
        v = jnp.repeat(v, rep, axis=1)
        att = jnp.einsum('shd,thd->hst', q, kk) / np.sqrt(HEAD_DIM)
        causal = jnp.tril(jnp.ones((S, S), bool))
        att = jnp.where(causal[None], att, jnp.finfo(att.dtype).min)
        att = jax.nn.softmax(att, axis=-1)
        attn_out = jnp.einsum('hst,thd->shd', att, v).reshape(S, N_HEADS * HEAD_DIM) @ wo
        x1 = x + attn_out
        h2 = _rms_norm(x1, ln2_w)
        mlp = jax.nn.silu(h2 @ w_gate) * (h2 @ w_up) @ w_down
        processed = x1 + mlp
        gate = jax.nn.sigmoid(sel_scores).reshape(S, 1)
        gated = gate * processed + (1.0 - gate) * x
        output = hidden_states.at[b, idx].set(gated.reshape(B, k, D))
        return output

    def _L1_attn_ref(x, w_qkv, b_qkv, w_out, b_out):
        import jax, jax.numpy as jnp
        import numpy as np
        B, N, C, H = (4, 256, 256, 16)
        DH = C // H
        b, n, c = x.shape
        qkv = x @ w_qkv.T + b_qkv
        qkv = qkv.reshape(b, n, 3, H, c // H)
        q, k, v = (qkv[:, :, 0], qkv[:, :, 1], qkv[:, :, 2])
        attn = jnp.einsum('bnhd,bngd->bnhg', q, k) / jnp.sqrt(jnp.float32(c))
        attn = jax.nn.softmax(attn, axis=-1)
        out = jnp.einsum('bnhg,bngd->bnhd', attn, v)
        out = out.transpose(0, 2, 1, 3).reshape(b, n, c)
        return out @ w_out.T + b_out

    def _L1_xattn_ref(q, latent_kv, Wq, Wkv_expand, Wout):
        import jax, jax.numpy as jnp
        import numpy as np
        B, S, H, NH, L = (2, 256, 256, 16, 64)
        HD = H // NH
        b, sq, _ = q.shape
        sk = latent_kv.shape[1]
        qp = q @ Wq.T
        kv = latent_kv @ Wkv_expand.T
        k, v = jnp.split(kv, 2, axis=-1)
        qh = qp.reshape(b, sq, NH, HD).transpose(0, 2, 1, 3)
        kh = k.reshape(b, sk, NH, HD).transpose(0, 2, 1, 3)
        vh = v.reshape(b, sk, NH, HD).transpose(0, 2, 1, 3)
        inv_sqrt_d = 1.0 / jnp.sqrt(jnp.float32(HD))
        scores = jnp.einsum('bhqd,bhkd->bhqk', qh, kh) * inv_sqrt_d
        causal = jnp.tril(jnp.ones((sq, sk), dtype=bool))
        scores = jnp.where(causal, scores, jnp.finfo(scores.dtype).min)
        attn = jax.nn.softmax(scores, axis=-1)
        out = jnp.einsum('bhqk,bhkd->bhqd', attn, vh)
        out = out.transpose(0, 2, 1, 3).reshape(b, sq, H)
        return out @ Wout.T

    def _L1_ffn_ref(hidden_states, gate_weight, w_gate, w_up, w_down):
        import jax, jax.numpy as jnp
        import numpy as np
        TOP_K = 6
        'DeepseekMoE forward (inference path): top-k softmax gating + expert\n            dispatch/combine. gate_weight: [E, H]; w_gate/w_up: [E, H, M]; w_down: [E, M, H].'
        B, S, H = hidden_states.shape
        x = hidden_states.reshape(-1, H)
        T = x.shape[0]
        E = gate_weight.shape[0]
        logits = x @ gate_weight.T
        scores = jax.nn.softmax(logits, axis=-1)
        topk_w, topk_idx = jax.lax.top_k(scores, TOP_K)
        topk_w = topk_w / (topk_w.sum(axis=-1, keepdims=True) + 1e-20)
        cw = jnp.zeros((T, E), x.dtype).at[jnp.arange(T)[:, None], topk_idx].add(topk_w)

        def step(y, inp):
            wg, wu, wd, w_tok = inp
            h = jax.nn.silu(x @ wg) * (x @ wu)
            return (y + w_tok[:, None] * (h @ wd), None)
        y0 = jnp.zeros_like(x)
        y, _ = jax.lax.scan(step, y0, (w_gate, w_up, w_down, cw.T))
        return y.reshape(B, S, H)
    x = x + _L0_attn_ref(_layernorm(x, axis=-1), L0_attn_W_DKV_w, L0_attn_W_DKV_b, L0_attn_W_UK_w, L0_attn_W_UK_b, L0_attn_W_UV_w, L0_attn_W_UV_b, L0_attn_W_KR_w, L0_attn_W_KR_b, L0_attn_W_DQ_w, L0_attn_W_DQ_b, L0_attn_W_UQ_w, L0_attn_W_UQ_b, L0_attn_W_QR_w, L0_attn_W_QR_b, L0_attn_W_O_w, L0_attn_W_O_b)
    x = x + _L0_xattn_ref(_layernorm(x, axis=-1), ctx_512, L0_xattn_W_k, L0_xattn_b_k, L0_xattn_ln_gamma, L0_xattn_ln_beta)
    x = x + _L0_ffn_ref(_layernorm(x, axis=-1), L0_ffn_w_router, L0_ffn_wq, L0_ffn_bq, L0_ffn_wk, L0_ffn_bk, L0_ffn_wv, L0_ffn_bv, L0_ffn_wo, L0_ffn_w_gate, L0_ffn_w_up, L0_ffn_w_down, L0_ffn_ln1_w, L0_ffn_ln2_w)
    x = x + _L1_attn_ref(_layernorm(x, axis=-1), L1_attn_w_qkv, L1_attn_b_qkv, L1_attn_w_out, L1_attn_b_out)
    x = x + _L1_xattn_ref(_layernorm(x, axis=-1), ctx_512, L1_xattn_Wq, L1_xattn_Wkv_expand, L1_xattn_Wout)
    x = x + _L1_ffn_ref(_layernorm(x, axis=-1), L1_ffn_gate_weight, L1_ffn_w_gate, L1_ffn_w_up, L1_ffn_w_down)
    return x

_drawn_inputs = setup_inputs


def setup_inputs(seed=0):
    import zlib

    import numpy as np

    out = dict(_drawn_inputs(seed))
    spreads = {'L0_xattn_b_k': (0.0, 2.0),
     'L0_xattn_ln_gamma': (1.0, 0.6),
     'L0_xattn_ln_beta': (0.0, 2.0),
     'L0_ffn_bq': (0.0, 0.8),
     'L0_ffn_bk': (0.0, 0.8),
     'L0_ffn_bv': (0.0, 0.771),
     'L0_ffn_ln1_w': (1.0, 0.6),
     'L0_ffn_ln2_w': (1.0, 0.6)}
    factors = {'ctx_512': 3.991,
     'L0_attn_W_DKV_w': 8.0,
     'L0_attn_W_DKV_b': 8.0,
     'L0_attn_W_UK_w': 8.0,
     'L0_attn_W_UK_b': 64.0,
     'L0_attn_W_UV_w': 8.0,
     'L0_attn_W_UV_b': 2.936,
     'L0_attn_W_DQ_w': 8.0,
     'L0_attn_W_DQ_b': 8.0,
     'L0_attn_W_UQ_w': 8.0,
     'L0_attn_W_UQ_b': 8.0,
     'L0_attn_W_O_w': 3.0,
     'L0_attn_W_O_b': 2.73,
     'L0_xattn_W_k': 54.778,
     'L0_ffn_w_router': 4.331,
     'L0_ffn_wq': 8.0,
     'L0_ffn_wk': 8.0,
     'L0_ffn_wv': 6.125,
     'L0_ffn_wo': 4.13,
     'L0_ffn_w_gate': 8.0,
     'L0_ffn_w_up': 8.0,
     'L0_ffn_w_down': 8.0,
     'L1_attn_w_qkv': 4.205,
     'L1_attn_b_qkv': 64.0,
     'L1_attn_w_out': 3.952,
     'L1_attn_b_out': 36.413,
     'L1_xattn_Wq': 8.0,
     'L1_xattn_Wkv_expand': 4.089,
     'L1_xattn_Wout': 4.175,
     'L1_ffn_gate_weight': 8.0,
     'L1_ffn_w_gate': 8.0,
     'L1_ffn_w_up': 8.0,
     'L1_ffn_w_down': 8.0}
    for name, (base, spread) in spreads.items():
        noise = np.random.default_rng([zlib.crc32(name.encode()), seed]).standard_normal(out[name].shape)
        drawn = base * np.exp(spread * noise) if base else spread * noise
        out[name] = jnp.asarray(drawn.astype(out[name].dtype))
    for name, factor in factors.items():
        out[name] = (out[name] * factor).astype(out[name].dtype)
    return out
```

```python
from contextlib import ExitStack

import numpy as np
import concourse.bass as bass
from concourse import mybir

F32 = mybir.dt.float32
BF16 = mybir.dt.bfloat16
ALU = mybir.AluOpType
ACT = mybir.ActivationFunctionType
X = mybir.AxisListType.X
NEG = -1.0e30
NCH = 39


class Queue:

    def __init__(self, sem, chain=False):
        self.sem = sem
        self.n = 0
        self.ops = []
        self.seen = {}
        self.chain = chain

    def wait(self, toks):
        need = {}
        for s, v in toks:
            if self.seen.get(s.name, 0) < v:
                need[s.name] = (s, max(v, need.get(s.name, (s, 0))[1]))
        for s, v in need.values():
            self.seen[s.name] = v
            self.ops.append(lambda e, s=s, v=v: e.wait_ge(s, v))

    def add(self, fn, toks=(), inc=True):
        self.wait(toks)
        if self.chain and self.n:
            self.wait([self.now()])
        if inc:
            self.n += 1
            self.ops.append(lambda e, fn=fn: fn(e).then_inc(self.sem, 1))
        else:
            self.ops.append(fn)
        return (self.sem, self.n)

    def now(self):
        return (self.sem, self.n)

    def play(self, e):
        for f in self.ops:
            f(e)


class DmaSem:
    def __init__(self, sem):
        self.sem = sem
        self.n = 0

    def load(self, q, out, in_, toks=()):
        q.wait(toks)
        self.n += 16
        q.ops.append(lambda e: e.dma_start(out, in_).then_inc(self.sem, 16))
        return (self.sem, self.n)

    def all(self):
        return (self.sem, self.n)


def tt(q, out, a, b, op, w=()):
    return q.add(lambda e: e.tensor_tensor(out, a, b, op), w)


def tsc(q, out, a, s1, s2, op0, op1=None, w=()):
    if op1 is None:
        return q.add(lambda e: e.tensor_scalar(out, a, s1, None, op0), w)
    return q.add(lambda e: e.tensor_scalar(out, a, s1, s2, op0, op1), w)


def stt(q, out, a, s, b, op0, op1, w=()):
    return q.add(lambda e: e.scalar_tensor_tensor(out=out, in0=a, scalar=s, in1=b, op0=op0, op1=op1), w)


def red(q, out, a, op, w=()):
    return q.add(lambda e: e.tensor_reduce(out, a, X, op), w)


def cp(q, out, a, w=()):
    return q.add(lambda e: e.tensor_copy(out, a), w)


def rec(q, out, a, w=()):
    return q.add(lambda e: e.reciprocal(out, a), w)


def act(q, out, a, func, w=(), bias=0.0, scale=1.0, accum=None):
    if accum is not None:
        return q.add(lambda e: e.activation(out, a, func, bias=bias, scale=scale, accum_out=accum), w)
    return q.add(lambda e: e.activation(out, a, func, bias=bias, scale=scale), w)


def acopy(q, out, a, w=()):
    return q.add(lambda e: e.activation(out, a, ACT.Copy), w)


def mm(q, out, l, r, start, stop, w=(), inc=False):
    return q.add(lambda e: e.matmul(out, l, r, start=start, stop=stop, skip_group_check=True), w, inc)


def tr(q, out, a, ident, w=(), inc=False):
    return q.add(lambda e: e.transpose(out, a, ident), w, inc)


def program(nc, D, out, debug=None):
    ctx = ExitStack()
    with ctx:
        def sb(name, shape, dt=F32):
            return ctx.enter_context(nc.sbuf_tensor(name, shape, dt))

        def sem(name):
            return ctx.enter_context(nc.semaphore(name))

        PE, V, A, G, SP = [Queue(sem("q_" + n), n == "pool") for n in ("pe", "dve", "act", "pool", "sp")]
        B = [ctx.enter_context(nc.psum_tensor(f"B{i}", [128, 512], F32)) for i in range(8)]
        free = [[] for _ in range(8)]

        x = sb("x", [128, 8, 256])
        xh = sb("xh", [128, 8, 256])
        xT = sb("xT", [128, 2, 1024])
        ctxT = sb("ctxT", [65, 1024])
        ident = sb("ident", [128, 128])
        utri = sb("utri", [128, 128])
        iota1 = sb("iota1", [128, 128])
        identb = sb("identb", [128, 128], BF16)
        negm = sb("negm", [128, 4, 128], BF16)
        ones = sb("ones", [128, 128])
        zb = sb("zb", [1, 512], BF16)
        st = sb("st", [128, 8, 6])
        mv = sb("mv", [128, 8, 2])
        rs = sb("rs", [128, 8])
        R1 = sb("R1", [128, 9248])
        R2 = sb("R2", [128, 13120])

        def view(R, off, *shape, parts=128):
            n = int(np.prod(shape))
            v = R[0:parts, off:off + n]
            if len(shape) == 2:
                v = v.rearrange("p (a b) -> p a b", b=shape[1])
            elif len(shape) == 3:
                v = v.rearrange("p (a b c) -> p a b c", b=shape[1], c=shape[2])
            return v

        class Carve:
            def __init__(self, R, size, at=0):
                self.R, self.size, self.at = R, size, at

            def __call__(self, *shape, parts=128):
                v = view(self.R, self.at, *shape, parts=parts)
                self.at += int(np.prod(shape))
                assert self.at <= self.size, self.at
                return v

        dsems = {}

        def load(group, out_, name, q=None, w=()):
            if group not in dsems:
                dsems[group] = DmaSem(sem("d_" + group))
            return dsems[group].load(q or SP, out_, D[name], w)

        def got(group):
            return dsems[group].all()

        def dump(n):
            if debug:
                toks = [q.now() for q in (PE, V, A, G)]
                if "dbg" not in dsems:
                    dsems["dbg"] = DmaSem(sem("d_dbg"))
                t = dsems["dbg"].load(SP, D["dbg"][n], x[:, :, :], toks)
                V.wait([t])

        def barrier():
            toks = [q.now() for q in (PE, V, A, G)]
            for q in (PE, V, A, G, SP):
                q.wait(toks)
            for f in free:
                f.clear()

        c1 = Carve(R1, 9248)
        wuq, wuk, wuv, wot = c1(16, 193), c1(16, 65), c1(16, 64), c1(16, 256)
        buv = sb("buv", [128, 16])[:, :]
        bo = sb("bo", [1, 256])[:, :]
        wdkv = sb("wdkv", [128, 2, 128])
        wdq = sb("wdq", [128, 2, 192])
        cols = sb("cols", [128, 8])
        bkvb = sb("bkvb", [128, 64])
        wk1 = sb("wk1", [65, 64])
        gb = sb("gb", [128, 2, 256])
        wrb = sb("wrb", [128, 256])
        load("x", x[:, :, :], "x")
        load("c", ident[:, :], "ident")
        load("c", wdkv[:, :, :], "wdkv", A)
        load("c", wdq[:, :, :], "wdq", A)
        load("c", cols[:, :], "cols", A)
        load("c", bkvb[:, :], "bkvb", A)
        load("s", wuq, "wuq")
        load("s", wuk, "wuk")
        load("s2", wuv, "wuv")
        load("s2", wot, "wot")
        load("s2", buv, "buv", A)
        load("s2", bo, "bo", A)
        load("k", ctxT[:, :], "ctxT", A)
        load("k", wk1[:, :], "wk1", A)
        load("k", gb[:, :, :], "gb", A)
        load("k", wrb[:, :], "wrb", A)
        load("k", utri[:, :], "utri", A)
        load("k", iota1[:, :], "iota1", A)
        load("kb", identb[:, :], "identb", A)
        load("kb", negm[:, :, :], "negm", A)
        bqkv = sb("bqkv", [128, 4096])
        fwo = sb("fwo", [128, 16, 256])
        fgu = sb("fgu", [128, 2, 2048])
        fwd = sb("fwd", [128, 8, 256])
        rope = sb("rope", [128, 2, 128])
        load("f", bqkv[:, :], "bqkv")
        load("f", fwo[:, :, :], "fwo")
        load("f", fgu[:, :, :], "fgu")
        load("f", fwd[:, :, :], "fwd")
        load("f", rope[:, :, :], "rope")
        fg = fgu[:, :, :].rearrange("p a b -> p (a b)")
        w1q = fg[:, 0:1536].rearrange("p (a b) -> p a b", a=2)
        b1q = fg[:, 1536:2304]
        w1o = fg[:, 2304:2816].rearrange("p (a b) -> p a b", a=2)
        b1o = fg[:, 2816:3072]
        xq = sb("xq", [128, 2, 4, 128])
        xk = sb("xk", [64, 4, 128])
        xv = fg[0:64, 3584:3840]
        xo = fg[:, 3072:3584].rearrange("p (a b) -> p a b", a=2)
        gt = sb("gt", [128, 2, 28])
        selm = bqkv[0:84, 0:NCH * 64].bitcast(BF16)
        load("l", xq[:, :, :, :], "xq")
        load("l", xk[:, :, :], "xk")
        load("l", gt[:, :, :], "gt")

        t_one = G.add(lambda e: e.memset(ones[:, :], 1.0))
        mh = sb("mh", [128, 1])
        t_mh = G.add(lambda e: e.memset(mh[:, :], -0.5))
        t_zb = G.add(lambda e: e.memset(zb[:, :], 0.0))

        def ln(t, w, eps=1e-5):
            a = V.add(lambda e: e.bn_stats(st[:, t, :], x[:, t, :]), w)
            a = V.add(lambda e: e.bn_aggr(mv[:, t, :], st[:, t, :]), [a])
            a = tsc(V, rs[:, t:t + 1], mv[:, t, 1:2], eps, None, ALU.add, w=[a])
            a = tt(G, rs[:, t:t + 1], rs[:, t:t + 1], mh[:, 0:1], ALU.pow, [a, t_mh])
            return tsc(V, xh[:, t, :], x[:, t, :], mv[:, t, 0:1], rs[:, t:t + 1], ALU.subtract, ALU.mult, [a])

        def xpose(t, w, bank, eng=None):
            for c in range(2):
                a = tr(PE, B[bank][:, c * 128:(c + 1) * 128], xh[:, t, c * 128:(c + 1) * 128], ident[:, :],
                       list(w) + free[bank] + [got("c")], inc=(c == 1))
            src = B[bank][:, 0:256].rearrange("p (c n) -> p c n", c=2)
            dst = xT[:, :, t * 128:(t + 1) * 128]
            if eng is V:
                a = cp(V, dst, src, [a])
            else:
                a = acopy(A, dst, src, [a])
            free[bank] = [a]
            return a

        c2 = Carve(R2, 13120)
        M0, M1 = c2(8, 128), c2(8, 128, parts=65)
        T0, T1 = c2(16), c2(16, parts=65)
        U = c2(8, 256)
        cq0, cq1 = c2(1024), c2(1024, parts=65)
        ckT = c2(1024)
        ckn = c2(8, 65)
        ts = c2(8, 16)
        qp = [c2(256) for _ in range(2)]
        P = [c2(2, 256) for _ in range(4)]
        PT = [c2(2, 256) for _ in range(4)]
        tail = Carve(R1, 9248, 8192)
        O = [tail(2, 128) for _ in range(2)]
        OT = [tail(256) for _ in range(2)]
        bo2 = c2(512, parts=1)
        mx = [c2(2, 2) for _ in range(2)]
        mts = [c2(2, 2) for _ in range(2)]
        nb = [c2(2, 2) for _ in range(2)]
        rc = [c2(4) for _ in range(2)]
        SA = float(128) ** -0.5

        xt = []
        for t in range(8):
            a = ln(t, [got("x")])
            xt.append(xpose(t, [a], t % 2))
        t_m1 = G.add(lambda e: e.memset(cq1[64:65, :], 1.0))
        t_m2 = G.add(lambda e: e.memset(ckn[:, :, 64:65], 1.0))
        tk = []
        for hf in range(2):
            cs = slice(hf * 512, hf * 512 + 512)
            w = [xt[4 * hf + 3], got("c")]
            for k in range(2):
                a = mm(PE, B[2][:, :], wdkv[:, k, :], xT[:, k, cs], k == 0, k == 1, w + free[2], k == 1)
            a = act(A, ckT[:, cs], B[2][:, :], ACT.Identity, [a], bias=cols[:, 0:1])
            free[2] = [a]
            for k in range(2):
                b = mm(PE, B[3][:, :], wdq[:, k, 0:128], xT[:, k, cs], k == 0, k == 1, w + free[3], k == 1)
            b = tsc(V, cq0[:, cs], B[3][:, :], cols[:, 1:2], None, ALU.add, w=[b])
            free[3] = [b]
            for k in range(2):
                d = mm(PE, B[4][0:64, :], wdq[:, k, 128:192], xT[:, k, cs], k == 0, k == 1, w + free[4], k == 1)
            d = act(A, cq1[0:64, cs], B[4][0:64, :], ACT.Identity, [d], bias=cols[0:64, 2:3])
            free[4] = [d]
            tk += [a, b, d]
        for t in range(8):
            for k in range(2):
                a = mm(PE, B[5][:, t * 64:(t + 1) * 64], xT[:, k, t * 128:(t + 1) * 128], wdkv[:, k, 0:64],
                       k == 0, k == 1, free[5], k == 1 and t == 7)
        for t in range(8):
            b = tt(V, ckn[:, t, 0:64], B[5][:, t * 64:(t + 1) * 64], bkvb[:, :], ALU.add, [a])
        free[5] = [b]
        tk += [b, t_m1, t_m2]
        for g in range(4):
            for c in range(2):
                bk = 6 + c
                n = (128, 65)[c]
                for h in range(4 * g, 4 * g + 4):
                    a = mm(PE, B[bk][0:n, (h % 4) * 65:(h % 4) * 65 + 65], wuq[:, h, c * 128:c * 128 + n], wuk[:, h, :],
                           True, True, [got("s")] + free[bk], h % 4 == 3)
                src = B[bk][0:n, 0:260].rearrange("p (h c) -> p h c", h=4)
                Mc, Tc = ((M0, T0), (M1, T1))[c]
                dst = Mc[0:n, 2 * g:2 * g + 2, :].rearrange("p a (h c) -> p (a h) c", h=2)
                a1 = cp(V, dst, src[:, :, 0:64], [a])
                a2 = cp(V, Tc[0:n, 4 * g:4 * g + 4], src[:, :, 64], [a])
                free[bk] = [a1, a2]
        t_M = a2
        for p in range(8):
            bk = p % 2
            for hh in range(2):
                a = mm(PE, B[bk][64 * hh:64 * hh + 64, 0:256], wuv[:, 2 * p + hh, :], wot[:, 2 * p + hh, :],
                       True, True, [got("s2")] + free[bk], hh == 1)
            a = acopy(A, U[:, p, :], B[bk][:, 0:256], [a])
            free[bk] = [a]
        t_U = a
        for h in range(16):
            a = mm(PE, B[2][0:1, 0:256], buv[:, h:h + 1], wot[:, h, :], h == 0, False, free[2])
        a = mm(PE, B[2][0:1, 0:256], ones[0:1, 0:1], bo, False, True, [t_one], True)
        a = acopy(A, bo2[:, 0:256], B[2][0:1, 0:256], [a])
        t_bo = acopy(A, bo2[:, 256:512], B[2][0:1, 0:256], [a])
        free[2] = [t_bo]
        t_setup = PE.now()
        for t in range(8):
            tsl = slice(t * 128, (t + 1) * 128)
            mm(PE, B[3][:, t * 16:t * 16 + 16], cq0[:, tsl], T0, True, False, tk + [t_M] + free[3])
            a = mm(PE, B[3][:, t * 16:t * 16 + 16], cq1[:, tsl], T1, False, True, (), t == 7)
        t_ts = act(A, ts, B[3][:, 0:128].rearrange("p (t h) -> p t h", h=16), ACT.Copy, [a], scale=SA)
        free[3] = [t_ts]
        wqkv = view(R1, 0, 2, 4096)
        load("wqkv", wqkv, "wqkv", SP, [t_setup])

        NP = 32
        S_max, nb_t, exp_t, P_t, T_t, PT_t, PV_t, O_t = {}, {}, {}, {}, {}, {}, {}, {}
        qp_t, S_pe, QP_rd, OT_t, OTr_t, x1_t = {}, {}, {}, {}, {}, {}

        def QP(j):
            b, p = divmod(j, 8)
            bs = slice(b * 256, b * 256 + 256)
            w = free[4] + [t_M] + tk
            mm(PE, B[4][:, 0:256], M0[:, p, :], cq0[:, bs], True, False, w)
            a = mm(PE, B[4][:, 0:256], M1[:, p, :], cq1[:, bs], False, True, (), True)
            w = [a] + ([S_pe[j - 2]] if j >= 2 else [])
            qp_t[j] = acopy(A, qp[j % 2], B[4][:, 0:256], w)
            free[4] = [qp_t[j]]

        def S(j):
            b, p = divmod(j, 8)
            for qc in range(2):
                for hh in range(2):
                    r = slice(64 * hh, 64 * hh + 64)
                    a = mm(PE, B[hh][:, qc * 256:qc * 256 + 256], qp[j % 2][r, qc * 128:qc * 128 + 128],
                           ckT[r, b * 256:b * 256 + 256], True, True, [qp_t[j]] + free[hh], qc == 1)
                    S_max[j, hh] = a
            S_pe[j] = a
            s = j % 2
            for hh in range(2):
                w = [S_max[j, hh]] + ([nb_t[j - 2]] if j >= 2 else [])
                a = red(V, mx[s][:, :, hh], B[hh][:, :].rearrange("p (q k) -> p q k", q=2), ALU.max, w)
            tv = ts[:, 2 * b:2 * b + 2, 2 * p:2 * p + 2]
            a = stt(V, mts[s], mx[s], SA, tv, ALU.mult, ALU.add, [a, t_ts])
            w = [a] + ([exp_t[j - 2]] if j >= 2 else [])
            nb_t[j] = tt(V, nb[s], tv, mts[s], ALU.subtract, w)
            for hh in range(2):
                for qc in range(2):
                    w = [nb_t[j]] + ([T_t[j - 2]] if j >= 2 else [])
                    a = act(A, P[2 * s + hh][:, qc, :], B[hh][:, qc * 256:qc * 256 + 256], ACT.Exp, w,
                            bias=nb[s][:, qc, hh:hh + 1], scale=SA)
                P_t[j, hh] = a
                free[hh] = [a]
            exp_t[j] = a

        def T(j):
            s = j % 2
            for hh in range(2):
                bk = 2 + hh
                for kc in range(2):
                    for qc in range(2):
                        a = tr(PE, B[bk][:, kc * 256 + qc * 128:kc * 256 + qc * 128 + 128],
                               P[2 * s + hh][:, qc, kc * 128:kc * 128 + 128], ident[:, :],
                               [P_t[j, hh]] + free[bk], kc == 1 and qc == 1)
                T_t[j] = a
                w = [a] + ([PV_t[j - 2]] if j >= 2 else [])
                src = B[bk][:, :].rearrange("p (k q) -> p k q", k=2)
                if hh == 0:
                    a = cp(V, PT[2 * s + hh], src, w)
                else:
                    a = acopy(A, PT[2 * s + hh], src, w)
                PT_t[j, hh] = a
                free[bk] = [a]

        def PV(j):
            b = j // 8
            s = j % 2
            for hh in range(2):
                for qc in range(2):
                    o = (qc * 2 + hh) * 65
                    for kc in range(2):
                        a = mm(PE, B[5][:, o:o + 65], PT[2 * s + hh][:, kc, qc * 128:qc * 128 + 128],
                               ckn[:, 2 * b + kc, :], kc == 0, kc == 1, [PT_t[j, hh]] + free[5],
                               hh == 1 and qc == 1 and kc == 1)
            PV_t[j] = a
            src = B[5][:, 0:260].rearrange("p (g c) -> p g c", g=4)
            a = rec(V, rc[s], src[:, :, 64], [a])
            w = [a] + ([OTr_t[j - 2]] if j >= 2 else [])
            dst = O[s].rearrange("p q (h c) -> p (q h) c", h=2)
            a = tt(V, dst, src[:, :, 0:64], rc[s].rearrange("p (g o) -> p g o", o=1).to_broadcast([128, 4, 64]), ALU.mult, w)
            O_t[j] = a
            free[5] = [a]

        def OTr(j):
            s = j % 2
            for qc in range(2):
                a = tr(PE, B[6][:, qc * 128:qc * 128 + 128], O[s][:, qc, :], ident[:, :],
                       [O_t[j]] + free[6], qc == 1)
            OTr_t[j] = a
            a = cp(V, OT[s], B[6][:, 0:256], [a] + ([OP_t[j - 2]] if j >= 2 else []))
            free[6] = [a]
            OT_t[j] = a

        OP_t = {}

        def OP(j):
            b, p = divmod(j, 8)
            s = j % 2
            if p == 0:
                mm(PE, B[7][:, :], ones[0:1, :], bo2, True, False, [t_bo] + free[7])
            for qc in range(2):
                a = mm(PE, B[7][:, qc * 256:qc * 256 + 256], OT[s][:, qc * 128:qc * 128 + 128], U[:, p, :],
                       False, p == 7, [OT_t[j], t_U], qc == 1)
            OP_t[j] = a
            if p == 7:
                xv_ = x[:, 2 * b:2 * b + 2, :]
                a = tt(V, xv_, B[7][:, :].rearrange("p (q n) -> p q n", q=2), xv_, ALU.add, [a])
                free[7] = [a]
                x1_t[b] = a

        QP(0)
        for j in range(NP + 4):
            if j < NP:
                S(j)
            if 1 <= j <= NP:
                T(j - 1)
            if j + 1 < NP:
                QP(j + 1)
            if 2 <= j <= NP + 1:
                PV(j - 2)
            if 3 <= j <= NP + 2:
                OTr(j - 3)
            if 4 <= j:
                OP(j - 4)
        barrier()
        dump(0)
        c2 = Carve(R2, 13120)
        kvT = c2(1024, parts=64)
        kvn = c2(8, 64)
        oX = [c2(256, parts=64) for _ in range(2)]
        z = [c2(256) for _ in range(2)]
        eX = [c2(256) for _ in range(2)]
        sx = c2(8, 6)
        mvx = c2(8, 2)
        rx = c2(8, 4)
        for hf in range(2):
            a = mm(PE, B[hf][0:64, :], wk1[:, :], ctxT[:, hf * 512:hf * 512 + 512], True, True,
                   [got("k")], True)
            t_kvT = acopy(A, kvT[:, hf * 512:hf * 512 + 512], B[hf][0:64, :], [a])
            free[hf] = [t_kvT]
        for t in range(8):
            a = mm(PE, B[2][:, t * 64:(t + 1) * 64], ctxT[:, t * 128:(t + 1) * 128], wk1[:, :], True, True, (), t == 7)
        t_kvn = acopy(A, kvn, B[2][:, :].rearrange("p (t c) -> p t c", c=64), [a])
        free[2] = [t_kvn]
        for t in range(8):
            a = ln(t, [])
            xt[t] = xpose(t, [a], t % 2)
        oX_t, sim_t = {}, {}
        x2_t = {}
        for b in range(4):
            s = b % 2
            for jc in range(2):
                a = mm(PE, B[3][0:64, 0:256], kvn[:, 2 * b + jc, :], xT[:, jc, b * 256:b * 256 + 256],
                       jc == 0, jc == 1, [t_kvn, xt[2 * b], xt[2 * b + 1]] + free[3], jc == 1)
            a = acopy(A, oX[s], B[3][0:64, 0:256], [a] + ([sim_t[b - 2]] if b >= 2 else []))
            free[3] = [a]
            bk = 4 + s
            for ic in range(2):
                a2 = mm(PE, B[bk][:, ic * 256:ic * 256 + 256], oX[s][:, ic * 128:ic * 128 + 128],
                        kvT[:, b * 256:b * 256 + 256], True, True, [a, t_kvT] + free[bk], ic == 1)
            sim_t[b] = a2
            for ic in range(2):
                t = 2 * b + ic
                sp = B[bk][:, ic * 256:ic * 256 + 256]
                a = V.add(lambda e, t=t, sp=sp: e.bn_stats(sx[:, t, :], sp), [a2])
                a = V.add(lambda e, t=t: e.bn_aggr(mvx[:, t, :], sx[:, t, :]), [a])
                a = tsc(V, rx[:, t, 0:1], mvx[:, t, 1:2], 1.0 / 256.0, 1e-6, ALU.mult, ALU.add, [a])
                a = tt(G, rx[:, t, 1:2], rx[:, t, 0:1], mh[:, 0:1], ALU.pow, [a])
                a = tsc(V, rx[:, t, 1:2], rx[:, t, 1:2], 1.0 / 16.0, None, ALU.mult, w=[a])
                a = tsc(V, z[ic], sp, mvx[:, t, 0:1], rx[:, t, 1:2], ALU.subtract, ALU.mult, [a])
                if ic == 1:
                    free[bk] = [a]
                a = tt(V, z[ic], z[ic], gb[:, 0, :], ALU.mult, [a])
                a = tt(V, z[ic], z[ic], gb[:, 1, :], ALU.add, [a])
                a = V.add(lambda e, t=t, ic=ic: e.tensor_reduce(rx[:, t, 2:3], z[ic], X, ALU.max, negate=True), [a])
                a = act(A, eX[ic], z[ic], ACT.Exp, [a], bias=rx[:, t, 2:3], accum=rx[:, t, 3:4])
                a = rec(V, rx[:, t, 3:4], rx[:, t, 3:4], [a])
                x2_t[t] = stt(V, x[:, t, :], eX[ic], rx[:, t, 3:4], x[:, t, :], ALU.mult, ALU.add, [a])
        barrier()
        dump(1)

        c2 = Carve(R2, 13120)
        qkv = c2(4096)
        rp = c2(24, 128)
        qkT = c2(24, 128)
        Pf = c2(16, 128)
        PTf = rp[:, 0:16, :]
        oT = view(R2, 0, 16, 128)
        hT = Pf[:, 0:8, :]
        r2c = Carve(R1, 9248, 8192)
        scz = sb("scz", [128, 8, 5])
        junk = sb("junk", [128, 256])
        sc4 = sb("sc4", [4, 256])
        wk4 = sb("wk4", [4, 256])
        m8 = sb("m8", [4, 8])
        mT = sb("mT", [128, 2, 4])
        cT = sb("cT", [128, 2, 4])
        Sel = qkT[:, 0:8, :]
        SelT = sb("SelT", [128, 8, 128])
        xs = r2c(256)
        xs1 = r2c(256)
        xn = r2c(256)
        cs = sb("cs", [128, 132])
        nT = sb("nT", [128, 2, 128])
        sm = sb("sm", [128, 8])
        mxf = sb("mxf", [128, 3, 16])
        a = G.add(lambda e: e.memset(scz[:, :, :], 0.0))
        t_z = a
        lnt = []
        for t in range(8):
            a = ln(t, [])
            lnt.append(a)
            a = V.add(lambda e, t=t: e.tensor_tensor_reduce(junk[:, :], xh[:, t, :], wrb[:, :], 1.0, 0.0, ALU.mult,
                                                            ALU.add, scz[:, t, t // 2:t // 2 + 1]), [a, t_z, got("k")])
            w = [a]
            if t >= 2:
                w.append(lnt[t])
            a = mm(PE, B[0][0:4, (t % 2) * 128:(t % 2) * 128 + 128], scz[:, t, 0:4], ident[:, :],
                   t == 0, t >= 6, w + free[0], t == 7)
            b = tt(V, x[:, t, :], x[:, t, :], xh[:, t, :], ALU.add, [lnt[t]])
        a = cp(V, sc4[:, :], B[0][0:4, 0:256], [a])
        a = cp(V, wk4[:, :], sc4[:, :], [a])
        for r in range(4):
            a = V.add(lambda e: e.max(m8[:, :], wk4[:, :]), [a])
            a = V.add(lambda e: e.match_replace(wk4[:, :], m8[:, :], wk4[:, :], -3.0e38), [a])
        a = tsc(V, wk4[:, :], wk4[:, :], -3.0e38, None, ALU.is_equal, w=[a])
        for c in range(2):
            a2 = tr(PE, B[1][:, c * 4:c * 4 + 4], wk4[:, c * 128:c * 128 + 128], ident[0:4, 0:4], [a], c == 1)
        a = cp(V, mT[:, :, :], B[1][:, 0:8].rearrange("p (c b) -> p c b", c=2), [a2])
        mm(PE, B[2][:, 0:4], utri[:, :], mT[:, 0, :], True, True, [a])
        mm(PE, B[2][:, 4:8], utri[:, :], mT[:, 1, :], True, False)
        a2 = mm(PE, B[2][:, 4:8], ones[:, :], mT[:, 0, :], False, True, (), True)
        for b in range(4):
            a = stt(V, cT[:, :, b], B[2][:, b:8:4], float(32 * b), mT[:, :, b], ALU.add, ALU.mult, [a2])
        for t in range(8):
            a2 = tsc(V, Sel[:, t, :], iota1[:, :], cT[:, t % 2, t // 2:t // 2 + 1], None, ALU.is_equal, w=[a])
        for t in range(8):
            mm(PE, B[3][:, 0:256], Sel[:, t, :], xh[:, t, :], t == 0, t == 7, [a2])
        for t in range(8):
            mm(PE, B[4][:, 0:128], Sel[:, t, :], rope[:, t % 2, :], t == 0, t == 7, [got("f")])
        a = PE.add(lambda e: e.matmul(B[5][:, 0:4], Sel[:, 0, :], scz[:, 0, 0:4], start=True, stop=False,
                                      skip_group_check=True), (), False)
        for t in range(1, 8):
            a = mm(PE, B[5][:, 0:4], Sel[:, t, :], scz[:, t, 0:4], False, t == 7, (), t == 7)
        t_x = cp(V, xs, B[3][:, 0:256], [a])
        t_cs = acopy(A, cs[:, 0:128], B[4][:, 0:128], [a])
        free[3], free[4] = [t_x], [t_cs]
        t_sc = red(V, sm[:, 0:1], B[5][:, 0:4], ALU.add, [a])
        t_th = act(A, sm[:, 1:2], sm[:, 0:1], ACT.Tanh, [t_sc], scale=0.5)
        t_gate = tsc(V, sm[:, 2:3], sm[:, 1:2], 0.5, 0.5, ALU.mult, ALU.add, [t_th])
        for hf in range(2):
            for t in range(4 * hf, 4 * hf + 4):
                a = tr(PE, B[6 + hf][:, (t % 4) * 128:(t % 4) * 128 + 128], Sel[:, t, :], ident[:, :], (), t % 4 == 3)
            t_selT = acopy(A, SelT[:, 4 * hf:4 * hf + 4, :],
                           B[6 + hf][:, :].rearrange("p (t n) -> p t n", t=4), [a])
            free[6 + hf] = [t_selT]

        def rms(src, col, ln_col, w, bank):
            a = act(A, junk[:, :], src, ACT.Square, w, accum=sm[:, col:col + 1])
            a = tsc(V, sm[:, col:col + 1], sm[:, col:col + 1], 1.0 / 256.0, 1e-6, ALU.mult, ALU.add, [a])
            a = tt(G, sm[:, col:col + 1], sm[:, col:col + 1], mh[:, 0:1], ALU.pow, [a])
            a = tsc(V, xn, src, sm[:, col:col + 1], None, ALU.mult, w=[a] + list(w))
            for c in range(2):
                a2 = tr(PE, B[bank][:, c * 128:c * 128 + 128], xn[:, c * 128:c * 128 + 128], ident[:, :],
                        [a] + free[bank], c == 1)
            for c in range(2):
                a = tsc(V, nT[:, c, :], B[bank][:, c * 128:c * 128 + 128], cols[:, ln_col + c:ln_col + c + 1],
                        None, ALU.mult, w=[a2])
            free[bank] = [a]
            return a

        t_h = rms(xs, 3, 3, [t_x], 1)
        tb = got("f")
        b_of = [0, 2, 3, 4, 5, 6, 7, 1]
        qkv_t = {}
        for i, n in enumerate([4, 5, 0, 1, 2, 3, 6, 7]):
            bk = b_of[i]
            for k in range(2):
                a = mm(PE, B[bk][:, :], nT[:, k, :], wqkv[:, k, n * 512:n * 512 + 512], k == 0, k == 1,
                       [t_h, got("wqkv")] + free[bk], k == 1)
            a = tt(V, qkv[:, n * 512:n * 512 + 512], B[bk][:, :], bqkv[:, n * 512:n * 512 + 512], ALU.add, [a, tb])
            free[bk] = [a]
            qkv_t[n] = a
        cosb = cs[:, 0:64].rearrange("p (o d) -> p o d", o=1)
        sinb = cs[:, 64:128].rearrange("p (o d) -> p o d", o=1)
        tmp = Pf.rearrange("p a b -> p (a b)")
        rp_t = {}
        for i, (eng, h0, nh) in enumerate(((V, 16, 4), (G, 20, 4), (V, 0, 4), (G, 4, 4), (V, 8, 4), (V, 12, 4))):
            src = qkv[:, h0 * 128:(h0 + nh) * 128].rearrange("p (h d) -> p h d", d=128)
            q1, q2 = src[:, :, 0:64], src[:, :, 64:128]
            cb, snb = cosb.to_broadcast([128, nh, 64]), sinb.to_broadcast([128, nh, 64])
            tmpa = tmp[:, (i % 4) * 512:(i % 4) * 512 + 256].rearrange("p (h d) -> p h d", d=64)
            tmpb = tmp[:, (i % 4) * 512 + 256:(i % 4) * 512 + 512].rearrange("p (h d) -> p h d", d=64)
            w = [qkv_t[h0 // 4], t_cs] + ([rp_t[[16, 20, 0, 4, 8, 12][i - 4]]] if i >= 4 else [])
            r1, r2 = rp[:, h0:h0 + nh, 0:64], rp[:, h0:h0 + nh, 64:128]
            a1 = tt(eng, r1, q1, cb, ALU.mult, w)
            a2 = tt(eng, tmpa, q2, snb, ALU.mult)
            a3 = tt(eng, r2, q2, cb, ALU.mult)
            a4 = tt(eng, tmpb, q1, snb, ALU.mult)
            a = tt(eng, r1, r1, tmpa, ALU.subtract, [a2])
            rp_t[h0] = tt(eng, r2, r2, tmpb, ALU.add, [a4])
        qk_t = {}
        for i, h0 in enumerate([16, 20, 0, 4, 8, 12]):
            bk = b_of[i]
            for h in range(4):
                a = tr(PE, B[bk][:, h * 128:h * 128 + 128], rp[:, h0 + h, :], ident[:, :],
                       [rp_t[h0]] + free[bk], h == 3)
            a = acopy(A, qkT[:, h0:h0 + 4, :], B[bk][:, :].rearrange("p (h n) -> p h n", h=4), [a, t_selT])
            free[bk] = [a]
            qk_t[h0] = a
        SF = float(128) ** -0.5
        pf_t, ptf_t = {}, {}
        for g in range(4):
            bk = b_of[g + 1]
            mm(PE, B[bk][:, :], identb[:, :], negm[:, :, :], True, False, [got("kb")] + free[bk])
            for hh in range(4):
                h = 4 * g + hh
                a = mm(PE, B[bk][:, hh * 128:hh * 128 + 128], qkT[:, h, :], qkT[:, 16 + h // 2, :], False, True,
                       [qk_t[4 * g], qk_t[16], qk_t[20]], hh == 3)
            sv = B[bk][:, :].rearrange("p (h n) -> p h n", h=4)
            a = red(V, mxf[:, 0, 4 * g:4 * g + 4], sv, ALU.max, [a])
            a = tsc(V, mxf[:, 1, 4 * g:4 * g + 4], mxf[:, 0, 4 * g:4 * g + 4], -SF, None, ALU.mult, w=[a])
            for hh in range(4):
                h = 4 * g + hh
                a = act(A, Pf[:, h, :], sv[:, hh, :], ACT.Exp, [a] + list(rp_t.values()), bias=mxf[:, 1, h:h + 1],
                        scale=SF, accum=mxf[:, 2, h:h + 1])
            free[bk] = [a]
            a = rec(V, mxf[:, 2, 4 * g:4 * g + 4], mxf[:, 2, 4 * g:4 * g + 4], [a])
            rb = mxf[:, 2, 4 * g:4 * g + 4].rearrange("p (g o) -> p g o", o=1).to_broadcast([128, 4, 128])
            pf_t[g] = tt(V, Pf[:, 4 * g:4 * g + 4, :], Pf[:, 4 * g:4 * g + 4, :], rb, ALU.mult, [a])
        of_t = {}
        for g in range(4):
            bk = (7, 6, 0, 1)[g]
            for hh in range(4):
                a = tr(PE, B[bk][:, hh * 128:hh * 128 + 128], Pf[:, 4 * g + hh, :], ident[:, :],
                       [pf_t[g]] + free[bk], hh == 3)
            ptf_t[g] = acopy(A, PTf[:, 4 * g:4 * g + 4, :], B[bk][:, :].rearrange("p (h n) -> p h n", h=4), [a])
            free[bk] = [ptf_t[g]]
        for g in range(4):
            bk = b_of[g + 1]
            for kv in range(2):
                vh = 2 * g + kv
                a = mm(PE, B[bk][:, kv * 256:kv * 256 + 256], qkv[:, 3072 + vh * 128:3072 + vh * 128 + 128],
                       PTf[:, 2 * vh:2 * vh + 2, :], True, True, [ptf_t[g], qkv_t[6], qkv_t[7]] + free[bk], kv == 1)
            eng = (V, A)[g % 2]
            f = cp if g % 2 == 0 else acopy
            of_t[g] = f(eng, oT[:, 4 * g:4 * g + 4, :], B[bk][:, :].rearrange("p (h n) -> p h n", h=4),
                        [a] + [rp_t[4 * g]])
            free[bk] = [of_t[g]]
        for h in range(16):
            a = mm(PE, B[7][:, 0:256], oT[:, h, :], fwo[:, h, :], h == 0, h == 15, [of_t[h // 4], tb] + free[7], h == 15)
        t_x1 = tt(V, xs1, B[7][:, 0:256], xs, ALU.add, [a])
        t_h = rms(xs1, 4, 5, [t_x1], 1)
        gu_t = {}
        t_hT = []
        for hf in range(2):
            for u in range(2):
                bk = 2 + 2 * hf + u
                for m in range(4):
                    mo = u * 1024 + (4 * hf + m) * 128
                    for k in range(2):
                        a = mm(PE, B[bk][:, m * 128:m * 128 + 128], fgu[:, k, mo:mo + 128], nT[:, k, :],
                               k == 0, k == 1, [t_h] + free[bk], k == 1 and m == 3)
                gu_t[hf, u] = a
            gp = B[2 + 2 * hf][:, :]
            up = B[3 + 2 * hf][:, :]
            th = view(R2, 4096 + hf * 512, 512)
            a = act(A, th, gp, ACT.Tanh, [gu_t[hf, 0], gu_t[0, 1]], scale=0.5)
            a = stt(V, th, th, 1.0, gp, ALU.add, ALU.mult, [a])
            hv = hT[:, 4 * hf:4 * hf + 4, :].rearrange("p a b -> p (a b)")
            a = stt(V, hv, th, 0.5, up, ALU.mult, ALU.mult, [a, gu_t[hf, 1]])
            t_hT.append(a)
        for nm, dst in (("w1q", w1q), ("b1q", b1q), ("w1o", w1o), ("b1o", b1o), ("xv", xv), ("xo", xo)):
            load("m", dst, nm, SP, list(gu_t.values()))
        for m in range(8):
            a = mm(PE, B[6][:, 0:256], hT[:, m, :], fwd[:, m, :], m == 0, m == 7, [t_hT[m // 4]] + free[6], m == 7)
        a2 = tt(V, xs1, xs1, xs, ALU.subtract, [t_h, t_x1])
        a = tt(V, xs1, B[6][:, 0:256], xs1, ALU.add, [a, a2])
        a = tsc(V, xs1, xs1, sm[:, 2:3], None, ALU.mult, w=[a, t_gate])
        for b in range(4):
            bk = (0, 2)[b % 2]
            for c in range(2):
                a2 = mm(PE, B[bk][:, c * 256:c * 256 + 256], SelT[:, 2 * b + c, :], xs1, True, True,
                        [a, t_selT] + free[bk], c == 1)
            xv_ = x[:, 2 * b:2 * b + 2, :]
            a3 = tt(V, xv_, B[bk][:, :].rearrange("p (q n) -> p q n", q=2), xv_, ALU.add, [a2])
            free[bk] = [a3]
        barrier()
        dump(2)

        load("lb", selm, "selm")
        c1 = Carve(R1, 9248)
        pr = [c1(4096) for _ in range(2)]
        c2 = Carve(R2, 13120)
        q1 = [c2(768) for _ in range(2)]
        Sx = [c2(256) for _ in range(2)]
        ms = [c2(16) for _ in range(2)]
        oa = [c2(256) for _ in range(2)]
        oaT = [c2(2, 128) for _ in range(2)]
        oT_t, l1_t = {}, {}
        pend = {}

        def bc(ap, shape):
            return ap.to_broadcast(shape)

        V.wait([got("m")])

        def l1a_proj(t):
            a = ln(t, [])
            a = xpose(t, [a], 0 + t % 2)
            s = t % 2
            xs_ = [xT[:, k, t * 128:t * 128 + 128] for k in range(2)]
            for k in range(2):
                mm(PE, B[2 + 2 * s][:, :], xs_[k], w1q[:, k, 0:512], k == 0, k == 1, [a, got("m")] + free[2 + 2 * s])
            for k in range(2):
                a = mm(PE, B[3 + 2 * s][:, 0:256], xs_[k], w1q[:, k, 512:768], k == 0, k == 1, free[3 + 2 * s], k == 1)
            w = [a] + ([l1_t[t - 2]] if t >= 2 else [])
            a1 = tt(V, q1[s][:, 0:512], B[2 + 2 * s][:, :], b1q[:, 0:512], ALU.add, w)
            a2 = tt(V, q1[s][:, 512:768], B[3 + 2 * s][:, 0:256], b1q[:, 512:768], ALU.add, w)
            free[2 + 2 * s] = [a1]
            free[3 + 2 * s] = [a2]
            pend[t] = a2

        def l1a_attn(t):
            s = t % 2
            a2 = pend[t]
            qv = q1[s][:, 0:256].rearrange("p (h o d) -> p h o d", o=1, d=16)
            kv_ = q1[s][:, 256:512].rearrange("p (o g d) -> p o g d", o=1, d=16)
            vv = q1[s][:, 512:768].rearrange("p (o g d) -> p o d g", o=1, d=16)
            pv4 = pr[s].rearrange("p (h g d) -> p h g d", g=16, d=16)
            a = tt(V, pv4, bc(qv, [128, 16, 16, 16]), bc(kv_, [128, 16, 16, 16]), ALU.mult, [a2])
            Sv = Sx[s].rearrange("p (h g) -> p h g", g=16)
            a = red(V, Sv, pv4, ALU.add, [a])
            a = red(V, ms[s], Sv, ALU.max, [a])
            msb = ms[s].rearrange("p (h o) -> p h o", o=1).to_broadcast([128, 16, 16])
            a = tt(V, Sv, Sv, msb, ALU.subtract, [a])
            a = act(A, Sx[s], Sx[s], ACT.Exp, [a], scale=1.0 / 16.0)
            a = red(V, ms[s], Sv, ALU.add, [a])
            a = rec(V, ms[s], ms[s], [a])
            a = tt(V, Sv, Sv, msb, ALU.mult, [a])
            P4 = Sx[s].rearrange("p (h o g) -> p h o g", o=1, g=16)
            a = tt(V, pv4, bc(P4, [128, 16, 16, 16]), bc(vv, [128, 16, 16, 16]), ALU.mult, [a])
            a = red(V, oa[s].rearrange("p (h d) -> p h d", d=16), pv4, ALU.add,
                    [a] + ([oT_t[t - 2]] if t >= 2 else []))
            l1_t[t] = a
            b, c = divmod(t, 2)
            dst = D["scr"][b, :, c * 128:c * 128 + 128, :].rearrange("h n d -> n h d")
            w_t[t] = wsem.load(SP, dst, oa[s].rearrange("p (h d) -> p h d", d=16), [a])
            oT_t[t] = w_t[t]
            if c == 1:
                src = D["scr"][b].rearrange("(q h) (m l) d -> (h m) q (l d)", q=2, l=16)
                z_t[b] = zsem.load(A, zin[b % 2], src, [w_t[t - 1], w_t[t]] + ([zt_t[b - 2]] if b >= 2 else []))

        def l1a_out(b):
            for q in range(2):
                t = 2 * b + q
                for c in range(2):
                    m = tr(PE, B[6][:, c * 128:c * 128 + 128], zin[b % 2][:, q, c * 128:c * 128 + 128], ident[:, :],
                           [z_t[b]] + free[6], c == 1)
                zt_t[b] = m
                m = acopy(A, oaT[q], B[6][:, 0:256].rearrange("p (c n) -> p c n", c=2), [m] + ([op_t[q]] if b else []))
                free[6] = [m]
                for k in range(2):
                    m = mm(PE, B[7][:, 0:256], oaT[q][:, k, :], w1o[:, k, :], k == 0, k == 1, [m] + free[7], k == 1)
                op_t[q] = m
                m = tt(V, x[:, t, :], B[7][:, 0:256], x[:, t, :], ALU.add, [m])
                free[7] = [m]
                tt(V, x[:, t, :], x[:, t, :], b1o, ALU.add, [m])

        wsem = DmaSem(sem("d_scrw"))
        zsem = DmaSem(sem("d_scrr"))
        zin = [c2(2, 256) for _ in range(2)]
        w_t, z_t, zt_t, op_t = {}, {}, {}, {}
        l1a_proj(0)
        for t in range(8):
            if t < 7:
                l1a_proj(t + 1)
            l1a_attn(t)
            if t % 2 == 0 and t:
                l1a_out(t // 2 - 1)
        l1a_out(3)
        barrier()
        dump(3)

        c2 = Carve(R2, 13120)
        qT_ = [c2(4, 256) for _ in range(2)]
        kT_ = [c2(4, 256) for _ in range(2)]
        va = [c2(2, 16, 17) for _ in range(2)]
        Px = [c2(3, 128) for _ in range(4)]
        PTx = [c2(3, 128) for _ in range(4)]
        Ox = [c2(2, 256) for _ in range(2)]
        OTx = [c2(2, 256) for _ in range(2)]
        mxx = [c2(4) for _ in range(4)]
        rcx = c2(2, 16)
        t_v1 = [G.add(lambda e, s=s: e.memset(va[s][:, :, :, 16:17], 1.0)) for s in range(2)][-1]
        pre = {}

        def l1x_pre(b):
            s = b % 2
            for t in (2 * b, 2 * b + 1):
                a = ln(t, [])
                a = xpose(t, [a], 6, V)
            bs = slice(b * 256, b * 256 + 256)
            w = [last_S[b - 2]] if b >= 2 else []
            toks = []
            for g in range(2):
                for cc in range(2):
                    c = 2 * g + cc
                    for k in range(2):
                        m = mm(PE, B[7][:, cc * 256:cc * 256 + 256], xq[:, k, c, :], xT[:, k, bs],
                               k == 0, k == 1, [a, got("l")] + free[7], k == 1 and cc == 1)
                m = acopy(A, qT_[s][:, 2 * g:2 * g + 2, :], B[7][:, :].rearrange("p (c n) -> p c n", c=2), [m] + w)
                free[7] = [m]
                toks.append(m)
                for cc in range(2):
                    m = mm(PE, B[6][:, cc * 256:cc * 256 + 256], xk[:, 2 * g + cc, :], ctxT[0:64, bs], True, True,
                           free[6], cc == 1)
                m = cp(V, kT_[s][:, 2 * g:2 * g + 2, :], B[6][:, :].rearrange("p (c n) -> p c n", c=2), [m] + w)
                free[6] = [m]
                toks.append(m)
            w = [last_PV[b - 2]] if b >= 2 else []
            for c in range(2):
                m = mm(PE, B[7][:, c * 256:c * 256 + 256], ctxT[0:64, (2 * b + c) * 128:(2 * b + c) * 128 + 128], xv[:, :],
                       True, True, free[7], c == 1)
            for c in range(2):
                m2 = acopy(A, va[s][:, c, :, 0:16], B[7][:, c * 256:c * 256 + 256].rearrange("p (h d) -> p h d", d=16),
                           [m, t_v1] + w)
            free[7] = [m2]
            pre[b] = toks + [m2]

        last_S, last_PV = {}, {}
        xS, xP, xT_t, xPT, xPV, xN = {}, {}, {}, {}, {}, {}
        SX = 0.25
        NH = 64

        def xs_step(i):
            b, h = divmod(i, 16)
            s = b % 2
            c, j = divmod(h, 4)
            bk = (0, 1, 2)[i % 3]
            r = slice(32 * j, 32 * j + 32)
            Q = qT_[s][r, c, :]
            Kk = kT_[s][r, c, :]
            mm(PE, B[bk][:, 0:384], identb[:, :], negx, True, False, pre[b] + free[bk])
            mm(PE, B[bk][:, 0:128], Q[:, 0:128], Kk[:, 0:128], False, True)
            a = mm(PE, B[bk][:, 128:384], Q[:, 128:256], Kk[:, 0:256], False, True, (), True)
            last_S[b] = a
            m = i % 4
            w = [a] + ([xP[i - 4]] if i >= 4 else [])
            red(V, mxx[m][:, 0:1], B[bk][:, 0:128], ALU.max, w)
            a = red(V, mxx[m][:, 1:2], B[bk][:, 128:384], ALU.max)
            a = tsc(V, mxx[m][:, 2:4], mxx[m][:, 0:2], -SX, None, ALU.mult, w=[a])
            w = [a] + ([xT_t[i - 4]] if i >= 4 else [])
            act(A, Px[m][:, 0, :], B[bk][:, 0:128], ACT.Exp, w, bias=mxx[m][:, 2:3], scale=SX)
            a = act(A, Px[m][:, 1:3, :].rearrange("p a b -> p (a b)"), B[bk][:, 128:384], ACT.Exp, (),
                    bias=mxx[m][:, 3:4], scale=SX)
            free[bk] = [a]
            xP[i] = a

        def xt_step(i):
            m = i % 4
            bk = 3
            for c in range(3):
                a = tr(PE, B[bk][:, c * 128:c * 128 + 128], Px[m][:, c, :], ident[:, :], [xP[i]] + free[bk], c == 2)
            xT_t[i] = a
            w = [a] + ([xPV[i - 4]] if i >= 4 else [])
            a = (cp if i % 3 == 0 else acopy)((V if i % 3 == 0 else A), PTx[m], B[bk][:, 0:384].rearrange("p (c n) -> p c n", c=3), w)
            free[bk] = [a]
            xPT[i] = a

        def xpv_step(i):
            b, h = divmod(i, 16)
            s = b % 2
            m = i % 4
            w = [xPT[i]]
            mm(PE, B[4][:, h * 17:h * 17 + 17], PTx[m][:, 0, :], va[s][:, 0, h, :], True, True, w + free[4])
            mm(PE, B[5][:, h * 17:h * 17 + 17], PTx[m][:, 1, :], va[s][:, 0, h, :], True, False, w + free[5])
            a = mm(PE, B[5][:, h * 17:h * 17 + 17], PTx[m][:, 2, :], va[s][:, 1, h, :], False, True, (), True)
            xPV[i] = a
            last_PV[b] = a

        def x_end(b):
            s = b % 2
            for qc in range(2):
                src = B[4 + qc][:, 0:272].rearrange("p (h d) -> p h d", d=17)
                a = rec(V, rcx[:, qc, :], src[:, :, 16], [last_PV[b]])
                a = tt(V, Ox[s][:, qc, :].rearrange("p (h d) -> p h d", d=16), src[:, :, 0:16],
                       rcx[:, qc, :].rearrange("p (h o) -> p h o", o=1).to_broadcast([128, 16, 16]), ALU.mult,
                       [a] + ([xN[b - 2]] if b >= 2 else []))
                free[4 + qc] = [a]
            for c in range(2):
                for qc in range(2):
                    m = tr(PE, B[6][:, c * 256 + qc * 128:c * 256 + qc * 128 + 128], Ox[s][:, qc, c * 128:c * 128 + 128],
                           ident[:, :], [a] + free[6], c == 1 and qc == 1)
            xN[b] = m
            m = acopy(A, OTx[s], B[6][:, :].rearrange("p (c n) -> p c n", c=2), [m])
            free[6] = [m]
            for qc in range(2):
                for k in range(2):
                    a = mm(PE, B[7][:, qc * 256:qc * 256 + 256], OTx[s][:, k, qc * 128:qc * 128 + 128], xo[:, k, :],
                           k == 0, k == 1, [m] + free[7], k == 1 and qc == 1)
            xv_ = x[:, 2 * b:2 * b + 2, :]
            a = tt(V, xv_, B[7][:, :].rearrange("p (q n) -> p q n", q=2), xv_, ALU.add, [a])
            free[7] = [a]

        negx = negm[:, 0:3, :]
        negx3 = sb("negx3", [128, 3, 128], BF16)
        a = G.add(lambda e: e.memset(negx3[:, 1, :], 0.0))
        G.add(lambda e: e.tensor_copy(negx3[:, 0, :], negm[:, 0, :]), [got("kb")])
        t_ng = G.add(lambda e: e.tensor_copy(negx3[:, 2, :], negm[:, 0, :]))
        negx = negx3[:, :, :]
        PE.wait([t_ng])
        l1x_pre(0)
        for i in range(NH + 3):
            if i < NH:
                xs_step(i)
                if i % 16 == 8 and i // 16 < 3:
                    l1x_pre(i // 16 + 1)
            if 2 <= i <= NH + 1:
                xt_step(i - 2)
            if i >= 3:
                xpv_step(i - 3)
                if (i - 3) % 16 == 15:
                    x_end((i - 3) // 16)
        barrier()
        dump(4)

        c2 = Carve(R2, 13120)
        p30 = [c2(30) for _ in range(2)]
        r30 = [c2(30) for _ in range(2)]
        m8b = [c2(8) for _ in range(2)]
        rr = [c2(4) for _ in range(2)]
        NR = 3
        ring = [c2(768) for _ in range(NR)]
        thb = [c2(512) for _ in range(2)]
        hb = [c2(512) for _ in range(4)]
        yo = [c2(512) for _ in range(2)]
        cwp = [sb(f"cwp{i}", [128, 3, 28], BF16) for i in range(2)]
        cwr = [c2(28) for _ in range(2)]
        cwT = sb("cwT", [84, 1024], BF16)
        BT = ctx.enter_context(nc.psum_tensor("BT", [128, 512], BF16)) if False else None
        for i in range(2):
            G.add(lambda e, i=i: e.memset(p30[i][:, 28:29], 2.0))
            t_pad = G.add(lambda e, i=i: e.memset(p30[i][:, 29:30], 3.0))
        rd = [DmaSem(sem(f"ring{i}")) for i in range(NR)]
        ring_free = [[] for _ in range(NR)]
        steps = [(hf, c) for hf in range(2) for c in range(NCH)]
        ring_t = {}

        def fetch(n):
            if n < len(steps):
                s = n % NR
                ring_t[n] = rd[s].load(SP, ring[s], D["wmo"][steps[n][1], :, :], ring_free[s])

        for n in range(NR):
            fetch(n)
        cw_t = {}
        for t in range(8):
            s = t % 2
            a = ln(t, [])
            a = xpose(t, [a], s)
            for k in range(2):
                a = mm(PE, B[2 + s][:, 0:28], xT[:, k, t * 128:t * 128 + 128], gt[:, k, :], k == 0, k == 1,
                       [a] + free[2 + s], k == 1)
            lg = B[2 + s][:, 0:28]
            a = V.add(lambda e, s=s, lg=lg: e.tensor_reduce(rr[s][:, 0:1], lg, X, ALU.max, negate=True), [a])
            a = act(A, p30[s][:, 0:28], lg, ACT.Exp, [a, t_pad], bias=rr[s][:, 0:1], accum=rr[s][:, 1:2])
            free[2 + s] = [a]
            a = rec(V, rr[s][:, 2:3], rr[s][:, 1:2], [a])
            a = tsc(V, p30[s][:, 0:28], p30[s][:, 0:28], rr[s][:, 2:3], None, ALU.mult, w=[a])
            a = V.add(lambda e, s=s: e.max(m8b[s], p30[s]), [a])
            a = V.add(lambda e, s=s: e.match_replace(r30[s], m8b[s], p30[s], 0.0), [a])
            a = tt(V, r30[s][:, 0:28], p30[s][:, 0:28], r30[s][:, 0:28], ALU.subtract, [a])
            a = red(V, rr[s][:, 3:4], r30[s][:, 0:28], ALU.add, [a])
            a = tsc(V, rr[s][:, 3:4], rr[s][:, 3:4], 1e-20, None, ALU.add, w=[a])
            a = rec(V, rr[s][:, 3:4], rr[s][:, 3:4], [a])
            a = tsc(V, cwr[s], r30[s][:, 0:28], rr[s][:, 3:4], 0.5, ALU.mult, ALU.mult, [a])
            w = [cw_t[t - 2]] if t >= 2 else []
            a = cp(V, cwp[s][:, 0, :], cwr[s], [a] + w)
            a = tt(V, cwr[s], cwr[s], cwp[s][:, 0, :], ALU.subtract, [a])
            a = cp(V, cwp[s][:, 1, :], cwr[s], [a])
            a = tt(V, cwr[s], cwr[s], cwp[s][:, 1, :], ALU.subtract, [a])
            a = cp(V, cwp[s][:, 2, :], cwr[s], [a])
            pb = B[4 + s][:, :].bitcast(BF16)
            a = tr(PE, pb[0:84, 0:128], cwp[s][:, :, :].rearrange("p a b -> p (a b)"), identb[:, :], [a] + free[4 + s], True)
            cw_t[t] = a
            a = cp(V, cwT[:, t * 128:t * 128 + 128], pb[0:84, 0:128], [a])
            free[4 + s] = [a]
            t_cw = a
            t_xT = a

        bi = 0
        e_t, hb_rd = {}, {}
        acc_b = [[4, 5], [4, 5]]

        def moe_up(n):
            nonlocal bi
            hf, c = steps[n]
            M = 128 if c < NCH - 1 else 64
            cs_ = slice(hf * 512, hf * 512 + 512)
            s = n % NR
            W = ring[s].rearrange("p (j m) -> p j m", m=128)
            bk = [(0, 1, 2, 3, 6, 7)[(bi + i) % 6] for i in range(3)]
            bi += 3
            for u in range(2):
                for k in range(2):
                    a = mm(PE, B[bk[u]][0:M, :], W[:, 2 * k + u, 0:M], xT[:, k, cs_], k == 0, k == 1,
                           [ring_t[n], t_xT] + free[bk[u]], k == 1)
                if u == 0:
                    g_ = a
            a = mm(PE, B[bk[2]][0:M, :], selm[:, c * 128:c * 128 + M], cwT[:, cs_], True, True,
                   [t_cw, got("lb")] + free[bk[2]], True)
            gp, up, cb = [B[i][0:M, :] for i in bk]
            th = thb[n % 2][0:M, :]
            h = hb[n % 4][0:M, :]
            w = [e_t[n - 2]] if n >= 2 else []
            t1 = act(A, th, gp, ACT.Tanh, [g_] + w, scale=0.5)
            t1 = stt(V, th, th, 1.0, gp, ALU.add, ALU.mult, [t1])
            free[bk[0]] = [t1]
            t1 = tt(V, th, th, up, ALU.mult, [t1, a])
            free[bk[1]] = [t1]
            w = [hb_rd[n - 4]] if n >= 4 else []
            t1 = tt(V, h, th, cb, ALU.mult, [t1] + w)
            free[bk[2]] = [t1]
            e_t[n] = t1

        def moe_down(n):
            hf, c = steps[n]
            M = 128 if c < NCH - 1 else 64
            W = ring[n % NR]
            h = hb[n % 4][0:M, :]
            if c == 0:
                for q in range(2):
                    mm(PE, B[4 + q][:, :], zb[0:1, 0:128], zb[0:1, :], True, False, [t_zb] + free[4 + q])
            for q in range(4):
                a = mm(PE, B[4 + q // 2][:, (q % 2) * 256:(q % 2) * 256 + 256], h[:, q * 128:q * 128 + 128],
                       W[0:M, 512:768], False, c == NCH - 1, [e_t[n]], q == 3)
            hb_rd[n] = a
            ring_free[n % NR] = [a]
            fetch(n + NR)
            if c == NCH - 1:
                for q in range(2):
                    t0 = 4 * hf + 2 * q
                    xv_ = x[:, t0:t0 + 2, :]
                    b = tt(V, xv_, B[4 + q][:, :].rearrange("p (q n) -> p q n", q=2), xv_, ALU.add, [a])
                    free[4 + q] = [b]
                    outs.append(dsems["out"].load(SP, D["outv"][:, t0:t0 + 2, :], xv_, [b]))

        dsems["out"] = DmaSem(sem("d_out"))
        outs = []
        if True:
            for n in range(len(steps) + 1):
                if n < len(steps):
                    moe_up(n)
                if n >= 1:
                    moe_down(n - 1)
        if debug:
            SP.wait([dsems["dbg"].all()])
        SP.wait([dsems["out"].all()])
        SP.wait([q.now() for q in (PE, V, A, G)])

        block = ctx.enter_context(nc.Block())

        @block.sync
        def _(e):
            SP.play(e)

        @block.tensor
        def _(e):
            PE.play(e)

        @block.vector
        def _(e):
            V.play(e)

        @block.scalar
        def _(e):
            A.play(e)

        @block.gpsimd
        def _(e):
            G.play(e)


def lay(inp):
    f = np.float32
    i = {k: np.asarray(v) for k, v in inp.items()}
    d = {}

    def kc(w):
        return w.reshape(-1, 128, w.shape[1]).transpose(1, 0, 2)

    def bcast(v):
        return np.broadcast_to(v.reshape(1, -1), (128, v.size))

    d["x"] = i["x"].reshape(8, 128, 256).transpose(1, 0, 2)
    d["ident"] = np.eye(128, dtype=f)
    wk = i["L0_attn_W_DKV_w"].T
    d["wdkv"] = kc(np.concatenate([wk, wk], 1))
    d["wdq"] = kc(i["L0_attn_W_DQ_w"].T)
    cols = np.zeros((128, 8), f)
    cols[:, 0] = np.concatenate([i["L0_attn_W_DKV_b"]] * 2)
    cols[:, 1] = i["L0_attn_W_DQ_b"][0:128]
    cols[0:64, 2] = i["L0_attn_W_DQ_b"][128:192]
    cols[:, 3:5] = i["L0_ffn_ln1_w"].reshape(2, 128).T
    cols[:, 5:7] = i["L0_ffn_ln2_w"].reshape(2, 128).T
    d["cols"] = cols
    d["bkvb"] = bcast(i["L0_attn_W_DKV_b"])
    hd = lambda w: w.reshape(16, 128, -1).transpose(1, 0, 2)
    d["wuq"] = np.concatenate([hd(i["L0_attn_W_UQ_w"]), hd(i["L0_attn_W_UQ_b"])], 2)
    d["wuk"] = np.concatenate([hd(i["L0_attn_W_UK_w"]), hd(i["L0_attn_W_UK_b"])], 2)
    d["wuv"] = hd(i["L0_attn_W_UV_w"])
    d["buv"] = i["L0_attn_W_UV_b"].reshape(16, 128).T
    d["wot"] = hd(i["L0_attn_W_O_w"].T)
    d["bo"] = i["L0_attn_W_O_b"].reshape(1, 256)
    d["ctxT"] = np.concatenate([i["ctx_512"].reshape(1024, 64).T, np.ones((1, 1024), f)], 0)
    d["wk1"] = np.concatenate([i["L0_xattn_W_k"].T, i["L0_xattn_b_k"].reshape(1, 64)], 0)
    d["gb"] = np.stack([bcast(i["L0_xattn_ln_gamma"]), bcast(i["L0_xattn_ln_beta"])], 1)
    d["wrb"] = bcast(i["L0_ffn_w_router"])
    d["utri"] = np.triu(np.ones((128, 128), f))
    d["iota1"] = np.broadcast_to(np.arange(1, 129, dtype=f).reshape(1, 128), (128, 128))
    bf = mybir.dt.np(BF16)
    d["identb"] = np.eye(128, dtype=f).astype(bf)
    neg = np.where(np.tril(np.ones((128, 128), bool)), 0.0, NEG).astype(f)
    d["negm"] = np.broadcast_to(neg.reshape(128, 1, 128), (128, 4, 128)).astype(bf)
    d["bqkv"] = bcast(np.concatenate([i["L0_ffn_bq"], i["L0_ffn_bk"], i["L0_ffn_bv"]]))
    d["wqkv"] = kc(np.concatenate([i["L0_ffn_wq"], i["L0_ffn_wk"], i["L0_ffn_wv"]], 1))
    d["fwo"] = kc(i["L0_ffn_wo"])
    d["fgu"] = kc(np.concatenate([i["L0_ffn_w_gate"], i["L0_ffn_w_up"]], 1))
    d["fwd"] = kc(i["L0_ffn_w_down"])
    inv = (1.0 / np.power(f(10000.0), np.arange(0, 128, 2, dtype=f) / f(128))).astype(f)
    ang = np.arange(256, dtype=f)[:, None] * inv
    d["rope"] = kc(np.concatenate([np.cos(ang), np.sin(ang)], 1).astype(f))
    d["w1q"] = kc(i["L1_attn_w_qkv"].T)
    d["b1q"] = bcast(i["L1_attn_b_qkv"])
    d["w1o"] = kc(i["L1_attn_w_out"].T)
    d["b1o"] = bcast(i["L1_attn_b_out"])

    def pad(w):
        o = np.zeros((w.shape[0], 16, 32), f)
        o[:, :, 0:16] = w.reshape(-1, 16, 16)
        return o.reshape(-1, 4, 128)

    d["xq"] = pad(i["L1_xattn_Wq"].T).reshape(2, 128, 4, 128).transpose(1, 0, 2, 3)
    d["xk"] = pad(i["L1_xattn_Wkv_expand"][0:256].T)
    d["xv"] = i["L1_xattn_Wkv_expand"][256:512].T
    d["xo"] = kc(i["L1_xattn_Wout"].T)
    d["gt"] = kc(i["L1_ffn_gate_weight"].T)
    e = np.zeros((3, 28, NCH * 128), f)
    for k in range(28):
        e[:, k, k * 176:(k + 1) * 176] = 1.0
    d["selm"] = e.reshape(84, NCH * 128).astype(bf)
    w = np.zeros((NCH * 128, 768), f)
    for u, nm in enumerate(("L1_ffn_w_gate", "L1_ffn_w_up")):
        a = i[nm].transpose(0, 2, 1).reshape(4928, 2, 128)
        full = np.zeros((NCH * 128, 2, 128), f)
        full[0:4928] = a
        full = full.reshape(NCH, 128, 2, 128).transpose(0, 3, 2, 1)
        w.reshape(NCH, 128, 6, 128)[:, :, u, :] = full[:, :, 0]
        w.reshape(NCH, 128, 6, 128)[:, :, 2 + u, :] = full[:, :, 1]
    w[0:4928, 512:768] = i["L1_ffn_w_down"].reshape(4928, 256)
    d["wmo"] = w.reshape(NCH, 128, 768)
    return {k: np.ascontiguousarray(v) for k, v in d.items()}


DEBUG = None


def kernel(**inputs):
    import concourse.bacc as _bacc
    from concourse.bass_utils import run_bass_kernel_spmd as _run

    nc = _bacc.Bacc("TRN2", target_bir_lowering=False, num_devices=1)
    arrays, D = {}, {}
    for name, a in lay(inputs).items():
        arrays[f"in_{name}"] = a
        D[name] = nc.dram_tensor(f"in_{name}", a.shape, mybir.dt.from_np(a.dtype), kind="ExternalInput").ap()
    o = nc.dram_tensor("out_0", (4, 256, 256), F32, kind="ExternalOutput").ap()
    D["scr"] = nc.dram_tensor("scr", (4, 16, 256, 16), F32).ap()
    D["outv"] = o.rearrange("b (c p) n -> p (b c) n", p=128)
    if DEBUG:
        D["dbg"] = nc.dram_tensor("dbg", (5, 128, 8, 256), F32, kind="ExternalOutput").ap()
    program(nc, D, o, DEBUG)
    r = _run(nc, [arrays], core_ids=[0])
    if DEBUG:
        return r.results[0]["out_0"], r.results[0]["dbg"]
    return r.results[0]["out_0"]
```

```python
from contextlib import ExitStack

import numpy as np
import concourse.bass as bass
from concourse import mybir

F32 = mybir.dt.float32
BF16 = mybir.dt.bfloat16
F32R = mybir.dt.float32r
ALU = mybir.AluOpType
ACT = mybir.ActivationFunctionType
X = mybir.AxisListType.X
NEG = -1.0e30
NCH = 39


class Queue:

    def __init__(self, sem, chain=False):
        self.sem = sem
        self.n = 0
        self.k = 0
        self.ops = []
        self.seen = {}
        self.chain = chain

    def wait(self, toks):
        need = {}
        for s, v in toks:
            if self.seen.get(s.name, 0) < v:
                need[s.name] = (s, max(v, need.get(s.name, (s, 0))[1]))
        for s, v in need.values():
            self.seen[s.name] = v
            self.ops.append(lambda e, s=s, v=v: e.wait_ge(s, v))

    def add(self, fn, toks=(), inc=True):
        self.wait(toks)
        if self.chain and self.n:
            self.wait([self.now()])
        self.k += 1
        if inc:
            self.n += 1
            self.ops.append(lambda e, fn=fn: fn(e).then_inc(self.sem, 1))
        else:
            self.ops.append(fn)
        return (self.sem, self.n)

    def now(self):
        return (self.sem, self.n)

    def play(self, e):
        for f in self.ops:
            f(e)


MARKS = []


class DmaSem:
    def __init__(self, sem):
        self.sem = sem
        self.n = 0

    def load(self, q, out, in_, toks=()):
        q.wait(toks)
        self.n += 16
        q.ops.append(lambda e: e.dma_start(out, in_).then_inc(self.sem, 16))
        return (self.sem, self.n)

    def all(self):
        return (self.sem, self.n)


def tt(q, out, a, b, op, w=()):
    return q.add(lambda e: e.tensor_tensor(out, a, b, op), w)


def tsc(q, out, a, s1, s2, op0, op1=None, w=()):
    if op1 is None:
        return q.add(lambda e: e.tensor_scalar(out, a, s1, None, op0), w)
    return q.add(lambda e: e.tensor_scalar(out, a, s1, s2, op0, op1), w)


def stt(q, out, a, s, b, op0, op1, w=()):
    return q.add(lambda e: e.scalar_tensor_tensor(out=out, in0=a, scalar=s, in1=b, op0=op0, op1=op1), w)


def red(q, out, a, op, w=()):
    return q.add(lambda e: e.tensor_reduce(out, a, X, op), w)


def cp(q, out, a, w=()):
    return q.add(lambda e: e.tensor_copy(out, a), w)


def rec(q, out, a, w=()):
    return q.add(lambda e: e.reciprocal(out, a), w)


def act(q, out, a, func, w=(), bias=0.0, scale=1.0, accum=None):
    if accum is not None:
        return q.add(lambda e: e.activation(out, a, func, bias=bias, scale=scale, accum_out=accum), w)
    return q.add(lambda e: e.activation(out, a, func, bias=bias, scale=scale), w)


def acopy(q, out, a, w=()):
    return q.add(lambda e: e.activation(out, a, ACT.Copy), w)


def mm(q, out, l, r, start, stop, w=(), inc=False):
    q.k += l.dtype == F32
    return q.add(lambda e: e.matmul(out, l, r, start=start, stop=stop, skip_group_check=True), w, inc)


def tr(q, out, a, ident, w=(), inc=False):
    return q.add(lambda e: e.transpose(out, a, ident), w, inc)


def program(nc, D, out, debug=None):
    ctx = ExitStack()
    with ctx:
        def sb(name, shape, dt=F32):
            return ctx.enter_context(nc.sbuf_tensor(name, shape, dt))

        def sem(name):
            return ctx.enter_context(nc.semaphore(name))

        PE, V, A, G, SP = [Queue(sem("q_" + n), n == "pool") for n in ("pe", "dve", "act", "pool", "sp")]
        B = [ctx.enter_context(nc.psum_tensor(f"B{i}", [128, 512], F32)) for i in range(8)]
        free = [[] for _ in range(8)]

        x = sb("x", [128, 8, 256])
        xh = sb("xh", [128, 8, 256])
        xT = sb("xT", [128, 2, 1024])
        ctxT = sb("ctxT", [65, 1024])
        ident = sb("ident", [128, 128])
        utri = sb("utri", [128, 128])
        iota1 = sb("iota1", [128, 128])
        identb = sb("identb", [128, 128], BF16)
        negm = sb("negm", [128, 4, 128], BF16)
        ones = sb("ones", [128, 128])
        zb = sb("zb", [1, 512], BF16)
        st = sb("st", [128, 8, 6])
        mv = sb("mv", [128, 8, 2])
        rs = sb("rs", [128, 8])
        r1_base = (nc.sbuf_base + 31) // 32 * 32
        R1 = sb("R1", [128, 9248])
        R2 = sb("R2", [128, 13120])

        def view(R, off, *shape, parts=128):
            n = int(np.prod(shape))
            v = R[0:parts, off:off + n]
            if len(shape) == 2:
                v = v.rearrange("p (a b) -> p a b", b=shape[1])
            elif len(shape) == 3:
                v = v.rearrange("p (a b c) -> p a b c", b=shape[1], c=shape[2])
            return v

        class Carve:
            def __init__(self, R, size, at=0):
                self.R, self.size, self.at = R, size, at

            def __call__(self, *shape, parts=128):
                v = view(self.R, self.at, *shape, parts=parts)
                self.at += int(np.prod(shape))
                assert self.at <= self.size, self.at
                return v

        dsems = {}

        def load(group, out_, name, q=None, w=()):
            if group not in dsems:
                dsems[group] = DmaSem(sem("d_" + group))
            return dsems[group].load(q or SP, out_, D[name], w)

        def got(group):
            return dsems[group].all()

        def mark(name):
            MARKS.append((name, {"pe": PE.k, "dve": V.k}))

        def dump(n):
            mark(f"stage {n}")
            if debug:
                toks = [q.now() for q in (PE, V, A, G)]
                if "dbg" not in dsems:
                    dsems["dbg"] = DmaSem(sem("d_dbg"))
                t = dsems["dbg"].load(SP, D["dbg"][n], x[:, :, :], toks)
                V.wait([t])

        def barrier():
            toks = [q.now() for q in (PE, V, A, G)]
            for q in (PE, V, A, G, SP):
                q.wait(toks)
            for f in free:
                f.clear()

        c1 = Carve(R1, 9248)
        wuq, wuk, wuv, wot = c1(16, 193), c1(16, 65), c1(16, 64), c1(16, 256)
        buv = sb("buv", [128, 16])[:, :]
        bo = sb("bo", [1, 256])[:, :]
        wdkv = sb("wdkv", [128, 2, 128])
        wdq = sb("wdq", [128, 2, 192])
        cols = sb("cols", [128, 8])
        bkvb = sb("bkvb", [128, 64])
        wk1 = sb("wk1", [65, 64])
        gb = sb("gb", [128, 2, 256])
        wrb = sb("wrb", [128, 256])
        load("x", x[:, :, :], "x")
        load("c", ident[:, :], "ident")
        load("c", wdkv[:, :, :], "wdkv", A)
        load("c", wdq[:, :, :], "wdq", A)
        load("c", cols[:, :], "cols", A)
        load("c", bkvb[:, :], "bkvb", A)
        load("s", wuq, "wuq")
        load("s", wuk, "wuk")
        load("s2", wuv, "wuv")
        load("s2", wot, "wot")
        load("s2", buv, "buv", A)
        load("s2", bo, "bo", A)
        load("k", ctxT[:, :], "ctxT", A)
        load("k", wk1[:, :], "wk1", A)
        load("k", gb[:, :, :], "gb", A)
        load("k", wrb[:, :], "wrb", A)
        load("k", utri[:, :], "utri", A)
        load("k", iota1[:, :], "iota1", A)
        load("kb", identb[:, :], "identb", A)
        load("kb", negm[:, :, :], "negm", A)
        bqkv = sb("bqkv", [128, 4096])
        fwo = sb("fwo", [128, 16, 256])
        fgu = sb("fgu", [128, 2, 2048])
        fwd = sb("fwd", [128, 8, 256])
        rope = sb("rope", [128, 2, 128])
        load("f", bqkv[:, :], "bqkv")
        load("f", fwo[:, :, :], "fwo")
        load("f", fgu[:, :, :], "fgu")
        load("f", fwd[:, :, :], "fwd")
        load("f", rope[:, :, :], "rope")
        fg = fgu[:, :, :].rearrange("p a b -> p (a b)")
        w1q = fg[:, 0:1536].rearrange("p (a b) -> p a b", a=2)
        b1q = fg[:, 1536:2304]
        w1o = fg[:, 2304:2816].rearrange("p (a b) -> p a b", a=2)
        b1o = fg[:, 2816:3072]
        xq = sb("xq", [128, 2, 4, 128])
        xk = sb("xk", [64, 4, 128])
        xv = fg[0:64, 3584:3840]
        xo = fg[:, 3072:3584].rearrange("p (a b) -> p a b", a=2)
        gt = sb("gt", [128, 2, 28])
        selm = bqkv[0:84, 0:NCH * 64].bitcast(BF16)
        load("l", xq[:, :, :, :], "xq")
        load("l", xk[:, :, :], "xk")
        load("l", gt[:, :, :], "gt")

        t_one = G.add(lambda e: e.memset(ones[:, :], 1.0))
        mh = sb("mh", [128, 1])
        t_mh = G.add(lambda e: e.memset(mh[:, :], -0.5))
        t_zb = G.add(lambda e: e.memset(zb[:, :], 0.0))

        def ln(t, w, eps=1e-5):
            a = V.add(lambda e: e.bn_stats(st[:, t, :], x[:, t, :]), w)
            a = V.add(lambda e: e.bn_aggr(mv[:, t, :], st[:, t, :]), [a])
            a = tsc(V, rs[:, t:t + 1], mv[:, t, 1:2], eps, None, ALU.add, w=[a])
            a = tt(G, rs[:, t:t + 1], rs[:, t:t + 1], mh[:, 0:1], ALU.pow, [a, t_mh])
            return tsc(V, xh[:, t, :], x[:, t, :], mv[:, t, 0:1], rs[:, t:t + 1], ALU.subtract, ALU.mult, [a])

        def xpose(t, w, bank, eng=None):
            for c in range(2):
                a = tr(PE, B[bank][:, c * 128:(c + 1) * 128], xh[:, t, c * 128:(c + 1) * 128], ident[:, :],
                       list(w) + free[bank] + [got("c")], inc=(c == 1))
            src = B[bank][:, 0:256].rearrange("p (c n) -> p c n", c=2)
            dst = xT[:, :, t * 128:(t + 1) * 128]
            if eng is V:
                a = cp(V, dst, src, [a])
            else:
                a = acopy(A, dst, src, [a])
            free[bank] = [a]
            return a

        c2 = Carve(R2, 13120)
        M0, M1 = c2(8, 128), c2(8, 128, parts=65)
        T0, T1 = c2(16), c2(16, parts=65)
        U = c2(8, 256)
        cq0, cq1 = c2(1024), c2(1024, parts=65)
        ckT = c2(1024)
        ckn = c2(8, 65)
        ts = c2(8, 16)
        qp = [c2(256) for _ in range(2)]
        P = [c2(2, 256) for _ in range(4)]
        PT = [c2(2, 256) for _ in range(4)]
        tail = Carve(R1, 9248, 8192)
        O = [tail(2, 128) for _ in range(2)]
        OT = [tail(256) for _ in range(2)]
        bo2 = c2(512, parts=1)
        mx = [c2(2, 2) for _ in range(2)]
        mts = [c2(2, 2) for _ in range(2)]
        nb = [c2(2, 2) for _ in range(2)]
        rc = [c2(4) for _ in range(2)]
        SA = float(128) ** -0.5

        xt = []
        for t in range(8):
            a = ln(t, [got("x")])
            xt.append(xpose(t, [a], t % 2))
        t_m1 = G.add(lambda e: e.memset(cq1[64:65, :], 1.0))
        t_m2 = G.add(lambda e: e.memset(ckn[:, :, 64:65], 1.0))
        tk = []
        for hf in range(2):
            cs = slice(hf * 512, hf * 512 + 512)
            w = [xt[4 * hf + 3], got("c")]
            for k in range(2):
                a = mm(PE, B[2][:, :], wdkv[:, k, :], xT[:, k, cs], k == 0, k == 1, w + free[2], k == 1)
            a = act(A, ckT[:, cs], B[2][:, :], ACT.Identity, [a], bias=cols[:, 0:1])
            free[2] = [a]
            for k in range(2):
                b = mm(PE, B[3][:, :], wdq[:, k, 0:128], xT[:, k, cs], k == 0, k == 1, w + free[3], k == 1)
            b = tsc(V, cq0[:, cs], B[3][:, :], cols[:, 1:2], None, ALU.add, w=[b])
            free[3] = [b]
            for k in range(2):
                d = mm(PE, B[4][0:64, :], wdq[:, k, 128:192], xT[:, k, cs], k == 0, k == 1, w + free[4], k == 1)
            d = act(A, cq1[0:64, cs], B[4][0:64, :], ACT.Identity, [d], bias=cols[0:64, 2:3])
            free[4] = [d]
            tk += [a, b, d]
        for t in range(8):
            for k in range(2):
                a = mm(PE, B[5][:, t * 64:(t + 1) * 64], xT[:, k, t * 128:(t + 1) * 128], wdkv[:, k, 0:64],
                       k == 0, k == 1, free[5], k == 1 and t == 7)
        for t in range(8):
            b = tt(V, ckn[:, t, 0:64], B[5][:, t * 64:(t + 1) * 64], bkvb[:, :], ALU.add, [a])
        free[5] = [b]
        tk += [b, t_m1, t_m2]
        for g in range(4):
            for c in range(2):
                bk = 6 + c
                n = (128, 65)[c]
                for h in range(4 * g, 4 * g + 4):
                    a = mm(PE, B[bk][0:n, (h % 4) * 65:(h % 4) * 65 + 65], wuq[:, h, c * 128:c * 128 + n], wuk[:, h, :],
                           True, True, [got("s")] + free[bk], h % 4 == 3)
                src = B[bk][0:n, 0:260].rearrange("p (h c) -> p h c", h=4)
                Mc, Tc = ((M0, T0), (M1, T1))[c]
                dst = Mc[0:n, 2 * g:2 * g + 2, :].rearrange("p a (h c) -> p (a h) c", h=2)
                a1 = cp(V, dst, src[:, :, 0:64], [a])
                a2 = cp(V, Tc[0:n, 4 * g:4 * g + 4], src[:, :, 64], [a])
                free[bk] = [a1, a2]
        t_M = a2
        for p in range(8):
            bk = p % 2
            for hh in range(2):
                a = mm(PE, B[bk][64 * hh:64 * hh + 64, 0:256], wuv[:, 2 * p + hh, :], wot[:, 2 * p + hh, :],
                       True, True, [got("s2")] + free[bk], hh == 1)
            a = acopy(A, U[:, p, :], B[bk][:, 0:256], [a])
            free[bk] = [a]
        t_U = a
        for h in range(16):
            a = mm(PE, B[2][0:1, 0:256], buv[:, h:h + 1], wot[:, h, :], h == 0, False, free[2])
        a = mm(PE, B[2][0:1, 0:256], ones[0:1, 0:1], bo, False, True, [t_one], True)
        a = acopy(A, bo2[:, 0:256], B[2][0:1, 0:256], [a])
        t_bo = acopy(A, bo2[:, 256:512], B[2][0:1, 0:256], [a])
        free[2] = [t_bo]
        t_setup = PE.now()
        for t in range(8):
            tsl = slice(t * 128, (t + 1) * 128)
            mm(PE, B[3][:, t * 16:t * 16 + 16], cq0[:, tsl], T0, True, False, tk + [t_M] + free[3])
            a = mm(PE, B[3][:, t * 16:t * 16 + 16], cq1[:, tsl], T1, False, True, (), t == 7)
        t_ts = act(A, ts, B[3][:, 0:128].rearrange("p (t h) -> p t h", h=16), ACT.Copy, [a], scale=SA)
        free[3] = [t_ts]
        wqkv = view(R1, 0, 2, 4096)
        load("wqkv", wqkv, "wqkv", SP, [t_setup])

        NP = 32
        S_max, nb_t, exp_t, P_t, T_t, PT_t, PV_t, O_t = {}, {}, {}, {}, {}, {}, {}, {}
        qp_t, S_pe, QP_rd, OT_t, OTr_t, x1_t = {}, {}, {}, {}, {}, {}

        def QP(j):
            b, p = divmod(j, 8)
            bs = slice(b * 256, b * 256 + 256)
            w = free[4] + [t_M] + tk
            mm(PE, B[4][:, 0:256], M0[:, p, :], cq0[:, bs], True, False, w)
            a = mm(PE, B[4][:, 0:256], M1[:, p, :], cq1[:, bs], False, True, (), True)
            w = [a] + ([S_pe[j - 2]] if j >= 2 else [])
            qp_t[j] = acopy(A, qp[j % 2], B[4][:, 0:256], w)
            free[4] = [qp_t[j]]

        def S(j):
            b, p = divmod(j, 8)
            for qc in range(2):
                for hh in range(2):
                    r = slice(64 * hh, 64 * hh + 64)
                    a = mm(PE, B[hh][:, qc * 256:qc * 256 + 256], qp[j % 2][r, qc * 128:qc * 128 + 128],
                           ckT[r, b * 256:b * 256 + 256], True, True, [qp_t[j]] + free[hh], qc == 1)
                    S_max[j, hh] = a
            S_pe[j] = a
            s = j % 2
            for hh in range(2):
                w = [S_max[j, hh]] + ([nb_t[j - 2]] if j >= 2 else [])
                a = red(V, mx[s][:, :, hh], B[hh][:, :].rearrange("p (q k) -> p q k", q=2), ALU.max, w)
            tv = ts[:, 2 * b:2 * b + 2, 2 * p:2 * p + 2]
            a = stt(V, mts[s], mx[s], SA, tv, ALU.mult, ALU.add, [a, t_ts])
            w = [a] + ([exp_t[j - 2]] if j >= 2 else [])
            nb_t[j] = tt(V, nb[s], tv, mts[s], ALU.subtract, w)
            for hh in range(2):
                for qc in range(2):
                    w = [nb_t[j]] + ([T_t[j - 2]] if j >= 2 else [])
                    a = act(A, P[2 * s + hh][:, qc, :], B[hh][:, qc * 256:qc * 256 + 256], ACT.Exp, w,
                            bias=nb[s][:, qc, hh:hh + 1], scale=SA)
                P_t[j, hh] = a
                free[hh] = [a]
            exp_t[j] = a

        def T(j):
            s = j % 2
            for hh in range(2):
                bk = 2 + hh
                for kc in range(2):
                    for qc in range(2):
                        a = tr(PE, B[bk][:, kc * 256 + qc * 128:kc * 256 + qc * 128 + 128],
                               P[2 * s + hh][:, qc, kc * 128:kc * 128 + 128], ident[:, :],
                               [P_t[j, hh]] + free[bk], kc == 1 and qc == 1)
                T_t[j] = a
                w = [a] + ([PV_t[j - 2]] if j >= 2 else [])
                src = B[bk][:, :].rearrange("p (k q) -> p k q", k=2)
                if hh == 0:
                    a = cp(V, PT[2 * s + hh], src, w)
                else:
                    a = acopy(A, PT[2 * s + hh], src, w)
                PT_t[j, hh] = a
                free[bk] = [a]

        def PV(j):
            b = j // 8
            s = j % 2
            for hh in range(2):
                for qc in range(2):
                    o = (qc * 2 + hh) * 65
                    for kc in range(2):
                        a = mm(PE, B[5][:, o:o + 65], PT[2 * s + hh][:, kc, qc * 128:qc * 128 + 128],
                               ckn[:, 2 * b + kc, :], kc == 0, kc == 1, [PT_t[j, hh]] + free[5],
                               hh == 1 and qc == 1 and kc == 1)
            PV_t[j] = a
            src = B[5][:, 0:260].rearrange("p (g c) -> p g c", g=4)
            a = rec(V, rc[s], src[:, :, 64], [a])
            w = [a] + ([OTr_t[j - 2]] if j >= 2 else [])
            dst = O[s].rearrange("p q (h c) -> p (q h) c", h=2)
            a = tt(V, dst, src[:, :, 0:64], rc[s].rearrange("p (g o) -> p g o", o=1).to_broadcast([128, 4, 64]), ALU.mult, w)
            O_t[j] = a
            free[5] = [a]

        def OTr(j):
            s = j % 2
            for qc in range(2):
                a = tr(PE, B[6][:, qc * 128:qc * 128 + 128], O[s][:, qc, :], ident[:, :],
                       [O_t[j]] + free[6], qc == 1)
            OTr_t[j] = a
            a = cp(V, OT[s], B[6][:, 0:256], [a] + ([OP_t[j - 2]] if j >= 2 else []))
            free[6] = [a]
            OT_t[j] = a

        OP_t = {}

        def OP(j):
            b, p = divmod(j, 8)
            s = j % 2
            if p == 0:
                mm(PE, B[7][:, :], ones[0:1, :], bo2, True, False, [t_bo] + free[7])
            for qc in range(2):
                a = mm(PE, B[7][:, qc * 256:qc * 256 + 256], OT[s][:, qc * 128:qc * 128 + 128], U[:, p, :],
                       False, p == 7, [OT_t[j], t_U], qc == 1)
            OP_t[j] = a
            if p == 7:
                xv_ = x[:, 2 * b:2 * b + 2, :]
                a = tt(V, xv_, B[7][:, :].rearrange("p (q n) -> p q n", q=2), xv_, ALU.add, [a])
                free[7] = [a]
                x1_t[b] = a

        mark("A setup")
        QP(0)
        for j in range(NP + 4):
            if j < NP:
                S(j)
            if 1 <= j <= NP:
                T(j - 1)
            if j + 1 < NP:
                QP(j + 1)
            if 2 <= j <= NP + 1:
                PV(j - 2)
            if 3 <= j <= NP + 2:
                OTr(j - 3)
            if 4 <= j:
                OP(j - 4)
        barrier()
        dump(0)
        c2 = Carve(R2, 13120)
        kvT = c2(1024, parts=64)
        kvn = c2(8, 64)
        oX = [c2(256, parts=64) for _ in range(2)]
        z = [c2(256) for _ in range(2)]
        eX = [c2(256) for _ in range(2)]
        sx = c2(8, 6)
        mvx = c2(8, 2)
        rx = c2(8, 4)
        for hf in range(2):
            a = mm(PE, B[hf][0:64, :], wk1[:, :], ctxT[:, hf * 512:hf * 512 + 512], True, True,
                   [got("k")], True)
            t_kvT = acopy(A, kvT[:, hf * 512:hf * 512 + 512], B[hf][0:64, :], [a])
            free[hf] = [t_kvT]
        for t in range(8):
            a = mm(PE, B[2][:, t * 64:(t + 1) * 64], ctxT[:, t * 128:(t + 1) * 128], wk1[:, :], True, True, (), t == 7)
        t_kvn = acopy(A, kvn, B[2][:, :].rearrange("p (t c) -> p t c", c=64), [a])
        free[2] = [t_kvn]
        for t in range(8):
            a = ln(t, [])
            xt[t] = xpose(t, [a], t % 2)
        oX_t, sim_t = {}, {}
        x2_t = {}
        for b in range(4):
            s = b % 2
            for jc in range(2):
                a = mm(PE, B[3][0:64, 0:256], kvn[:, 2 * b + jc, :], xT[:, jc, b * 256:b * 256 + 256],
                       jc == 0, jc == 1, [t_kvn, xt[2 * b], xt[2 * b + 1]] + free[3], jc == 1)
            a = acopy(A, oX[s], B[3][0:64, 0:256], [a] + ([sim_t[b - 2]] if b >= 2 else []))
            free[3] = [a]
            bk = 4 + s
            for ic in range(2):
                a2 = mm(PE, B[bk][:, ic * 256:ic * 256 + 256], oX[s][:, ic * 128:ic * 128 + 128],
                        kvT[:, b * 256:b * 256 + 256], True, True, [a, t_kvT] + free[bk], ic == 1)
            sim_t[b] = a2
            for ic in range(2):
                t = 2 * b + ic
                sp = B[bk][:, ic * 256:ic * 256 + 256]
                a = V.add(lambda e, t=t, sp=sp: e.bn_stats(sx[:, t, :], sp), [a2])
                a = V.add(lambda e, t=t: e.bn_aggr(mvx[:, t, :], sx[:, t, :]), [a])
                a = tsc(V, rx[:, t, 0:1], mvx[:, t, 1:2], 1.0 / 256.0, 1e-6, ALU.mult, ALU.add, [a])
                a = tt(G, rx[:, t, 1:2], rx[:, t, 0:1], mh[:, 0:1], ALU.pow, [a])
                a = tsc(V, rx[:, t, 1:2], rx[:, t, 1:2], 1.0 / 16.0, None, ALU.mult, w=[a])
                a = tsc(V, z[ic], sp, mvx[:, t, 0:1], rx[:, t, 1:2], ALU.subtract, ALU.mult, [a])
                if ic == 1:
                    free[bk] = [a]
                a = tt(V, z[ic], z[ic], gb[:, 0, :], ALU.mult, [a])
                a = tt(V, z[ic], z[ic], gb[:, 1, :], ALU.add, [a])
                a = V.add(lambda e, t=t, ic=ic: e.tensor_reduce(rx[:, t, 2:3], z[ic], X, ALU.max, negate=True), [a])
                a = act(A, eX[ic], z[ic], ACT.Exp, [a], bias=rx[:, t, 2:3], accum=rx[:, t, 3:4])
                a = rec(V, rx[:, t, 3:4], rx[:, t, 3:4], [a])
                x2_t[t] = stt(V, x[:, t, :], eX[ic], rx[:, t, 3:4], x[:, t, :], ALU.mult, ALU.add, [a])
        barrier()
        dump(1)

        c2 = Carve(R2, 13120)
        qkv = c2(4096)
        rp = c2(24, 128)
        qkT = c2(24, 128)
        Pf = c2(16, 128)
        PTf = rp[:, 0:16, :]
        oT = view(R2, 0, 16, 128)
        hT = Pf[:, 0:8, :]
        r2c = Carve(R1, 9248, 8192)
        scz = sb("scz", [128, 8, 5])
        junk = sb("junk", [128, 256])
        sc4 = sb("sc4", [4, 256])
        wk4 = sb("wk4", [4, 256])
        m8 = sb("m8", [4, 8])
        mT = sb("mT", [128, 2, 4])
        cT = sb("cT", [128, 2, 4])
        Sel = qkT[:, 0:8, :]
        SelT = sb("SelT", [128, 8, 128])
        xs = r2c(256)
        xs1 = r2c(256)
        xn = r2c(256)
        cs = sb("cs", [128, 132])
        nT = sb("nT", [128, 2, 128])
        sm = sb("sm", [128, 8])
        mxf = sb("mxf", [128, 3, 16])
        a = G.add(lambda e: e.memset(scz[:, :, :], 0.0))
        t_z = a
        lnt = []
        for t in range(8):
            a = ln(t, [])
            lnt.append(a)
            a = V.add(lambda e, t=t: e.tensor_tensor_reduce(junk[:, :], xh[:, t, :], wrb[:, :], 1.0, 0.0, ALU.mult,
                                                            ALU.add, scz[:, t, t // 2:t // 2 + 1]), [a, t_z, got("k")])
            w = [a]
            if t >= 2:
                w.append(lnt[t])
            a = mm(PE, B[0][0:4, (t % 2) * 128:(t % 2) * 128 + 128], scz[:, t, 0:4], ident[:, :],
                   t == 0, t >= 6, w + free[0], t == 7)
            b = tt(V, x[:, t, :], x[:, t, :], xh[:, t, :], ALU.add, [lnt[t]])
        a = cp(V, sc4[:, :], B[0][0:4, 0:256], [a])
        a = cp(V, wk4[:, :], sc4[:, :], [a])
        for r in range(4):
            a = V.add(lambda e: e.max(m8[:, :], wk4[:, :]), [a])
            a = V.add(lambda e: e.match_replace(wk4[:, :], m8[:, :], wk4[:, :], -3.0e38), [a])
        a = tsc(V, wk4[:, :], wk4[:, :], -3.0e38, None, ALU.is_equal, w=[a])
        for c in range(2):
            a2 = tr(PE, B[1][:, c * 4:c * 4 + 4], wk4[:, c * 128:c * 128 + 128], ident[0:4, 0:4], [a], c == 1)
        a = cp(V, mT[:, :, :], B[1][:, 0:8].rearrange("p (c b) -> p c b", c=2), [a2])
        mm(PE, B[2][:, 0:4], utri[:, :], mT[:, 0, :], True, True, [a])
        mm(PE, B[2][:, 4:8], utri[:, :], mT[:, 1, :], True, False)
        a2 = mm(PE, B[2][:, 4:8], ones[:, :], mT[:, 0, :], False, True, (), True)
        for b in range(4):
            a = stt(V, cT[:, :, b], B[2][:, b:8:4], float(32 * b), mT[:, :, b], ALU.add, ALU.mult, [a2])
        for t in range(8):
            a2 = tsc(V, Sel[:, t, :], iota1[:, :], cT[:, t % 2, t // 2:t // 2 + 1], None, ALU.is_equal, w=[a])
        for t in range(8):
            mm(PE, B[3][:, 0:256], Sel[:, t, :], xh[:, t, :], t == 0, t == 7, [a2])
        for t in range(8):
            mm(PE, B[4][:, 0:128], Sel[:, t, :], rope[:, t % 2, :], t == 0, t == 7, [got("f")])
        a = PE.add(lambda e: e.matmul(B[5][:, 0:4], Sel[:, 0, :], scz[:, 0, 0:4], start=True, stop=False,
                                      skip_group_check=True), (), False)
        for t in range(1, 8):
            a = mm(PE, B[5][:, 0:4], Sel[:, t, :], scz[:, t, 0:4], False, t == 7, (), t == 7)
        t_x = cp(V, xs, B[3][:, 0:256], [a])
        t_cs = acopy(A, cs[:, 0:128], B[4][:, 0:128], [a])
        free[3], free[4] = [t_x], [t_cs]
        t_sc = red(V, sm[:, 0:1], B[5][:, 0:4], ALU.add, [a])
        t_th = act(A, sm[:, 1:2], sm[:, 0:1], ACT.Tanh, [t_sc], scale=0.5)
        t_gate = tsc(V, sm[:, 2:3], sm[:, 1:2], 0.5, 0.5, ALU.mult, ALU.add, [t_th])
        for hf in range(2):
            for t in range(4 * hf, 4 * hf + 4):
                a = tr(PE, B[6 + hf][:, (t % 4) * 128:(t % 4) * 128 + 128], Sel[:, t, :], ident[:, :], (), t % 4 == 3)
            t_selT = acopy(A, SelT[:, 4 * hf:4 * hf + 4, :],
                           B[6 + hf][:, :].rearrange("p (t n) -> p t n", t=4), [a])
            free[6 + hf] = [t_selT]

        def rms(src, col, ln_col, w, bank):
            a = act(A, junk[:, :], src, ACT.Square, w, accum=sm[:, col:col + 1])
            a = tsc(V, sm[:, col:col + 1], sm[:, col:col + 1], 1.0 / 256.0, 1e-6, ALU.mult, ALU.add, [a])
            a = tt(G, sm[:, col:col + 1], sm[:, col:col + 1], mh[:, 0:1], ALU.pow, [a])
            a = tsc(V, xn, src, sm[:, col:col + 1], None, ALU.mult, w=[a] + list(w))
            for c in range(2):
                a2 = tr(PE, B[bank][:, c * 128:c * 128 + 128], xn[:, c * 128:c * 128 + 128], ident[:, :],
                        [a] + free[bank], c == 1)
            for c in range(2):
                a = tsc(V, nT[:, c, :], B[bank][:, c * 128:c * 128 + 128], cols[:, ln_col + c:ln_col + c + 1],
                        None, ALU.mult, w=[a2])
            free[bank] = [a]
            return a

        t_h = rms(xs, 3, 3, [t_x], 1)
        tb = got("f")
        b_of = [0, 2, 3, 4, 5, 6, 7, 1]
        qkv_t = {}
        for i, n in enumerate([4, 5, 0, 1, 2, 3, 6, 7]):
            bk = b_of[i]
            for k in range(2):
                a = mm(PE, B[bk][:, :], nT[:, k, :], wqkv[:, k, n * 512:n * 512 + 512], k == 0, k == 1,
                       [t_h, got("wqkv")] + free[bk], k == 1)
            a = tt(V, qkv[:, n * 512:n * 512 + 512], B[bk][:, :], bqkv[:, n * 512:n * 512 + 512], ALU.add, [a, tb])
            free[bk] = [a]
            qkv_t[n] = a
        cosb = cs[:, 0:64].rearrange("p (o d) -> p o d", o=1)
        sinb = cs[:, 64:128].rearrange("p (o d) -> p o d", o=1)
        tmp = Pf.rearrange("p a b -> p (a b)")
        rp_t = {}
        for i, (eng, h0, nh) in enumerate(((V, 16, 4), (G, 20, 4), (V, 0, 4), (G, 4, 4), (V, 8, 4), (V, 12, 4))):
            src = qkv[:, h0 * 128:(h0 + nh) * 128].rearrange("p (h d) -> p h d", d=128)
            q1, q2 = src[:, :, 0:64], src[:, :, 64:128]
            cb, snb = cosb.to_broadcast([128, nh, 64]), sinb.to_broadcast([128, nh, 64])
            tmpa = tmp[:, (i % 4) * 512:(i % 4) * 512 + 256].rearrange("p (h d) -> p h d", d=64)
            tmpb = tmp[:, (i % 4) * 512 + 256:(i % 4) * 512 + 512].rearrange("p (h d) -> p h d", d=64)
            w = [qkv_t[h0 // 4], t_cs] + ([rp_t[[16, 20, 0, 4, 8, 12][i - 4]]] if i >= 4 else [])
            r1, r2 = rp[:, h0:h0 + nh, 0:64], rp[:, h0:h0 + nh, 64:128]
            a1 = tt(eng, r1, q1, cb, ALU.mult, w)
            a2 = tt(eng, tmpa, q2, snb, ALU.mult)
            a3 = tt(eng, r2, q2, cb, ALU.mult)
            a4 = tt(eng, tmpb, q1, snb, ALU.mult)
            a = tt(eng, r1, r1, tmpa, ALU.subtract, [a2])
            rp_t[h0] = tt(eng, r2, r2, tmpb, ALU.add, [a4])
        qk_t = {}
        for i, h0 in enumerate([16, 20, 0, 4, 8, 12]):
            bk = b_of[i]
            for h in range(4):
                a = tr(PE, B[bk][:, h * 128:h * 128 + 128], rp[:, h0 + h, :], ident[:, :],
                       [rp_t[h0]] + free[bk], h == 3)
            a = acopy(A, qkT[:, h0:h0 + 4, :], B[bk][:, :].rearrange("p (h n) -> p h n", h=4), [a, t_selT])
            free[bk] = [a]
            qk_t[h0] = a
        SF = float(128) ** -0.5
        pf_t, ptf_t = {}, {}
        for g in range(4):
            bk = b_of[g + 1]
            mm(PE, B[bk][:, :], identb[:, :], negm[:, :, :], True, False, [got("kb")] + free[bk])
            for hh in range(4):
                h = 4 * g + hh
                a = mm(PE, B[bk][:, hh * 128:hh * 128 + 128], qkT[:, h, :], qkT[:, 16 + h // 2, :], False, True,
                       [qk_t[4 * g], qk_t[16], qk_t[20]], hh == 3)
            sv = B[bk][:, :].rearrange("p (h n) -> p h n", h=4)
            a = red(V, mxf[:, 0, 4 * g:4 * g + 4], sv, ALU.max, [a])
            a = tsc(V, mxf[:, 1, 4 * g:4 * g + 4], mxf[:, 0, 4 * g:4 * g + 4], -SF, None, ALU.mult, w=[a])
            for hh in range(4):
                h = 4 * g + hh
                a = act(A, Pf[:, h, :], sv[:, hh, :], ACT.Exp, [a] + list(rp_t.values()), bias=mxf[:, 1, h:h + 1],
                        scale=SF, accum=mxf[:, 2, h:h + 1])
            free[bk] = [a]
            a = rec(V, mxf[:, 2, 4 * g:4 * g + 4], mxf[:, 2, 4 * g:4 * g + 4], [a])
            rb = mxf[:, 2, 4 * g:4 * g + 4].rearrange("p (g o) -> p g o", o=1).to_broadcast([128, 4, 128])
            pf_t[g] = tt(V, Pf[:, 4 * g:4 * g + 4, :], Pf[:, 4 * g:4 * g + 4, :], rb, ALU.mult, [a])
        of_t = {}
        for g in range(4):
            bk = (7, 6, 0, 1)[g]
            for hh in range(4):
                a = tr(PE, B[bk][:, hh * 128:hh * 128 + 128], Pf[:, 4 * g + hh, :], ident[:, :],
                       [pf_t[g]] + free[bk], hh == 3)
            ptf_t[g] = acopy(A, PTf[:, 4 * g:4 * g + 4, :], B[bk][:, :].rearrange("p (h n) -> p h n", h=4), [a])
            free[bk] = [ptf_t[g]]
        for g in range(4):
            bk = b_of[g + 1]
            for kv in range(2):
                vh = 2 * g + kv
                a = mm(PE, B[bk][:, kv * 256:kv * 256 + 256], qkv[:, 3072 + vh * 128:3072 + vh * 128 + 128],
                       PTf[:, 2 * vh:2 * vh + 2, :], True, True, [ptf_t[g], qkv_t[6], qkv_t[7]] + free[bk], kv == 1)
            eng = (V, A)[g % 2]
            f = cp if g % 2 == 0 else acopy
            of_t[g] = f(eng, oT[:, 4 * g:4 * g + 4, :], B[bk][:, :].rearrange("p (h n) -> p h n", h=4),
                        [a] + [rp_t[4 * g]])
            free[bk] = [of_t[g]]
        for h in range(16):
            a = mm(PE, B[7][:, 0:256], oT[:, h, :], fwo[:, h, :], h == 0, h == 15, [of_t[h // 4], tb] + free[7], h == 15)
        t_x1 = tt(V, xs1, B[7][:, 0:256], xs, ALU.add, [a])
        t_h = rms(xs1, 4, 5, [t_x1], 1)
        gu_t = {}
        t_hT = []
        for hf in range(2):
            for u in range(2):
                bk = 2 + 2 * hf + u
                for m in range(4):
                    mo = u * 1024 + (4 * hf + m) * 128
                    for k in range(2):
                        a = mm(PE, B[bk][:, m * 128:m * 128 + 128], fgu[:, k, mo:mo + 128], nT[:, k, :],
                               k == 0, k == 1, [t_h] + free[bk], k == 1 and m == 3)
                gu_t[hf, u] = a
            gp = B[2 + 2 * hf][:, :]
            up = B[3 + 2 * hf][:, :]
            th = view(R2, 4096 + hf * 512, 512)
            a = act(A, th, gp, ACT.Tanh, [gu_t[hf, 0], gu_t[0, 1]], scale=0.5)
            a = stt(V, th, th, 1.0, gp, ALU.add, ALU.mult, [a])
            hv = hT[:, 4 * hf:4 * hf + 4, :].rearrange("p a b -> p (a b)")
            a = stt(V, hv, th, 0.5, up, ALU.mult, ALU.mult, [a, gu_t[hf, 1]])
            t_hT.append(a)
        for nm, dst in (("w1q", w1q), ("b1q", b1q), ("w1o", w1o), ("b1o", b1o), ("xv", xv), ("xo", xo)):
            load("m", dst, nm, SP, list(gu_t.values()))
        for m in range(8):
            a = mm(PE, B[6][:, 0:256], hT[:, m, :], fwd[:, m, :], m == 0, m == 7, [t_hT[m // 4]] + free[6], m == 7)
        a2 = tt(V, xs1, xs1, xs, ALU.subtract, [t_h, t_x1])
        a = tt(V, xs1, B[6][:, 0:256], xs1, ALU.add, [a, a2])
        a = tsc(V, xs1, xs1, sm[:, 2:3], None, ALU.mult, w=[a, t_gate])
        for b in range(4):
            bk = (0, 2)[b % 2]
            for c in range(2):
                a2 = mm(PE, B[bk][:, c * 256:c * 256 + 256], SelT[:, 2 * b + c, :], xs1, True, True,
                        [a, t_selT] + free[bk], c == 1)
            xv_ = x[:, 2 * b:2 * b + 2, :]
            a3 = tt(V, xv_, B[bk][:, :].rearrange("p (q n) -> p q n", q=2), xv_, ALU.add, [a2])
            free[bk] = [a3]
        barrier()
        dump(2)

        load("lb", selm, "selm")
        r1_at = r1_base

        def over_r1(name, *shape):
            nonlocal r1_at
            t = nc.alloc_sbuf_tensor_at(name, [128, *shape], F32R, offset=r1_at)
            r1_at += 4 * int(np.prod(shape))
            assert r1_at <= r1_base + 4 * 9248
            return t

        xTh = over_r1("xTh", 2, 512)
        xTl = over_r1("xTl", 2, 512)
        hh_ = [over_r1(f"hh{i}", 512) for i in range(3)]
        hl_ = [over_r1(f"hl{i}", 512) for i in range(3)]
        uh_ = [over_r1(f"uh{i}", 512) for i in range(2)]
        ul_ = [over_r1(f"ul{i}", 512) for i in range(2)]
        dh_ = [over_r1(f"dh{i}", 256) for i in range(4)]
        dl_ = [over_r1(f"dl{i}", 256) for i in range(4)]
        c2 = Carve(R2, 13120)
        fwo_ = fwo[:, :, :].rearrange("p a b -> p (a b)")
        fwd_ = fwd[:, :, :].rearrange("p a b -> p (a b)")
        pr = fwo_
        bq = Carve(bqkv, 4096, 2496)
        q1 = [bq(768) for _ in range(2)]
        sT = Carve(SelT[:, :, :].rearrange("p a b -> p (a b)"), 1024)
        Sx = [sT(256) for _ in range(2)]
        oa = [sT(256) for _ in range(2)]
        ms = [c2(16) for _ in range(2)]
        oaT = [c2(2, 128) for _ in range(2)]
        zin = [c2(2, 256) for _ in range(2)]
        wsem = [DmaSem(sem(f"d_scrw{t}")) for t in range(8)]
        zsem = [DmaSem(sem(f"d_scrr{b}")) for b in range(4)]
        w_t, z_t, zt_t, op_t, oT_t, l1_t, prr = {}, {}, {}, {}, {}, {}, {}
        V.wait([got("m")])

        def l1a_proj(t):
            a = ln(t, [])
            a = xpose(t, [a], 0)
            s = t % 2
            xs_ = [xT[:, k, t * 128:t * 128 + 128] for k in range(2)]
            for k in range(2):
                b = mm(PE, B[0][:, :], xs_[k], w1q[:, k, 0:512], k == 0, k == 1, [a, got("m")] + free[0], k == 1)
            w = [l1_t[t - 2]] if t - 2 in l1_t else []
            free[0] = [tt(V, q1[s][:, 0:512], B[0][:, :], b1q[:, 0:512], ALU.add, [b] + w)]
            for k in range(2):
                b = mm(PE, B[1][:, 0:256], xs_[k], w1q[:, k, 512:768], k == 0, k == 1, free[1], k == 1)
            b = tt(V, q1[s][:, 512:768], B[1][:, 0:256], b1q[:, 512:768], ALU.add, [b])
            free[1] = [b]
            return b

        def l1a_attn(t, pool, ready):
            s = t % 2
            q3 = q1[s][:, 0:256].rearrange("p (h o d) -> p h o d", o=1, d=16)
            k3 = q1[s][:, 256:512].rearrange("p (o g d) -> p o g d", o=1, d=16).to_broadcast([128, 4, 16, 16])
            sh = [128, 4, 16, 16]
            reds = []
            engs = [G, V, G, V] if pool else [V] * 4
            mt = []
            for i in range(4):
                pv4 = pr[:, i * 1024:(i + 1) * 1024].rearrange("p (h g d) -> p h g d", g=16, d=16)
                mt.append(tt(engs[i], pv4, q3[:, 4 * i:4 * i + 4].to_broadcast(sh), k3, ALU.mult, [ready] + prr.get(i, [])))
                if not pool:
                    yield
            for i in ((1, 3, 0, 2) if pool else range(4)):
                pv4 = pr[:, i * 1024:(i + 1) * 1024].rearrange("p (h g d) -> p h g d", g=16, d=16)
                Sv = Sx[s][:, i * 64:i * 64 + 64].rearrange("p (h g) -> p h g", g=16)
                a = red(V, Sv, pv4, ALU.add, [mt[i]])
                prr[i] = [a]
                yield
            Sv = Sx[s].rearrange("p (h g) -> p h g", g=16)
            a = red(V, ms[s], Sv, ALU.max, [a])
            msb = ms[s].rearrange("p (h o) -> p h o", o=1).to_broadcast([128, 16, 16])
            a = tt(V, Sv, Sv, msb, ALU.subtract, [a])
            a = act(A, Sx[s], Sx[s], ACT.Exp, [a], scale=1.0 / 16.0)
            yield
            a = red(V, ms[s], Sv, ALU.add, [a])
            a = rec(V, ms[s], ms[s], [a])
            a = tt(V, Sv, Sv, msb, ALU.mult, [a])
            yield
            tP = a
            mt = []
            if pool:
                for i in range(4):
                    Pg = Sx[s].rearrange("p (h g o) -> p g h o", g=16, o=1)[:, 4 * i:4 * i + 4].to_broadcast(sh)
                    vg = q1[s][:, 512 + 64 * i:512 + 64 * i + 64].rearrange("p (g o d) -> p g o d", o=1, d=16).to_broadcast(sh)
                    pv4 = pr[:, i * 1024:(i + 1) * 1024].rearrange("p (g h d) -> p g h d", h=16, d=16)
                    mt.append(tt(engs[i], pv4, Pg, vg, ALU.mult, [tP] + prr[i]))
                n = 0
                for i in (1, 0, 3, 2):
                    for g in range(4):
                        a = mm(PE, B[0][:, 0:256], ident[:, :], pr[:, i * 1024 + g * 256:i * 1024 + g * 256 + 256],
                               n == 0, n == 15, [mt[i]] + free[0], g == 3)
                        n += 1
                    prr[i] = [a]
                a = acopy(A, oa[s], B[0][:, 0:256], [a] + ([oT_t[t - 2]] if t - 2 in oT_t else []))
                free[0] = [a]
                l1_t[t] = a
                yield
            else:
                for i in range(4):
                    P4 = Sx[s][:, i * 64:i * 64 + 64].rearrange("p (h o g) -> p h o g", o=1, g=16).to_broadcast(sh)
                    vd = q1[s][:, 512:768].rearrange("p (o g d) -> p o d g", o=1, d=16).to_broadcast(sh)
                    pv4 = pr[:, i * 1024:(i + 1) * 1024].rearrange("p (h d g) -> p h d g", g=16, d=16)
                    mt.append(tt(V, pv4, P4, vd, ALU.mult, [tP] + prr[i]))
                    yield
                for i in range(4):
                    pv4 = pr[:, i * 1024:(i + 1) * 1024].rearrange("p (h d g) -> p h d g", g=16, d=16)
                    a = red(V, oa[s][:, i * 64:i * 64 + 64].rearrange("p (h d) -> p h d", d=16), pv4, ALU.add,
                            [mt[i]] + ([oT_t[t - 2]] if t - 2 in oT_t else []))
                    prr[i] = [a]
                    yield
                l1_t[t] = a
            b, c = divmod(t, 2)
            dst = D["scr"][b, :, c * 128:c * 128 + 128, :].rearrange("h n d -> n h d")
            w_t[t] = wsem[t].load(SP, dst, oa[s].rearrange("p (h d) -> p h d", d=16), [a])
            oT_t[t] = w_t[t]
            if c == 1:
                src = D["scr"][b].rearrange("(q h) (m l) d -> (h m) q (l d)", q=2, l=16)
                z_t[b] = zsem[b].load(SP, zin[b % 2], src, [w_t[t - 1], w_t[t]] + ([zt_t[b - 2]] if b >= 2 else []))

        def l1a_out(b):
            for q in range(2):
                t = 2 * b + q
                for c in range(2):
                    m = tr(PE, B[1][:, c * 128:c * 128 + 128], zin[b % 2][:, q, c * 128:c * 128 + 128], ident[:, :],
                           [z_t[b]] + free[1], c == 1)
                zt_t[b] = m
                m = acopy(A, oaT[q], B[1][:, 0:256].rearrange("p (c n) -> p c n", c=2), [m] + ([op_t[q]] if b else []))
                free[1] = [m]
                for k in range(2):
                    m = mm(PE, B[1][:, 256:512], oaT[q][:, k, :], w1o[:, k, :], k == 0, k == 1, [m] + free[1], k == 1)
                op_t[q] = m
                m = tt(V, x[:, t, :], B[1][:, 256:512], x[:, t, :], ALU.add, [m])
                free[1] = [m]
                x3_t[t] = tt(V, x[:, t, :], x[:, t, :], b1o, ALU.add, [m])
                yield

        x3_t = {}

        def l1a(tiles, pool):
            ready = l1a_proj(tiles[0])
            yield
            for t in tiles:
                nxt = ready
                if t + 1 in tiles:
                    nxt = l1a_proj(t + 1)
                    yield
                yield from l1a_attn(t, pool, ready)
                ready = nxt
                if t % 2 == 0 and t != tiles[0]:
                    yield from l1a_out(t // 2 - 1)
            for _ in range(3):
                yield
            yield from l1a_out(tiles[-1] // 2)

        qT_ = [c2(4, 256) for _ in range(2)]
        kT_ = [c2(4, 256) for _ in range(2)]
        va = [c2(2, 16, 17) for _ in range(2)]
        Px = [c2(3, 128) for _ in range(4)]
        PTx = [c2(3, 128) for _ in range(4)]
        OxT = c2(4, 256)
        Ox = view(fwd_, 0, 2, 256)
        OTx = view(fwd_, 512, 2, 256)
        mxx = [c2(4) for _ in range(4)]
        rcx = c2(2, 16)
        t_v1 = [G.add(lambda e, s=s: e.memset(va[s][:, :, :, 16:17], 1.0)) for s in range(2)][-1]
        t_ox = G.add(lambda e: e.memset(OxT, 0.0))
        negx3 = sb("negx3", [128, 3, 128], BF16)
        G.add(lambda e: e.memset(negx3[:, 1, :], 0.0))
        G.add(lambda e: e.tensor_copy(negx3[:, 0, :], negm[:, 0, :]), [got("kb")])
        t_ng = G.add(lambda e: e.tensor_copy(negx3[:, 2, :], negm[:, 0, :]))
        negx = negx3[:, :, :]
        pre = {}
        last_S, last_PV, ox_t, on_t, ot_t = {}, {}, {}, {}, {}
        xP, xT_t, xPT, xPV = {}, {}, {}, {}
        SX = 0.25
        x4_t = {}

        def l1x_pre(b):
            s = b % 2
            for t in (2 * b, 2 * b + 1):
                a = ln(t, [x3_t[t]])
                a = xpose(t, [a], 6, V)
            bs = slice(b * 256, b * 256 + 256)
            w = [last_S[b - 2]] if b >= 2 else []
            toks = []
            yield
            for g in range(2):
                for cc in range(2):
                    c = 2 * g + cc
                    for k in range(2):
                        m = mm(PE, B[7][:, cc * 256:cc * 256 + 256], xq[:, k, c, :], xT[:, k, bs],
                               k == 0, k == 1, [a, got("l")] + free[7], k == 1 and cc == 1)
                m = acopy(A, qT_[s][:, 2 * g:2 * g + 2, :], B[7][:, :].rearrange("p (c n) -> p c n", c=2), [m] + w)
                free[7] = [m]
                toks.append(m)
                yield
                for cc in range(2):
                    m = mm(PE, B[6][:, cc * 256:cc * 256 + 256], xk[:, 2 * g + cc, :], ctxT[0:64, bs], True, True,
                           free[6], cc == 1)
                m = cp(V, kT_[s][:, 2 * g:2 * g + 2, :], B[6][:, :].rearrange("p (c n) -> p c n", c=2), [m] + w)
                free[6] = [m]
                toks.append(m)
                yield
            w = [last_PV[b - 2]] if b >= 2 else []
            for c in range(2):
                m = mm(PE, B[7][:, c * 256:c * 256 + 256], ctxT[0:64, (2 * b + c) * 128:(2 * b + c) * 128 + 128], xv,
                       True, True, free[7], c == 1)
            for c in range(2):
                m2 = acopy(A, va[s][:, c, :, 0:16], B[7][:, c * 256:c * 256 + 256].rearrange("p (h d) -> p h d", d=16),
                           [m, t_v1] + w)
            free[7] = [m2]
            pre[b] = toks + [m2]
            yield

        def xs_step(b, h):
            i = b * 16 + h
            s = b % 2
            c, j = divmod(h, 4)
            bk = 2 + i % 2
            r = slice(32 * j, 32 * j + 32)
            Q = qT_[s][r, c, :]
            Kk = kT_[s][r, c, :]
            mm(PE, B[bk][:, 0:384], identb[:, :], negx, True, False, pre[b] + free[bk] + [t_ng])
            mm(PE, B[bk][:, 0:128], Q[:, 0:128], Kk[:, 0:128], False, True)
            a = mm(PE, B[bk][:, 128:384], Q[:, 128:256], Kk[:, 0:256], False, True, (), True)
            last_S[b] = a
            m = i % 4
            w = [a] + ([xP[i - 4]] if i >= 4 else [])
            red(V, mxx[m][:, 0:1], B[bk][:, 0:128], ALU.max, w)
            a = red(V, mxx[m][:, 1:2], B[bk][:, 128:384], ALU.max)
            a = tsc(V, mxx[m][:, 2:4], mxx[m][:, 0:2], -SX, None, ALU.mult, w=[a])
            w = [a] + ([xT_t[i - 4]] if i >= 4 else [])
            act(A, Px[m][:, 0, :], B[bk][:, 0:128], ACT.Exp, w, bias=mxx[m][:, 2:3], scale=SX)
            a = act(A, Px[m][:, 1:3, :].rearrange("p a b -> p (a b)"), B[bk][:, 128:384], ACT.Exp, (),
                    bias=mxx[m][:, 3:4], scale=SX)
            free[bk] = [a]
            xP[i] = a

        def xt_step(b, h):
            i = b * 16 + h
            m = i % 4
            for c in range(3):
                a = tr(PE, B[4][:, c * 128:c * 128 + 128], Px[m][:, c, :], ident[:, :], [xP[i]] + free[4], c == 2)
            xT_t[i] = a
            w = [a] + ([xPV[i - 4]] if i >= 4 else [])
            a = acopy(A, PTx[m], B[4][:, 0:384].rearrange("p (c n) -> p c n", c=3), w)
            free[4] = [a]
            xPT[i] = a

        def xpv_step(b, h):
            i = b * 16 + h
            s = b % 2
            m = i % 4
            c, j = divmod(h, 4)
            o = B[5][32 * j:32 * j + 17, 0:256]
            mm(PE, o, va[s][:, 0, h, :], PTx[m][:, 0:2, :], True, False, [xPT[i]] + free[5])
            a = mm(PE, o[:, 128:256], va[s][:, 1, h, :], PTx[m][:, 2, :], False, True, (), True)
            xPV[i] = a
            last_PV[b] = a
            for_rows = slice(32 * j, 32 * j + 17)
            a = cp(V, OxT[for_rows, c, :], o, [a, t_ox] + ([ox_t[b - 1]] if b - 1 in ox_t else []))
            free[5] = [a]
            ot_t[b] = a

        def x_end(b):
            for qc in range(2):
                for c in range(4):
                    m = tr(PE, B[6][:, c * 128:c * 128 + 128], OxT[:, c, qc * 128:qc * 128 + 128], ident[:, :],
                           [ot_t[b]] + free[6], c == 3)
                if qc == 1:
                    ox_t[b] = m
                src = B[6][:, :].rearrange("p (h d) -> p h d", d=32)
                a = rec(V, rcx[:, qc, :], src[:, :, 16], [m])
                a = tt(V, Ox[:, qc, :].rearrange("p (h d) -> p h d", d=16), src[:, :, 0:16],
                       rcx[:, qc, :].rearrange("p (h o) -> p h o", o=1).to_broadcast([128, 16, 16]), ALU.mult,
                       [a] + ([on_t[b - 1]] if b - 1 in on_t else []))
                free[6] = [a]
            yield
            for c in range(2):
                for qc in range(2):
                    m = tr(PE, B[6][:, c * 256 + qc * 128:c * 256 + qc * 128 + 128], Ox[:, qc, c * 128:c * 128 + 128],
                           ident[:, :], [a] + free[6], c == 1 and qc == 1)
            on_t[b] = m
            m = acopy(A, OTx, B[6][:, :].rearrange("p (c n) -> p c n", c=2), [m] + ([x4_pe[b - 1]] if b - 1 in x4_pe else []))
            free[6] = [m]
            for qc in range(2):
                for k in range(2):
                    a = mm(PE, B[7][:, qc * 256:qc * 256 + 256], OTx[:, k, qc * 128:qc * 128 + 128], xo[:, k, :],
                           k == 0, k == 1, [m] + free[7], k == 1 and qc == 1)
            x4_pe[b] = a
            xv_ = x[:, 2 * b:2 * b + 2, :]
            a = tt(V, xv_, B[7][:, :].rearrange("p (q n) -> p q n", q=2), xv_, ALU.add, [a])
            free[7] = [a]
            x4_t[b] = a
            yield

        x4_pe = {}

        def l1x(b0, first_pre=True):
            if first_pre:
                yield from l1x_pre(b0)
            late = []
            heads = [(b, h) for b in (b0, b0 + 1) for h in range(16)]
            extra_ = []
            for i in range(len(heads) + 4):
                if i < len(heads):
                    xs_step(*heads[i])
                    if i == 6:
                        extra_.append(l1x_pre(b0 + 1))
                if 2 <= i <= len(heads) + 1:
                    xt_step(*heads[i - 2])
                if i >= 4:
                    xpv_step(*heads[i - 4])
                    if heads[i - 4][1] == 15:
                        b = heads[i - 4][0]
                        extra_.append(x_end(b))
                        if b == b0:
                            extra_.append(router(2 * b, 2 * b + 1))
                if extra_ and next(extra_[0], "end") == "end":
                    extra_.pop(0)
                yield
            for g in extra_:
                yield from g
            yield from router(2 * b0 + 2, 2 * b0 + 3)

        xTm = xT
        p30 = [c2(30) for _ in range(2)]
        r30 = [c2(30) for _ in range(2)]
        m8b = [c2(8) for _ in range(2)]
        rr = [c2(4) for _ in range(2)]
        cwr = [c2(28) for _ in range(2)]
        cwp = [sb(f"cwp{i}", [128, 3, 28], BF16) for i in range(2)]
        cwT = fg[0:84, 3840:4096].bitcast(BF16)
        for i in range(2):
            G.add(lambda e, i=i: e.memset(p30[i][:, 28:29], 2.0))
            t_pad = G.add(lambda e, i=i: e.memset(p30[i][:, 29:30], 3.0))
        cw_t, cwc_t, xs_t = {}, {}, {}
        moe_last = []

        def router(*tiles):
            for t in tiles:
                s = t % 2
                bk = 6 + s
                hs = slice((t % 4) * 128, (t % 4) * 128 + 128)
                a = ln(t, [x4_t[t // 2]])
                for c in range(2):
                    a2 = tr(PE, B[bk][:, c * 128:c * 128 + 128], xh[:, t, c * 128:c * 128 + 128], ident[:, :],
                            [a] + free[bk], c == 1)
                src = B[bk][:, 0:256].rearrange("p (c n) -> p c n", c=2)
                f = acopy(A, xT[:, :, t * 128:t * 128 + 128], src, [a2])
                h_ = acopy(A, xTh[:, :, hs], src, moe_last)
                l_ = tt(V, xTl[:, :, hs], src, xTh[:, :, hs], ALU.subtract, [h_])
                free[bk] = [h_, l_]
                xs_t[t] = l_
                yield
                for k in range(2):
                    a = mm(PE, B[bk][:, 256:284], xT[:, k, t * 128:t * 128 + 128], gt[:, k, :], k == 0, k == 1,
                           [f, l_] + free[bk], k == 1)
                lg = B[bk][:, 256:284]
                a = V.add(lambda e, s=s, lg=lg: e.tensor_reduce(rr[s][:, 0:1], lg, X, ALU.max, negate=True), [a])
                a = act(A, p30[s][:, 0:28], lg, ACT.Exp, [a, t_pad], bias=rr[s][:, 0:1], accum=rr[s][:, 1:2])
                free[bk] = [a]
                yield
                a = rec(V, rr[s][:, 2:3], rr[s][:, 1:2], [a])
                a = tsc(V, p30[s][:, 0:28], p30[s][:, 0:28], rr[s][:, 2:3], None, ALU.mult, w=[a])
                a = V.add(lambda e, s=s: e.max(m8b[s], p30[s]), [a])
                a = V.add(lambda e, s=s: e.match_replace(r30[s], m8b[s], p30[s], 0.0), [a])
                a = tt(V, r30[s][:, 0:28], p30[s][:, 0:28], r30[s][:, 0:28], ALU.subtract, [a])
                a = red(V, rr[s][:, 3:4], r30[s][:, 0:28], ALU.add, [a])
                a = tsc(V, rr[s][:, 3:4], rr[s][:, 3:4], 1e-20, None, ALU.add, w=[a])
                a = rec(V, rr[s][:, 3:4], rr[s][:, 3:4], [a])
                a = tsc(V, cwr[s], r30[s][:, 0:28], rr[s][:, 3:4], None, ALU.mult, w=[a])
                w = [cw_t[t - 2]] if t >= 2 else []
                a = cp(V, cwp[s][:, 0, :], cwr[s], [a] + w)
                a = tt(V, cwr[s], cwr[s], cwp[s][:, 0, :], ALU.subtract, [a])
                a = cp(V, cwp[s][:, 1, :], cwr[s], [a])
                a = tt(V, cwr[s], cwr[s], cwp[s][:, 1, :], ALU.subtract, [a])
                a = cp(V, cwp[s][:, 2, :], cwr[s], [a])
                yield
                pb = B[bk][:, :].bitcast(BF16)
                a = tr(PE, pb[0:84, 0:128], cwp[s][:, :, :].rearrange("p a b -> p (a b)"), identb[:, :],
                       [a] + free[bk], True)
                cw_t[t] = a
                a = cp(V, cwT[:, hs], pb[0:84, 0:128], [a] + moe_last)
                free[bk] = [a]
                cwc_t[t] = a
                yield

        NR = 2
        ring = [c2(768) for _ in range(NR)]
        thb = [view(fwd_, 1024 + 512 * i, 512) for i in range(2)]
        rd = [DmaSem(sem(f"ring{i}")) for i in range(NR)]
        steps = [(hf, c) for hf in range(2) for c in range(NCH)]
        ring_t, ring_free = {}, [[] for _ in range(NR)]
        usp, dsp, g_t, h_t, hrd, hp_t, up_pe = {}, {}, {}, {}, {}, {}, {}
        LAG = 2

        def fetch(n):
            if n < len(steps):
                ring_t[n] = rd[n % NR].load(SP, ring[n % NR], D["wmo"][steps[n][1], :, :], ring_free[n % NR])

        def wsplit(n):
            if n < len(steps):
                s, r, d = n % 2, ring[n % NR], n % 4
                w = [ring_t[n]] + ([up_pe[n - 2]] if n >= 2 else [])
                a = acopy(A, uh_[s][:, :], r[:, 0:512], w)
                b = tt(G, ul_[s][:, :], r[:, 0:512], uh_[s][:, :], ALU.subtract, [a])
                usp[n] = [a, b]
                a = acopy(A, dh_[d][:, :], r[:, 512:768], [hrd[n - 4]] if n >= 4 else [])
                b = tt(G, dl_[d][:, :], r[:, 512:768], dh_[d][:, :], ALU.subtract, [a])
                dsp[n] = [a, b]
                ring_free[n % NR] = [b]
                fetch(n + NR)

        def three(out_, lh, ll, rh, rl, start, stop, w, inc=False):
            mm(PE, out_, lh, rh, start, False, w)
            mm(PE, out_, lh, rl, False, False)
            return mm(PE, out_, ll, rh, False, stop, (), inc)

        def moe_up(n):
            hf, c = steps[n]
            s = n % 2
            Wh = uh_[s][:, :].rearrange("p (j m) -> p j m", m=128)
            Wl = ul_[s][:, :].rearrange("p (j m) -> p j m", m=128)
            bk = [4 + (3 * n + i) % 4 for i in range(3)]
            for u in range(2):
                for k in range(2):
                    a = three(B[bk[u]][:, :], Wh[:, 2 * k + u, :], Wl[:, 2 * k + u, :], xTh[:, k, :], xTl[:, k, :],
                              k == 0, k == 1, usp[n] + [xs_t[4 * hf + q] for q in range(4)] + free[bk[u]], k == 1)
                if u == 0:
                    g_ = a
            up_pe[n] = a
            a = mm(PE, B[bk[2]][:, :], selm[:, c * 128:c * 128 + 128], cwT, True, True,
                   [cwc_t[4 * hf + q] for q in range(4)] + [got("lb")] + free[bk[2]], True)
            gp, up, cb = [B[i][:, :] for i in bk]
            th = thb[s]
            t1 = act(A, th, gp, ACT.Silu, [g_] + ([hp_t[n - 2]] if n >= 2 else []))
            free[bk[0]] = [t1]
            t1 = tt(V, th, up, th, ALU.mult, [t1, a])
            free[bk[1]] = [t1]
            t1 = tt(V, th, cb, th, ALU.mult, [t1])
            free[bk[2]] = [t1]
            m = n % 3
            w = [t1] + ([hrd[n - 3]] if n >= 3 else [])
            a1 = acopy(A, hh_[m][:, :], th, w)
            a2 = tt(G, hl_[m][:, :], th, hh_[m][:, :], ALU.subtract, [a1])
            hp_t[n] = a2
            h_t[n] = [a1, a2]

        outs = []

        def moe_down(n):
            hf, c = steps[n]
            m = n % 3
            if c == 0:
                for q in range(2):
                    mm(PE, B[2 + q][:, :], zb[0:1, 0:128], zb[0:1, :], True, False, [t_zb] + free[2 + q])
            for q in range(4):
                qs = slice(q * 128, q * 128 + 128)
                a = three(B[2 + q // 2][:, (q % 2) * 256:(q % 2) * 256 + 256], hh_[m][:, qs], hl_[m][:, qs],
                          dh_[n % 4][:, :], dl_[n % 4][:, :], False, c == NCH - 1, h_t[n] + dsp[n], q == 3)
            hrd[n] = a
            if c == NCH - 1:
                moe_last[:] = [a]
                for q in range(2):
                    t0 = 4 * hf + 2 * q
                    xv_ = x[:, t0:t0 + 2, :]
                    b = tt(V, xv_, B[2 + q][:, :].rearrange("p (q n) -> p q n", q=2), xv_, ALU.add, [a])
                    free[2 + q] = [b]
                    outs.append(dsems["out"].load(SP, D["outv"][:, t0:t0 + 2, :], xv_, [b]))

        def moe(hf):
            n0 = hf * NCH
            for c in range(NCH + LAG):
                if c < NCH:
                    wsplit(n0 + c + 1)
                    moe_up(n0 + c)
                if c >= LAG:
                    moe_down(n0 + c - LAG)
                yield

        dsems["out"] = DmaSem(sem("d_out"))
        for n in range(NR):
            fetch(n)

        def drive(main, side, ratio):
            due = 0.0
            for _ in main:
                due += ratio
                while side is not None and due >= 1.0:
                    due -= 1.0
                    if next(side, "end") == "end":
                        side = None
            return side

        mark("L1 start")
        for _ in l1a(range(0, 4), True):
            pass
        mark("L1A h0")
        side = l1a(range(4, 8), False)
        side = drive(l1x(0), side, 1.0)
        wsplit(0)
        mark("L1X h0")
        side = drive(moe(0), side, 2.0)
        for _ in side or ():
            pass
        mark("MoE h0")
        drive(l1x(2), None, 0)
        mark("L1X h1")
        drive(moe(1), None, 0)
        mark("end")
        if debug:
            SP.wait([dsems["dbg"].all()])
        SP.wait([dsems["out"].all()])
        SP.wait([q.now() for q in (PE, V, A, G)])

        block = ctx.enter_context(nc.Block())

        @block.sync
        def _(e):
            SP.play(e)

        @block.tensor
        def _(e):
            PE.play(e)

        @block.vector
        def _(e):
            V.play(e)

        @block.scalar
        def _(e):
            A.play(e)

        @block.gpsimd
        def _(e):
            G.play(e)


def lay(inp):
    f = np.float32
    i = {k: np.asarray(v) for k, v in inp.items()}
    d = {}

    def kc(w):
        return w.reshape(-1, 128, w.shape[1]).transpose(1, 0, 2)

    def bcast(v):
        return np.broadcast_to(v.reshape(1, -1), (128, v.size))

    d["x"] = i["x"].reshape(8, 128, 256).transpose(1, 0, 2)
    d["ident"] = np.eye(128, dtype=f)
    wk = i["L0_attn_W_DKV_w"].T
    d["wdkv"] = kc(np.concatenate([wk, wk], 1))
    d["wdq"] = kc(i["L0_attn_W_DQ_w"].T)
    cols = np.zeros((128, 8), f)
    cols[:, 0] = np.concatenate([i["L0_attn_W_DKV_b"]] * 2)
    cols[:, 1] = i["L0_attn_W_DQ_b"][0:128]
    cols[0:64, 2] = i["L0_attn_W_DQ_b"][128:192]
    cols[:, 3:5] = i["L0_ffn_ln1_w"].reshape(2, 128).T
    cols[:, 5:7] = i["L0_ffn_ln2_w"].reshape(2, 128).T
    d["cols"] = cols
    d["bkvb"] = bcast(i["L0_attn_W_DKV_b"])
    hd = lambda w: w.reshape(16, 128, -1).transpose(1, 0, 2)
    d["wuq"] = np.concatenate([hd(i["L0_attn_W_UQ_w"]), hd(i["L0_attn_W_UQ_b"])], 2)
    d["wuk"] = np.concatenate([hd(i["L0_attn_W_UK_w"]), hd(i["L0_attn_W_UK_b"])], 2)
    d["wuv"] = hd(i["L0_attn_W_UV_w"])
    d["buv"] = i["L0_attn_W_UV_b"].reshape(16, 128).T
    d["wot"] = hd(i["L0_attn_W_O_w"].T)
    d["bo"] = i["L0_attn_W_O_b"].reshape(1, 256)
    d["ctxT"] = np.concatenate([i["ctx_512"].reshape(1024, 64).T, np.ones((1, 1024), f)], 0)
    d["wk1"] = np.concatenate([i["L0_xattn_W_k"].T, i["L0_xattn_b_k"].reshape(1, 64)], 0)
    d["gb"] = np.stack([bcast(i["L0_xattn_ln_gamma"]), bcast(i["L0_xattn_ln_beta"])], 1)
    d["wrb"] = bcast(i["L0_ffn_w_router"])
    d["utri"] = np.triu(np.ones((128, 128), f))
    d["iota1"] = np.broadcast_to(np.arange(1, 129, dtype=f).reshape(1, 128), (128, 128))
    bf = mybir.dt.np(BF16)
    d["identb"] = np.eye(128, dtype=f).astype(bf)
    neg = np.where(np.tril(np.ones((128, 128), bool)), 0.0, NEG).astype(f)
    d["negm"] = np.broadcast_to(neg.reshape(128, 1, 128), (128, 4, 128)).astype(bf)
    d["bqkv"] = bcast(np.concatenate([i["L0_ffn_bq"], i["L0_ffn_bk"], i["L0_ffn_bv"]]))
    d["wqkv"] = kc(np.concatenate([i["L0_ffn_wq"], i["L0_ffn_wk"], i["L0_ffn_wv"]], 1))
    d["fwo"] = kc(i["L0_ffn_wo"])
    d["fgu"] = kc(np.concatenate([i["L0_ffn_w_gate"], i["L0_ffn_w_up"]], 1))
    d["fwd"] = kc(i["L0_ffn_w_down"])
    inv = (1.0 / np.power(f(10000.0), np.arange(0, 128, 2, dtype=f) / f(128))).astype(f)
    ang = np.arange(256, dtype=f)[:, None] * inv
    d["rope"] = kc(np.concatenate([np.cos(ang), np.sin(ang)], 1).astype(f))
    d["w1q"] = kc(i["L1_attn_w_qkv"].T)
    d["b1q"] = bcast(i["L1_attn_b_qkv"])
    d["w1o"] = kc(i["L1_attn_w_out"].T)
    d["b1o"] = bcast(i["L1_attn_b_out"])

    def pad(w):
        o = np.zeros((w.shape[0], 16, 32), f)
        o[:, :, 0:16] = w.reshape(-1, 16, 16)
        return o.reshape(-1, 4, 128)

    d["xq"] = pad(i["L1_xattn_Wq"].T).reshape(2, 128, 4, 128).transpose(1, 0, 2, 3)
    d["xk"] = pad(i["L1_xattn_Wkv_expand"][0:256].T)
    d["xv"] = i["L1_xattn_Wkv_expand"][256:512].T
    d["xo"] = kc(i["L1_xattn_Wout"].T)
    d["gt"] = kc(i["L1_ffn_gate_weight"].T)
    e = np.zeros((3, 28, NCH * 128), f)
    for k in range(28):
        e[:, k, k * 176:(k + 1) * 176] = 1.0
    d["selm"] = e.reshape(84, NCH * 128).astype(bf)
    w = np.zeros((NCH * 128, 768), f)
    for u, nm in enumerate(("L1_ffn_w_gate", "L1_ffn_w_up")):
        a = i[nm].transpose(0, 2, 1).reshape(4928, 2, 128)
        full = np.zeros((NCH * 128, 2, 128), f)
        full[0:4928] = a
        full = full.reshape(NCH, 128, 2, 128).transpose(0, 3, 2, 1)
        w.reshape(NCH, 128, 6, 128)[:, :, u, :] = full[:, :, 0]
        w.reshape(NCH, 128, 6, 128)[:, :, 2 + u, :] = full[:, :, 1]
    w[0:4928, 512:768] = i["L1_ffn_w_down"].reshape(4928, 256)
    d["wmo"] = w.reshape(NCH, 128, 768)
    return {k: np.ascontiguousarray(v) for k, v in d.items()}


def extra(nc, D, o):
    D["scr"] = nc.dram_tensor("scr", (4, 16, 256, 16), F32).ap()
    D["outv"] = o.rearrange("b (c p) n -> p (b c) n", p=128)


DEBUG = None


def kernel(**inputs):
    import concourse.bacc as _bacc
    from concourse.bass_utils import run_bass_kernel_spmd as _run

    nc = _bacc.Bacc("TRN2", target_bir_lowering=False, num_devices=1)
    arrays, D = {}, {}
    for name, a in lay(inputs).items():
        arrays[f"in_{name}"] = a
        D[name] = nc.dram_tensor(f"in_{name}", a.shape, mybir.dt.from_np(a.dtype), kind="ExternalInput").ap()
    o = nc.dram_tensor("out_0", (4, 256, 256), F32, kind="ExternalOutput").ap()
    extra(nc, D, o)
    if DEBUG:
        D["dbg"] = nc.dram_tensor("dbg", (5, 128, 8, 256), F32, kind="ExternalOutput").ap()
    program(nc, D, o, DEBUG)
    r = _run(nc, [arrays], core_ids=[0])
    if DEBUG:
        return r.results[0]["out_0"], r.results[0]["dbg"]
    return r.results[0]["out_0"]
```

```python
from contextlib import ExitStack

import numpy as np
import concourse.bass as bass
from concourse import mybir

F32 = mybir.dt.float32
BF16 = mybir.dt.bfloat16
F32R = mybir.dt.float32r
ALU = mybir.AluOpType
ACT = mybir.ActivationFunctionType
X = mybir.AxisListType.X
NEG = -1.0e30
NCH = 39


class Queue:

    def __init__(self, sem, chain=False):
        self.sem = sem
        self.n = 0
        self.ops = []
        self.seen = {}
        self.chain = chain

    def wait(self, toks):
        need = {}
        for s, v in toks:
            if self.seen.get(s.name, 0) < v:
                need[s.name] = (s, max(v, need.get(s.name, (s, 0))[1]))
        for s, v in need.values():
            self.seen[s.name] = v
            self.ops.append(lambda e, s=s, v=v: e.wait_ge(s, v))

    def add(self, fn, toks=(), inc=True):
        self.wait(toks)
        if self.chain and self.n:
            self.wait([self.now()])
        if inc:
            self.n += 1
            self.ops.append(lambda e, fn=fn: fn(e).then_inc(self.sem, 1))
        else:
            self.ops.append(fn)
        return (self.sem, self.n)

    def now(self):
        return (self.sem, self.n)

    def play(self, e):
        for f in self.ops:
            f(e)


class DmaSem:
    def __init__(self, sem):
        self.sem = sem
        self.n = 0

    def load(self, q, out, in_, toks=()):
        q.wait(toks)
        self.n += 16
        q.ops.append(lambda e: e.dma_start(out, in_).then_inc(self.sem, 16))
        return (self.sem, self.n)

    def all(self):
        return (self.sem, self.n)


def tt(q, out, a, b, op, w=()):
    return q.add(lambda e: e.tensor_tensor(out, a, b, op), w)


def tsc(q, out, a, s1, s2, op0, op1=None, w=()):
    if op1 is None:
        return q.add(lambda e: e.tensor_scalar(out, a, s1, None, op0), w)
    return q.add(lambda e: e.tensor_scalar(out, a, s1, s2, op0, op1), w)


def stt(q, out, a, s, b, op0, op1, w=()):
    return q.add(lambda e: e.scalar_tensor_tensor(out=out, in0=a, scalar=s, in1=b, op0=op0, op1=op1), w)


def red(q, out, a, op, w=()):
    return q.add(lambda e: e.tensor_reduce(out, a, X, op), w)


def cp(q, out, a, w=()):
    return q.add(lambda e: e.tensor_copy(out, a), w)


def rec(q, out, a, w=()):
    return q.add(lambda e: e.reciprocal(out, a), w)


def act(q, out, a, func, w=(), bias=0.0, scale=1.0, accum=None):
    if accum is not None:
        return q.add(lambda e: e.activation(out, a, func, bias=bias, scale=scale, accum_out=accum), w)
    return q.add(lambda e: e.activation(out, a, func, bias=bias, scale=scale), w)


def acopy(q, out, a, w=()):
    return q.add(lambda e: e.activation(out, a, ACT.Copy), w)


def mm(q, out, l, r, start, stop, w=(), inc=False):
    return q.add(lambda e: e.matmul(out, l, r, start=start, stop=stop, skip_group_check=True), w, inc)


def tr(q, out, a, ident, w=(), inc=False):
    return q.add(lambda e: e.transpose(out, a, ident), w, inc)


def program(nc, D, out):
    ctx = ExitStack()
    with ctx:
        def sb(name, shape, dt=F32):
            return ctx.enter_context(nc.sbuf_tensor(name, shape, dt))

        def sem(name):
            return ctx.enter_context(nc.semaphore(name))

        PE, V, A, G, SP = [Queue(sem("q_" + n), n == "pool") for n in ("pe", "dve", "act", "pool", "sp")]
        B = [ctx.enter_context(nc.psum_tensor(f"B{i}", [128, 512], F32)) for i in range(8)]
        free = [[] for _ in range(8)]

        x = sb("x", [128, 8, 256])
        xh = sb("xh", [128, 8, 256])
        xT = sb("xT", [128, 2, 1024])
        ctxT = sb("ctxT", [65, 1024])
        ident = sb("ident", [128, 128])
        utri = sb("utri", [128, 128])
        iota1 = sb("iota1", [128, 128])
        identb = sb("identb", [128, 128], BF16)
        negm = sb("negm", [128, 4, 128], BF16)
        ones = sb("ones", [128, 128])
        zb = sb("zb", [1, 512], BF16)
        st = sb("st", [128, 8, 6])
        mv = sb("mv", [128, 8, 2])
        rs = sb("rs", [128, 8])
        r1_base = (nc.sbuf_base + 31) // 32 * 32
        R1 = sb("R1", [128, 9248])
        r2_base = (nc.sbuf_base + 31) // 32 * 32
        R2 = sb("R2", [128, 13120])

        def view(R, off, *shape, parts=128):
            n = int(np.prod(shape))
            v = R[0:parts, off:off + n]
            if len(shape) == 2:
                v = v.rearrange("p (a b) -> p a b", b=shape[1])
            elif len(shape) == 3:
                v = v.rearrange("p (a b c) -> p a b c", b=shape[1], c=shape[2])
            return v

        class Carve:
            def __init__(self, R, size, at=0):
                self.R, self.size, self.at = R, size, at

            def __call__(self, *shape, parts=128):
                v = view(self.R, self.at, *shape, parts=parts)
                self.at += int(np.prod(shape))
                assert self.at <= self.size, self.at
                return v

        dsems = {}

        def load(group, out_, name, q=None, w=(), src=lambda d: d):
            if group not in dsems:
                dsems[group] = DmaSem(sem("d_" + group))
            return dsems[group].load(q or SP, out_, src(D[name]), w)

        def got(group):
            return dsems[group].all()

        def barrier():
            toks = [q.now() for q in (PE, V, A, G)]
            for q in (PE, V, A, G, SP):
                q.wait(toks)
            for f in free:
                f.clear()

        c1 = Carve(R1, 9248)
        wuq, wuk, wuv, wot = c1(16, 193), c1(16, 65), c1(16, 64), c1(16, 256)
        buv = sb("buv", [128, 16])[:, :]
        bo = sb("bo", [1, 256])[:, :]
        wdkv = sb("wdkv", [128, 2, 128])
        wdq = sb("wdq", [128, 2, 192])
        cols = sb("cols", [128, 8])
        bkvb = sb("bkvb", [128, 64])
        wk1 = sb("wk1", [65, 64])
        gb = sb("gb", [128, 2, 256])
        wrb = sb("wrb", [128, 256])
        load("i", ident[:, :], "ident")
        for b in range(4):
            load(f"x{b}", x[:, 2 * b:2 * b + 2, :], "x", SP, src=lambda d, b=b: d[:, 2 * b:2 * b + 2, :])
        mh = sb("mh", [128, 1])
        t_mh = G.add(lambda e: e.memset(mh[:, :], -0.5))
        act(A, sb("early", [128, 1])[:, :], mh[:, :], ACT.Exp, [t_mh])
        load("c", wdkv[:, :, :], "wdkv", A)
        load("c", wdq[:, :, :], "wdq", A)
        load("c", cols[:, :], "cols", A)
        load("c", bkvb[:, :], "bkvb", A)
        load("s", wuq, "wuq")
        load("s", wuk, "wuk")
        load("s2", wuv, "wuv")
        load("s2", wot, "wot")
        load("s2", buv, "buv", A)
        load("s2", bo, "bo", A)
        load("k", ctxT[:, :], "ctxT")
        load("k", wk1[:, :], "wk1")
        load("k", gb[:, :, :], "gb")
        load("k", wrb[:, :], "wrb")
        load("k", utri[:, :], "utri")
        load("k", iota1[:, :], "iota1")
        load("kb", identb[:, :], "identb")
        load("kb", negm[:, :, :], "negm")
        bqkv_base = (nc.sbuf_base + 31) // 32 * 32
        bqkv = sb("bqkv", [128, 4096])
        fwo_base = (nc.sbuf_base + 31) // 32 * 32
        fwo = sb("fwo", [128, 16, 256])
        fgu_base = (nc.sbuf_base + 31) // 32 * 32
        fgu = sb("fgu", [128, 2, 2048])
        fwd_base = (nc.sbuf_base + 31) // 32 * 32
        fwd = sb("fwd", [128, 8, 256])
        rope = sb("rope", [128, 2, 128])
        load("f", rope[:, :, :], "rope")
        fg = fgu[:, :, :].rearrange("p a b -> p (a b)")
        w1q = fg[:, 0:1536].rearrange("p (a b) -> p a b", a=2)
        b1q = fg[:, 1536:2304]
        w1o = fg[:, 2304:2816].rearrange("p (a b) -> p a b", a=2)
        b1o = fg[:, 2816:3072]
        xq = sb("xq", [128, 2, 4, 128])
        xk = sb("xk", [64, 4, 128])
        xv = fg[0:64, 3584:3840]
        xo = fg[:, 3072:3584].rearrange("p (a b) -> p a b", a=2)
        gt = sb("gt", [128, 2, 28])
        selm = bqkv[0:84, 0:NCH * 64].bitcast(BF16)
        load("l", xq[:, :, :, :], "xq")
        load("l", xk[:, :, :], "xk")
        load("l", gt[:, :, :], "gt")

        t_one = G.add(lambda e: e.memset(ones[:, :], 1.0))
        t_zb = G.add(lambda e: e.memset(zb[:, :], 0.0))

        def ln(t, w, eps=1e-5):
            a = V.add(lambda e: e.bn_stats(st[:, t, :], x[:, t, :]), w)
            a = V.add(lambda e: e.bn_aggr(mv[:, t, :], st[:, t, :]), [a])
            a = tsc(V, rs[:, t:t + 1], mv[:, t, 1:2], eps, None, ALU.add, w=[a])
            a = tt(G, rs[:, t:t + 1], rs[:, t:t + 1], mh[:, 0:1], ALU.pow, [a, t_mh])
            return tsc(V, xh[:, t, :], x[:, t, :], mv[:, t, 0:1], rs[:, t:t + 1], ALU.subtract, ALU.mult, [a])

        def lnx(tiles, w):
            for t in tiles:
                a = V.add(lambda e, t=t: e.bn_stats(st[:, t, :], x[:, t, :]), w)
                a = V.add(lambda e, t=t: e.bn_aggr(mv[:, t, :], st[:, t, :]), [a])
                a = tsc(V, rs[:, t:t + 1], mv[:, t, 1:2], 1e-5, None, ALU.add, w=[a])
                rs_t[t] = tt(G, rs[:, t:t + 1], rs[:, t:t + 1], mh[:, 0:1], ALU.pow, [a, t_mh])
            yield
            for t in tiles:
                xh_t[t] = tsc(V, xh[:, t, :], x[:, t, :], mv[:, t, 0:1], rs[:, t:t + 1], ALU.subtract, ALU.mult, [rs_t[t]])
            yield

        rs_t, xh_t = {}, {}

        def xpose(t, w, bank, eng=None):
            for c in range(2):
                a = tr(PE, B[bank][:, c * 128:(c + 1) * 128], xh[:, t, c * 128:(c + 1) * 128], ident[:, :],
                       list(w) + free[bank] + [got("i")], inc=(c == 1))
            src = B[bank][:, 0:256].rearrange("p (c n) -> p c n", c=2)
            dst = xT[:, :, t * 128:(t + 1) * 128]
            if eng is V:
                a = cp(V, dst, src, [a])
            else:
                a = acopy(A, dst, src, [a])
            free[bank] = [a]
            return a

        c2 = Carve(R2, 13120)
        T0, T1 = c2(16), c2(16, parts=65)
        cq0, cq1 = c2(1024), c2(1024, parts=65)
        ckn = c2(8, 65)
        ts = c2(8, 16)
        P = [c2(2, 256) for _ in range(4)]
        PT = [c2(2, 256) for _ in range(4)]
        bo2 = c2(512, parts=1)
        mx = [c2(2, 2) for _ in range(2)]
        mts = [c2(2, 2) for _ in range(2)]
        nb = [c2(2, 2) for _ in range(2)]
        rc = [c2(4) for _ in range(2)]
        c3 = Carve(fwo[:, :, :].rearrange("p a b -> p (a b)"), 4096)
        O = [c3(2, 128) for _ in range(2)]
        kvT = c3(1024, parts=64)
        kvn = c3(8, 64)
        oX = c3(256, parts=64)
        z = [c3(256) for _ in range(2)]
        eX = [c3(256) for _ in range(2)]
        sx = c3(8, 6)
        mvx = c3(8, 2)
        rx = c3(8, 4)
        scz = sb("scz", [128, 8, 5])
        junk = sb("junk", [128, 256])
        SA = float(128) ** -0.5
        at = bqkv_base

        def parts(name, *shape):
            nonlocal at
            r = []
            for k in "hl":
                r.append(nc.alloc_sbuf_tensor_at(name + k, [128, *shape], F32R, offset=at))
                at += 4 * int(np.prod(shape))
            return r

        M0, M1 = parts("M0", 8, 128), parts("M1", 8, 128)
        at = fgu_base
        U = parts("U", 8, 256)
        at = r2_base + 4 * c2.at
        cks = parts("cks", 1024)
        cqs1 = parts("cqs1", 1024)
        qp = [parts(f"qp{i}", 256) for i in range(2)]
        OT = [parts("OT0", 256)]
        assert at <= r2_base + 4 * 13120
        at = fwo_base + 4 * c3.at
        OT.append(parts("OT1", 256))
        assert at <= fwo_base + 4 * 4096
        at = fwd_base
        cqs0 = parts("cqs0", 1024)

        def three(out_, l, r, start, stop, w, inc=False):
            mm(PE, out_, l[0], r[0], start, False, w)
            mm(PE, out_, l[0], r[1], False, False)
            return mm(PE, out_, l[1], r[0], False, stop, (), inc)

        t_m1 = G.add(lambda e: e.memset(cq1[64:65, :], 1.0))
        t_m2 = G.add(lambda e: e.memset(ckn[:, :, 64:65], 1.0))
        t_z = G.add(lambda e: e.memset(scz[:, :, :], 0.0))
        ck_t, ts_t, U_t, x1_t, x2_t, kv_t, f_t = {}, {}, {}, {}, {}, {}, {}

        def latents(hf, bk):
            yield from lnx(range(4 * hf, 4 * hf + 4), [got("x0"), got("x1")] if hf == 0 else [got("x2"), got("x3")])
            for i, t in enumerate(range(4 * hf, 4 * hf + 4)):
                xt = xpose(t, [xh_t[t]], bk[i % len(bk)])
                yield
            cs = slice(hf * 512, hf * 512 + 512)
            w = [xt, got("c")]
            toks = [t_m1, t_m2]
            for i in range(3):
                k3, rows = bk[i % len(bk)], (128, 128, 64)[i]
                for k in range(2):
                    wt = (wdkv[:, k, :], wdq[:, k, 0:128], wdq[:, k, 128:192])[i]
                    a = mm(PE, B[k3][0:rows, :], wt, xT[:, k, cs], k == 0, k == 1, w + free[k3], k == 1)
                src, col = B[k3][0:rows, :], cols[0:rows, i:i + 1]
                if i == 0:
                    a = act(A, cks[0][:, cs], src, ACT.Identity, [a], bias=col)
                    a = stt(V, cks[1][:, cs], src, col, cks[0][:, cs], ALU.add, ALU.subtract, [a])
                    free[k3] = [a]
                else:
                    cq, cqs, n = ((cq0, cqs0, 128), (cq1, cqs1, 65))[i - 1]
                    a = act(A, cq[0:rows, cs], src, ACT.Identity, [a, t_m1], bias=col)
                    free[k3] = [a]
                    toks.append(a)
                    a = cp(V, cqs[0][0:n, cs], cq[0:n, cs], [a])
                    a = tt(G, cqs[1][0:n, cs], cq[0:n, cs], cqs[0][0:n, cs], ALU.subtract, [a])
                toks.append(a)
                yield
            k3 = bk[0]
            for i in range(4):
                t = 4 * hf + i
                for k in range(2):
                    a = mm(PE, B[k3][:, i * 64:i * 64 + 64], xT[:, k, t * 128:(t + 1) * 128], wdkv[:, k, 0:64],
                           k == 0, k == 1, free[k3], k == 1 and i == 3)
            a = tt(V, ckn[:, 4 * hf:4 * hf + 4, 0:64], B[k3][:, 0:256].rearrange("p (t c) -> p t c", c=64),
                   bkvb[:, :].rearrange("p (o c) -> p o c", o=1).to_broadcast([128, 4, 64]), ALU.add, [a])
            free[k3] = [a]
            toks.append(a)
            ck_t[hf] = toks
            yield

        def offsets(hf, bk):
            for i in range(4):
                tsl = slice((4 * hf + i) * 128, (4 * hf + i + 1) * 128)
                mm(PE, B[bk][:, i * 16:i * 16 + 16], cq0[:, tsl], T0, True, False, ck_t[hf] + [t_M, A_M] + free[bk])
                a = mm(PE, B[bk][:, i * 16:i * 16 + 16], cq1[:, tsl], T1, False, True, (), i == 3)
            a = act(A, ts[:, 4 * hf:4 * hf + 4, :], B[bk][:, 0:64].rearrange("p (t h) -> p t h", h=16), ACT.Copy, [a], scale=SA)
            free[bk] = [a]
            ts_t[hf] = a
            yield

        def out_weights():
            for p in range(8):
                for hh in range(2):
                    a = mm(PE, B[6][64 * hh:64 * hh + 64, 0:256], wuv[:, 2 * p + hh, :], wot[:, 2 * p + hh, :],
                           True, True, [got("s2")] + free[6], hh == 1)
                a = acopy(A, U[0][:, p, :], B[6][:, 0:256], [a])
                a = tt(V, U[1][:, p, :], B[6][:, 0:256], U[0][:, p, :], ALU.subtract, [a])
                free[6] = [a]
                U_t[p] = a
                yield
                if p == 1:
                    for h in range(16):
                        a = mm(PE, B[6][0:1, 0:256], buv[:, h:h + 1], wot[:, h, :], h == 0, False, free[6])
                    a = mm(PE, B[6][0:1, 0:256], ones[0:1, 0:1], bo, False, True, [t_one], True)
                    a = acopy(A, bo2[:, 0:256], B[6][0:1, 0:256], [a])
                    a = acopy(A, bo2[:, 256:512], B[6][0:1, 0:256])
                    free[6] = [a]
                    U_t["bo"] = a
                    yield
            load("wqkv", wqkv, "wqkv", SP, [PE.now()])

        def ctx_kv():
            for hf in range(2):
                a = mm(PE, B[6][0:64, :], wk1[:, :], ctxT[:, hf * 512:hf * 512 + 512], True, True,
                       [got("k")] + free[6], True)
                a = acopy(A, kvT[:, hf * 512:hf * 512 + 512], B[6][0:64, :], [a])
                free[6] = [a]
                yield
            for t in range(8):
                a = mm(PE, B[6][:, t * 64:(t + 1) * 64], ctxT[:, t * 128:(t + 1) * 128], wk1[:, :], True, True, free[6], t == 7)
            a = acopy(A, kvn, B[6][:, :].rearrange("p (t c) -> p t c", c=64), [a])
            free[6] = [a]
            kv_t[0] = a
            yield

        def x0(b):
            tl = (2 * b, 2 * b + 1)
            yield from lnx(tl, [x1_t[b]])
            for i, t in enumerate(tl):
                for c in range(2):
                    a = tr(PE, B[6][:, (2 * i + c) * 128:(2 * i + c) * 128 + 128], xh[:, t, c * 128:(c + 1) * 128],
                           ident[:, :], [xh_t[t]] + free[6], c == 1)
            for i, t in enumerate(tl):
                a2 = acopy(A, xT[:, :, t * 128:(t + 1) * 128],
                           B[6][:, i * 256:i * 256 + 256].rearrange("p (c n) -> p c n", c=2), [a])
            free[6] = [a2]
            yield
            for jc in range(2):
                a = mm(PE, B[6][0:64, 0:256], kvn[:, 2 * b + jc, :], xT[:, jc, b * 256:b * 256 + 256],
                       jc == 0, jc == 1, [kv_t[0]] + free[6], jc == 1)
            a = acopy(A, oX, B[6][0:64, 0:256], [a])
            free[6] = [a]
            yield
            for ic in range(2):
                a2 = mm(PE, B[6][:, ic * 256:ic * 256 + 256], oX[:, ic * 128:ic * 128 + 128],
                        kvT[:, b * 256:b * 256 + 256], True, True, [a], ic == 1)
            yield
            g = []
            for ic, t in enumerate(tl):
                sp = B[6][:, ic * 256:ic * 256 + 256]
                a = V.add(lambda e, t=t, sp=sp: e.bn_stats(sx[:, t, :], sp), [a2])
                a = V.add(lambda e, t=t: e.bn_aggr(mvx[:, t, :], sx[:, t, :]), [a])
                a = tsc(V, rx[:, t, 0:1], mvx[:, t, 1:2], 1.0 / 256.0, 1e-6, ALU.mult, ALU.add, [a])
                g.append(tt(G, rx[:, t, 1:2], rx[:, t, 0:1], mh[:, 0:1], ALU.pow, [a]))
            yield
            for ic, t in enumerate(tl):
                sp = B[6][:, ic * 256:ic * 256 + 256]
                a = tsc(V, rx[:, t, 1:2], rx[:, t, 1:2], 1.0 / 16.0, None, ALU.mult, w=[g[ic]])
                g[ic] = tsc(V, z[ic], sp, mvx[:, t, 0:1], rx[:, t, 1:2], ALU.subtract, ALU.mult, [a])
            free[6] = [g[1]]
            yield
            for ic, t in enumerate(tl):
                a = tt(V, z[ic], z[ic], gb[:, 0, :], ALU.mult, [g[ic], got("k")])
                g[ic] = tt(V, z[ic], z[ic], gb[:, 1, :], ALU.add, [a])
            yield
            for ic, t in enumerate(tl):
                a = V.add(lambda e, t=t, ic=ic: e.tensor_reduce(rx[:, t, 2:3], z[ic], X, ALU.max, negate=True), [g[ic]])
                g[ic] = act(A, eX[ic], z[ic], ACT.Exp, [a], bias=rx[:, t, 2:3], accum=rx[:, t, 3:4])
            yield
            for ic, t in enumerate(tl):
                a = rec(V, rx[:, t, 3:4], rx[:, t, 3:4], [g[ic]])
                x2_t[t] = stt(V, x[:, t, :], eX[ic], rx[:, t, 3:4], x[:, t, :], ALU.mult, ALU.add, [a])
            yield
            yield from lnx(tl, [x2_t[tl[1]]])
            last = [f_t[2 * b - 1]] if b else []
            for t in tl:
                f_t[t] = V.add(lambda e, t=t: e.tensor_tensor_reduce(junk[:, :], xh[:, t, :], wrb[:, :], 1.0, 0.0, ALU.mult,
                                                                     ALU.add, scz[:, t, t // 2:t // 2 + 1]),
                               [xh_t[t], t_z, got("k")] + last)
                last = [f_t[t]]
                tt(V, x[:, t, :], x[:, t, :], xh[:, t, :], ALU.add)
            yield

        wqkv = view(R1, 0, 2, 4096)
        for _ in latents(0, [0, 1, 2, 3, 4, 5]):
            pass
        for g in range(4):
            for c in range(2):
                bk = (6, 7, 4, 5)[2 * (g % 2) + c]
                n = (128, 65)[c]
                for h in range(4 * g, 4 * g + 4):
                    a = mm(PE, B[bk][0:n, (h % 4) * 65:(h % 4) * 65 + 65], wuq[:, h, c * 128:c * 128 + n], wuk[:, h, :],
                           True, True, [got("s")] + free[bk], h % 4 == 3)
                src = B[bk][0:n, 0:260].rearrange("p (h c) -> p h c", h=4)
                Mc, Tc = ((M0, T0), (M1, T1))[c]
                dst = [m[0:n, 2 * g:2 * g + 2, :].rearrange("p a (h c) -> p (a h) c", h=2) for m in Mc]
                acopy(A, Tc[0:n, 4 * g:4 * g + 4], src[:, :, 64], [a])
                a = acopy(A, dst[0], src[:, :, 0:64])
                a = tt(V, dst[1], src[:, :, 0:64], dst[0], ALU.subtract, [a])
                free[bk] = [a]
        t_M = V.now()
        A_M = A.now()
        for _ in offsets(0, 3):
            pass

        NP = 32
        S_max, nb_t, exp_t, P_t, T_t, PT_t, PV_t, O_t = {}, {}, {}, {}, {}, {}, {}, {}
        qp_t, S_pe, QP_rd, OT_t, OTr_t, x1_t = {}, {}, {}, {}, {}, {}

        def QP(j):
            b, p = divmod(j, 8)
            bs = slice(b * 256, b * 256 + 256)
            w = free[4] + [t_M, A_M] + ck_t[j // 16]
            q = B[4][:, 0:256]
            three(q, [m[:, p, :] for m in M0], [m[:, bs] for m in cqs0], True, False, w)
            a = three(q, [m[0:65, p, :] for m in M1], [m[0:65, bs] for m in cqs1], False, True, (), True)
            h, l = qp[j % 2]
            a = cp(V, h[:, :], q, [a] + ([S_pe[j - 2]] if j >= 2 else []))
            qp_t[j] = tt(V, l[:, :], q, h[:, :], ALU.subtract, [a])
            free[4] = [qp_t[j]]

        def S(j):
            b, p = divmod(j, 8)
            for qc in range(2):
                for hh in range(2):
                    r = slice(64 * hh, 64 * hh + 64)
                    a = three(B[hh][:, qc * 256:qc * 256 + 256], [m[r, qc * 128:qc * 128 + 128] for m in qp[j % 2]],
                              [m[r, b * 256:b * 256 + 256] for m in cks], True, True, [qp_t[j]] + free[hh], qc == 1)
                    S_max[j, hh] = a
            S_pe[j] = a
            s = j % 2
            for hh in range(2):
                w = [S_max[j, hh]] + ([nb_t[j - 2]] if j >= 2 else [])
                a = red(V, mx[s][:, :, hh], B[hh][:, :].rearrange("p (q k) -> p q k", q=2), ALU.max, w)
            tv = ts[:, 2 * b:2 * b + 2, 2 * p:2 * p + 2]
            a = stt(V, mts[s], mx[s], SA, tv, ALU.mult, ALU.add, [a, ts_t[j // 16]])
            w = [a] + ([exp_t[j - 2]] if j >= 2 else [])
            nb_t[j] = tt(V, nb[s], tv, mts[s], ALU.subtract, w)
            for hh in range(2):
                for qc in range(2):
                    w = [nb_t[j]] + ([T_t[j - 2]] if j >= 2 else [])
                    a = act(A, P[2 * s + hh][:, qc, :], B[hh][:, qc * 256:qc * 256 + 256], ACT.Exp, w,
                            bias=nb[s][:, qc, hh:hh + 1], scale=SA)
                P_t[j, hh] = a
                free[hh] = [a]
            exp_t[j] = a

        def T(j):
            s = j % 2
            for hh in range(2):
                bk = 2 + hh
                for kc in range(2):
                    for qc in range(2):
                        a = tr(PE, B[bk][:, kc * 256 + qc * 128:kc * 256 + qc * 128 + 128],
                               P[2 * s + hh][:, qc, kc * 128:kc * 128 + 128], ident[:, :],
                               [P_t[j, hh]] + free[bk], kc == 1 and qc == 1)
                T_t[j] = a
                w = [a] + ([PV_t[j - 2]] if j >= 2 else [])
                src = B[bk][:, :].rearrange("p (k q) -> p k q", k=2)
                if hh == 0:
                    a = cp(V, PT[2 * s + hh], src, w)
                else:
                    a = acopy(A, PT[2 * s + hh], src, w)
                PT_t[j, hh] = a
                free[bk] = [a]

        def PV(j):
            b = j // 8
            s = j % 2
            for hh in range(2):
                for qc in range(2):
                    o = (qc * 2 + hh) * 65
                    for kc in range(2):
                        a = mm(PE, B[5][:, o:o + 65], PT[2 * s + hh][:, kc, qc * 128:qc * 128 + 128],
                               ckn[:, 2 * b + kc, :], kc == 0, kc == 1, [PT_t[j, hh]] + free[5],
                               hh == 1 and qc == 1 and kc == 1)
            PV_t[j] = a
            src = B[5][:, 0:260].rearrange("p (g c) -> p g c", g=4)
            a = rec(V, rc[s], src[:, :, 64], [a])
            w = [a] + ([OTr_t[j - 2]] if j >= 2 else [])
            dst = O[s].rearrange("p q (h c) -> p (q h) c", h=2)
            a = tt(V, dst, src[:, :, 0:64], rc[s].rearrange("p (g o) -> p g o", o=1).to_broadcast([128, 4, 64]), ALU.mult, w)
            O_t[j] = a
            free[5] = [a]

        def OTr(j):
            s = j % 2
            for qc in range(2):
                a = tr(PE, B[4][:, qc * 128:qc * 128 + 128], O[s][:, qc, :], ident[:, :],
                       [O_t[j]] + free[4], qc == 1)
            OTr_t[j] = a
            a = cp(V, OT[s][0][:, :], B[4][:, 0:256], [a] + ([OP_t[j - 2]] if j >= 2 else []))
            a = tt(V, OT[s][1][:, :], B[4][:, 0:256], OT[s][0][:, :], ALU.subtract, [a])
            free[4] = [a]
            OT_t[j] = a

        OP_t = {}

        def OP(j):
            b, p = divmod(j, 8)
            s = j % 2
            if p == 0:
                mm(PE, B[7][:, :], ones[0:1, :], bo2, True, False, [U_t["bo"]] + free[7])
            for qc in range(2):
                a = three(B[7][:, qc * 256:qc * 256 + 256], [m[:, qc * 128:qc * 128 + 128] for m in OT[s]],
                          [m[:, p, :] for m in U], False, p == 7, [OT_t[j], U_t[p]], qc == 1)
            OP_t[j] = a
            if p == 7:
                xv_ = x[:, 2 * b:2 * b + 2, :]
                a = tt(V, xv_, B[7][:, :].rearrange("p (q n) -> p q n", q=2), xv_, ALU.add, [a])
                free[7] = [a]
                x1_t[b] = a

        more = [out_weights(), ctx_kv(), latents(1, [6]), offsets(1, 6)]

        def tick(n=1):
            for _ in range(n):
                while more and next(more[0], "end") == "end":
                    more.pop(0)

        QP(0)
        QP(1)
        for j in range(NP + 4):
            if j < NP:
                S(j)
            if 1 <= j <= NP:
                T(j - 1)
            if j + 2 < NP:
                QP(j + 2)
            tick()
            if j == NP:
                load("fb", bqkv[:, :], "bqkv", SP, [PE.now()])
            if 2 <= j <= NP + 1:
                PV(j - 2)
            if 4 <= j:
                OP(j - 4)
                if (j - 4) % 8 == 7:
                    more.append(x0((j - 4) // 8))
            if 3 <= j <= NP + 2:
                OTr(j - 3)
            tick()
        load("fg", fgu[:, :, :], "fgu", SP, [OP_t[NP - 1]])
        load("fg", fwd[:, :, :], "fwd")
        while more:
            tick()
        barrier()
        c2 = Carve(R2, 13120)
        qkv = c2(4096)
        rp = c2(24, 128)
        qkT = c2(24, 128)
        Pf = c2(16, 128)
        PTf = rp[:, 0:16, :]
        oT = view(R2, 0, 16, 128)
        hT = Pf[:, 0:8, :]
        r2c = Carve(R1, 9248, 8192)
        wk4 = sb("wk4", [4, 256])
        m8 = sb("m8", [4, 8])
        mT = sb("mT", [128, 2, 4])
        cT = sb("cT", [128, 2, 4])
        Sel = qkT[:, 0:8, :]
        SelT = sb("SelT", [128, 8, 128])
        xs = r2c(256)
        xs1 = r2c(256)
        xn = r2c(256)
        cs = sb("cs", [128, 132])
        nT = sb("nT", [128, 2, 128])
        sm = sb("sm", [128, 8])
        mxf = sb("mxf", [128, 3, 16])
        load("fo", fwo[:, :, :], "fwo")
        scf = scz[:, :, :].rearrange("p a b -> p (a b)")
        for c in range(2):
            a = mm(PE, B[0][0:4, c * 128:c * 128 + 128], scf[:, 5 * c:5 * c + 34:11], ident[:, :],
                   True, True, [f_t[t] for t in range(8)], c == 1)
        a = cp(V, wk4[:, :], B[0][0:4, 0:256], [a])
        for r in range(4):
            a = V.add(lambda e: e.max(m8[:, :], wk4[:, :]), [a])
            a = V.add(lambda e: e.match_replace(wk4[:, :], m8[:, :], wk4[:, :], -3.0e38), [a])
        a = tsc(V, wk4[:, :], wk4[:, :], -3.0e38, None, ALU.is_equal, w=[a])
        for c in range(2):
            a2 = tr(PE, B[1][:, c * 4:c * 4 + 4], wk4[:, c * 128:c * 128 + 128], ident[0:4, 0:4], [a], c == 1)
        a = cp(V, mT[:, :, :], B[1][:, 0:8].rearrange("p (c b) -> p c b", c=2), [a2])
        mm(PE, B[2][:, 0:4], utri[:, :], mT[:, 0, :], True, True, [a])
        mm(PE, B[2][:, 4:8], utri[:, :], mT[:, 1, :], True, False)
        a2 = mm(PE, B[2][:, 4:8], ones[:, :], mT[:, 0, :], False, True, (), True)
        for b in range(4):
            a = stt(V, cT[:, :, b], B[2][:, b:8:4], float(32 * b), mT[:, :, b], ALU.add, ALU.mult, [a2])
        sel_t = {}
        for t in range(8):
            sel_t[t] = tsc(V, Sel[:, t, :], iota1[:, :], cT[:, t % 2, t // 2:t // 2 + 1], None, ALU.is_equal, w=[a])
        for t in range(8):
            ax = mm(PE, B[3][:, 0:256], Sel[:, t, :], xh[:, t, :], t == 0, t == 7, [sel_t[t]], t == 7)
        for t in range(8):
            ar = mm(PE, B[4][:, 0:128], Sel[:, t, :], rope[:, t % 2, :], t == 0, t == 7, [got("f")], t == 7)
        a = PE.add(lambda e: e.matmul(B[5][:, 0:4], Sel[:, 0, :], scz[:, 0, 0:4], start=True, stop=False,
                                      skip_group_check=True), (), False)
        for t in range(1, 8):
            a = mm(PE, B[5][:, 0:4], Sel[:, t, :], scz[:, t, 0:4], False, t == 7, (), t == 7)
        t_x = cp(V, xs, B[3][:, 0:256], [ax])
        t_cs = acopy(A, cs[:, 0:128], B[4][:, 0:128], [ar])
        free[3], free[4] = [t_x], [t_cs]
        st_pe = []
        for hf in range(2):
            for t in range(4 * hf, 4 * hf + 4):
                c = tr(PE, B[6 + hf][:, (t % 4) * 128:(t % 4) * 128 + 128], Sel[:, t, :], ident[:, :], (), t % 4 == 3)
            st_pe.append(c)

        def rms(src, col, ln_col, w, bank):
            a = act(A, junk[:, :], src, ACT.Square, w, accum=sm[:, col:col + 1])
            a = tsc(V, sm[:, col:col + 1], sm[:, col:col + 1], 1.0 / 256.0, 1e-6, ALU.mult, ALU.add, [a])
            a = tt(G, sm[:, col:col + 1], sm[:, col:col + 1], mh[:, 0:1], ALU.pow, [a])
            a = tsc(V, xn, src, sm[:, col:col + 1], None, ALU.mult, w=[a] + list(w))
            for c in range(2):
                a2 = tr(PE, B[bank][:, c * 128:c * 128 + 128], xn[:, c * 128:c * 128 + 128], ident[:, :],
                        [a] + free[bank], c == 1)
            for c in range(2):
                a = tsc(V, nT[:, c, :], B[bank][:, c * 128:c * 128 + 128], cols[:, ln_col + c:ln_col + c + 1],
                        None, ALU.mult, w=[a2])
            free[bank] = [a]
            return a

        t_h = rms(xs, 3, 3, [t_x], 1)
        t_sc = red(V, sm[:, 0:1], B[5][:, 0:4], ALU.add, [a])
        free[5] = [t_sc]
        t_th = act(A, sm[:, 1:2], sm[:, 0:1], ACT.Tanh, [t_sc], scale=0.5)
        t_gate = tsc(V, sm[:, 2:3], sm[:, 1:2], 0.5, 0.5, ALU.mult, ALU.add, [t_th])
        for hf in range(2):
            t_selT = acopy(A, SelT[:, 4 * hf:4 * hf + 4, :],
                           B[6 + hf][:, :].rearrange("p (t n) -> p t n", t=4), [st_pe[hf]])
            free[6 + hf] = [t_selT]
        tb = got("f")
        b_of = [0, 2, 3, 4, 5, 6, 7, 1]
        qkv_t = {}
        cosb = cs[:, 0:64].rearrange("p (o d) -> p o d", o=1)
        sinb = cs[:, 64:128].rearrange("p (o d) -> p o d", o=1)
        tmp = Pf.rearrange("p a b -> p (a b)")
        rp_t = {}

        def rotate(i, eng, h0, nh, before):
            src = qkv[:, h0 * 128:(h0 + nh) * 128].rearrange("p (h d) -> p h d", d=128)
            q1, q2 = src[:, :, 0:64], src[:, :, 64:128]
            cb, snb = cosb.to_broadcast([128, nh, 64]), sinb.to_broadcast([128, nh, 64])
            tmpa = tmp[:, (i % 4) * 512:(i % 4) * 512 + 256].rearrange("p (h d) -> p h d", d=64)
            tmpb = tmp[:, (i % 4) * 512 + 256:(i % 4) * 512 + 512].rearrange("p (h d) -> p h d", d=64)
            w = [qkv_t[h0 // 4], t_cs] + [rp_t[h] for h in before]
            r1, r2 = rp[:, h0:h0 + nh, 0:64], rp[:, h0:h0 + nh, 64:128]
            tt(eng, r1, q1, cb, ALU.mult, w)
            a2 = tt(eng, tmpa, q2, snb, ALU.mult)
            tt(eng, r2, q2, cb, ALU.mult)
            a4 = tt(eng, tmpb, q1, snb, ALU.mult)
            tt(eng, r1, r1, tmpa, ALU.subtract, [a2])
            rp_t[h0] = tt(eng, r2, r2, tmpb, ALU.add, [a4])

        turns = {4: (V, []), 5: (G, []), 0: (V, []), 1: (G, []), 2: (V, [16]), 3: (V, [20])}
        for i, n in enumerate([4, 5, 0, 1, 2, 3, 6, 7]):
            bk = b_of[i]
            for k in range(2):
                a = mm(PE, B[bk][:, :], nT[:, k, :], wqkv[:, k, n * 512:n * 512 + 512], k == 0, k == 1,
                       [t_h, got("wqkv")] + free[bk], k == 1)
            a = tt(V, qkv[:, n * 512:n * 512 + 512], B[bk][:, :], bqkv[:, n * 512:n * 512 + 512], ALU.add, [a, got("fb")])
            free[bk] = [a]
            qkv_t[n] = a
            if n in turns:
                rotate(i, turns[n][0], 4 * n, 4, turns[n][1])
        qk_t = {}
        for i, h0 in enumerate([16, 20, 0, 4, 8, 12]):
            bk = b_of[i]
            for h in range(4):
                a = tr(PE, B[bk][:, h * 128:h * 128 + 128], rp[:, h0 + h, :], ident[:, :],
                       [rp_t[h0]] + free[bk], h == 3)
            a = acopy(A, qkT[:, h0:h0 + 4, :], B[bk][:, :].rearrange("p (h n) -> p h n", h=4), [a, t_selT])
            free[bk] = [a]
            qk_t[h0] = a
        SF = float(128) ** -0.5
        pf_t, ptf_t, pe_t = {}, {}, {}
        for g in range(4):
            bk = b_of[g + 1]
            mm(PE, B[bk][:, :], identb[:, :], negm[:, :, :], True, False, [got("kb")] + free[bk])
            for hh in range(4):
                h = 4 * g + hh
                a = mm(PE, B[bk][:, hh * 128:hh * 128 + 128], qkT[:, h, :], qkT[:, 16 + h // 2, :], False, True,
                       [qk_t[4 * g], qk_t[16], qk_t[20]], hh == 3)
            sv = B[bk][:, :].rearrange("p (h n) -> p h n", h=4)
            a = red(V, mxf[:, 0, 4 * g:4 * g + 4], sv, ALU.max, [a])
            a = tsc(V, mxf[:, 1, 4 * g:4 * g + 4], mxf[:, 0, 4 * g:4 * g + 4], -SF, None, ALU.mult, w=[a])
            for hh in range(4):
                h = 4 * g + hh
                a = act(A, Pf[:, h, :], sv[:, hh, :], ACT.Exp, [a] + list(rp_t.values()), bias=mxf[:, 1, h:h + 1],
                        scale=SF, accum=mxf[:, 2, h:h + 1])
            free[bk] = [a]
            pe_t[g] = a
        for g in range(4):
            a = rec(V, mxf[:, 2, 4 * g:4 * g + 4], mxf[:, 2, 4 * g:4 * g + 4], [pe_t[g]])
            rb = mxf[:, 2, 4 * g:4 * g + 4].rearrange("p (g o) -> p g o", o=1).to_broadcast([128, 4, 128])
            pf_t[g] = tt(V, Pf[:, 4 * g:4 * g + 4, :], Pf[:, 4 * g:4 * g + 4, :], rb, ALU.mult, [a])
        of_t = {}
        for g in range(4):
            bk = (7, 6, 0, 1)[g]
            for hh in range(4):
                a = tr(PE, B[bk][:, hh * 128:hh * 128 + 128], Pf[:, 4 * g + hh, :], ident[:, :],
                       [pf_t[g]] + free[bk], hh == 3)
            ptf_t[g] = acopy(A, PTf[:, 4 * g:4 * g + 4, :], B[bk][:, :].rearrange("p (h n) -> p h n", h=4), [a])
            free[bk] = [ptf_t[g]]
        for g in range(4):
            bk = b_of[g + 1]
            for kv in range(2):
                vh = 2 * g + kv
                a = mm(PE, B[bk][:, kv * 256:kv * 256 + 256], qkv[:, 3072 + vh * 128:3072 + vh * 128 + 128],
                       PTf[:, 2 * vh:2 * vh + 2, :], True, True, [ptf_t[g], qkv_t[6], qkv_t[7]] + free[bk], kv == 1)
            eng = (V, A)[g % 2]
            f = cp if g % 2 == 0 else acopy
            of_t[g] = f(eng, oT[:, 4 * g:4 * g + 4, :], B[bk][:, :].rearrange("p (h n) -> p h n", h=4),
                        [a] + [rp_t[4 * g]])
            free[bk] = [of_t[g]]
        for h in range(16):
            a = mm(PE, B[7][:, 0:256], oT[:, h, :], fwo[:, h, :], h == 0, h == 15, [of_t[h // 4], got("fo")] + free[7], h == 15)
        t_x1 = tt(V, xs1, B[7][:, 0:256], xs, ALU.add, [a])
        t_h = rms(xs1, 4, 5, [t_x1], 1)
        gu_t = {}
        t_hT = []
        for hf in range(2):
            for u in range(2):
                bk = 2 + 2 * hf + u
                for m in range(4):
                    mo = u * 1024 + (4 * hf + m) * 128
                    for k in range(2):
                        a = mm(PE, B[bk][:, m * 128:m * 128 + 128], fgu[:, k, mo:mo + 128], nT[:, k, :],
                               k == 0, k == 1, [t_h, got("fg")] + free[bk], k == 1 and m == 3)
                gu_t[hf, u] = a
            gp = B[2 + 2 * hf][:, :]
            up = B[3 + 2 * hf][:, :]
            th = view(R2, 4096 + hf * 512, 512)
            a = act(A, th, gp, ACT.Tanh, [gu_t[hf, 0], gu_t[0, 1]], scale=0.5)
            a = stt(V, th, th, 1.0, gp, ALU.add, ALU.mult, [a])
            hv = hT[:, 4 * hf:4 * hf + 4, :].rearrange("p a b -> p (a b)")
            a = stt(V, hv, th, 0.5, up, ALU.mult, ALU.mult, [a, gu_t[hf, 1]])
            t_hT.append(a)
        for nm, dst in (("w1q", w1q), ("b1q", b1q), ("w1o", w1o), ("b1o", b1o), ("xv", xv), ("xo", xo)):
            load("m", dst, nm, SP, list(gu_t.values()))
        for m in range(8):
            a = mm(PE, B[6][:, 0:256], hT[:, m, :], fwd[:, m, :], m == 0, m == 7, [t_hT[m // 4]] + free[6], m == 7)
        a2 = tt(V, xs1, xs1, xs, ALU.subtract, [t_h, t_x1])
        a = tt(V, xs1, B[6][:, 0:256], xs1, ALU.add, [a, a2])
        a = tsc(V, xs1, xs1, sm[:, 2:3], None, ALU.mult, w=[a, t_gate])
        barrier()
        for b in range(4):
            bk = (0, 2, 3, 4)[b]
            for c in range(2):
                a2 = mm(PE, B[bk][:, c * 256:c * 256 + 256], SelT[:, 2 * b + c, :], xs1, True, True, (), c == 1)
            xv_ = x[:, 2 * b:2 * b + 2, :]
            a3 = tt(V, xv_, B[bk][:, :].rearrange("p (q n) -> p q n", q=2), xv_, ALU.add, [a2])
            free[bk] = [a3]
            if b == 0:
                first = lnx((0, 1), [a3])
                next(first)
        next(first)

        load("lb", selm, "selm")
        r1_at = r1_base

        def over_r1(name, *shape):
            nonlocal r1_at
            t = nc.alloc_sbuf_tensor_at(name, [128, *shape], F32R, offset=r1_at)
            r1_at += 4 * int(np.prod(shape))
            assert r1_at <= r1_base + 4 * 9248
            return t

        xTh = [over_r1("xTh", 2, 512)]
        xTl = [over_r1("xTl", 2, 512)]
        xTh.append(nc.alloc_sbuf_tensor_at("xTh1", [128, 2, 512], F32R, offset=fwo_base))
        xTl.append(nc.alloc_sbuf_tensor_at("xTl1", [128, 2, 512], F32R, offset=fwo_base + 4096))
        hh_ = [over_r1(f"hh{i}", 512) for i in range(3)]
        hl_ = [over_r1(f"hl{i}", 512) for i in range(3)]
        uh_ = [over_r1(f"uh{i}", 512) for i in range(2)]
        ul_ = [over_r1(f"ul{i}", 512) for i in range(2)]
        dh_ = [over_r1(f"dh{i}", 256) for i in range(4)]
        dl_ = [over_r1(f"dl{i}", 256) for i in range(4)]
        c2 = Carve(R2, 13120)
        fwo_ = fwo[:, :, :].rearrange("p a b -> p (a b)")
        fwd_ = fwd[:, :, :].rearrange("p a b -> p (a b)")
        pr = fwo_
        pr2 = view(R1, 2048, 4096)
        bq = Carve(bqkv, 4096, 2496)
        q1 = [bq(768) for _ in range(2)]
        sT = Carve(SelT[:, :, :].rearrange("p a b -> p (a b)"), 1024)
        Sx = [sT(256) for _ in range(2)]
        oa = [sT(256) for _ in range(2)]
        ms = [c2(16) for _ in range(2)]
        oaT = [c2(2, 128) for _ in range(2)]
        zin = [c2(2, 256) for _ in range(2)]
        wsem = [DmaSem(sem(f"d_scrw{t}")) for t in range(8)]
        zsem = [DmaSem(sem(f"d_scrr{b}")) for b in range(4)]
        w_t, z_t, zt_t, op_t, oT_t, l1_t, prr, prr2, qk_t, m2_t = {}, {}, {}, {}, {}, {}, {}, {}, {}, {}
        V.wait([got("m")])

        def l1a_mm(t):
            xs_ = [xT[:, k, t * 128:t * 128 + 128] for k in range(2)]
            for k in range(2):
                a = mm(PE, B[1][:, :], xs_[k], w1q[:, k, 0:512], k == 0, k == 1, [xt_t[t], got("m")] + free[1], k == 1)
            for k in range(2):
                b = mm(PE, B[7][:, 0:256], xs_[k], w1q[:, k, 512:768], k == 0, k == 1, free[7], k == 1)
            qk_t[t] = (a, b)

        def l1a_add(t):
            a, b = qk_t[t]
            s = t % 2
            w = m2_t.get(t - 2, [])
            c = tt(V, q1[s][:, 0:512], B[1][:, :], b1q[:, 0:512], ALU.add, [a] + w)
            free[1] = [c]
            c = tt(V, q1[s][:, 512:768], B[7][:, 0:256], b1q[:, 512:768], ALU.add, [b])
            free[7] = [c]
            qk_t[t] = c

        SH = [128, 4, 16, 16]

        def m1(eng, t, i):
            q3 = q1[t % 2][:, 0:256].rearrange("p (h o d) -> p h o d", o=1, d=16)
            k3 = q1[t % 2][:, 256:512].rearrange("p (o g d) -> p o g d", o=1, d=16).to_broadcast(SH)
            pv4 = pr[:, i * 1024:(i + 1) * 1024].rearrange("p (h g d) -> p h g d", g=16, d=16)
            m1_t[i] = tt(eng, pv4, q3[:, 4 * i:4 * i + 4].to_broadcast(SH), k3, ALU.mult, [qk_t[t]] + prr.get(i, []))

        m1_t = {}

        def r1(t, i):
            pv4 = pr[:, i * 1024:(i + 1) * 1024].rearrange("p (h g d) -> p h g d", g=16, d=16)
            Sv = Sx[t % 2][:, i * 64:i * 64 + 64].rearrange("p (h g) -> p h g", g=16)
            a = red(V, Sv, pv4, ALU.add, [m1_t[i]] + m2_t.get(t - 2, []))
            prr[i] = [a]
            return a

        def smax1(t, a):
            s = t % 2
            Sv = Sx[s].rearrange("p (h g) -> p h g", g=16)
            a = red(V, ms[s], Sv, ALU.max, [a])
            a = tt(V, Sv, Sv, ms[s].rearrange("p (h o) -> p h o", o=1).to_broadcast([128, 16, 16]), ALU.subtract, [a])
            return act(A, Sx[s], Sx[s], ACT.Exp, [a], scale=1.0 / 16.0)

        def smax2(t, a):
            s = t % 2
            Sv = Sx[s].rearrange("p (h g) -> p h g", g=16)
            a = red(V, ms[s], Sv, ALU.add, [a])
            a = rec(V, ms[s], ms[s], [a])
            return tt(V, Sv, Sv, ms[s].rearrange("p (h o) -> p h o", o=1).to_broadcast([128, 16, 16]), ALU.mult, [a])

        def to_scr(t, a):
            b, c = divmod(t, 2)
            dst = D["scr"][b, :, c * 128:c * 128 + 128, :].rearrange("h n d -> n h d")
            w_t[t] = wsem[t].load(SP, dst, oa[t % 2].rearrange("p (h d) -> p h d", d=16), [a])
            oT_t[t] = w_t[t]
            if c == 1:
                src = D["scr"][b].rearrange("(q h) (m l) d -> (h m) q (l d)", q=2, l=16)
                z_t[b] = zsem[b].load(SP, zin[b % 2], src, [w_t[t - 1], w_t[t]] + ([zt_t[b - 2]] if b >= 2 else []))

        def l1a_out(b):
            tl = (2 * b, 2 * b + 1)
            for q in range(2):
                for c in range(2):
                    m = tr(PE, B[1][:, (2 * q + c) * 128:(2 * q + c) * 128 + 128], zin[b % 2][:, q, c * 128:c * 128 + 128],
                           ident[:, :], [z_t[b]] + free[1], q == 1 and c == 1)
            zt_t[b] = m
            for q in range(2):
                m2 = acopy(A, oaT[q], B[1][:, q * 256:q * 256 + 256].rearrange("p (c n) -> p c n", c=2),
                           [m] + ([op_t[0]] if b else []))
            free[1] = [m2]
            yield
            for q in range(2):
                for k in range(2):
                    m = mm(PE, B[1][:, q * 256:q * 256 + 256], oaT[q][:, k, :], w1o[:, k, :], k == 0, k == 1, [m2] + free[1],
                           k == 1 and q == 1)
            op_t[0] = m
            xv_ = x[:, tl[0]:tl[0] + 2, :]
            m = tt(V, xv_, B[1][:, :].rearrange("p (q n) -> p q n", q=2), xv_, ALU.add, [m])
            free[1] = [m]
            m = tt(V, xv_, xv_, b1o.rearrange("p (o n) -> p o n", o=1).to_broadcast([128, 2, 256]), ALU.add, [m])
            for t in tl:
                x3_t[t] = m
            yield

        x3_t = {}

        def l1a_three(tiles):

            def m2(eng, t, i):
                Pg = Sx[t % 2].rearrange("p (h g o) -> p g h o", g=16, o=1)[:, 4 * i:4 * i + 4].to_broadcast(SH)
                vg = q1[t % 2][:, 512 + 64 * i:576 + 64 * i].rearrange("p (g o d) -> p g o d", o=1, d=16).to_broadcast(SH)
                pv4 = pr2[:, i * 1024:(i + 1) * 1024].rearrange("p (g h d) -> p g h d", h=16, d=16)
                return tt(eng, pv4, Pg, vg, ALU.mult, [p_t[t]] + prr2.get(i, []))

            def sums(t, ii):
                for i in ii:
                    for g in range(4):
                        a = mm(PE, B[0][:, 0:256], ident[:, :], pr2[:, i * 1024 + g * 256:i * 1024 + g * 256 + 256],
                               i == 1 and g == 0, i == 2 and g == 3, [mt[t][i]] + free[0], g == 3)
                    prr2[i] = [a]
                if ii[-1] == 2:
                    a = acopy(A, oa[t % 2], B[0][:, 0:256], [a] + ([oT_t[t - 2]] if t - 2 in oT_t else []))
                    free[0] = [a]
                    l1_t[t] = a
                    to_scr(t, a)

            p_t, mt = {}, {}
            l1a_mm(tiles[0])
            l1a_add(tiles[0])
            yield
            for i, e in ((0, G), (1, V), (2, G), (3, V)):
                m1(e, tiles[0], i)
            yield
            for t in tiles:
                nx = t + 1 in tiles
                r1(t, 1)
                if nx:
                    l1a_mm(t + 1)
                yield
                r1(t, 3)
                if t - 1 in mt:
                    sums(t - 1, (1, 3))
                yield
                if nx:
                    l1a_add(t + 1)
                r1(t, 0)
                yield
                a = r1(t, 2)
                yield
                a = smax1(t, a)
                yield
                if t - 1 in mt:
                    sums(t - 1, (0, 2))
                if nx:
                    m1(G, t + 1, 0)
                    m1(V, t + 1, 1)
                    yield
                    m1(G, t + 1, 2)
                    m1(V, t + 1, 3)
                    yield
                p_t[t] = smax2(t, a)
                yield
                mt[t] = {}
                for i, j in ((1, 0), (3, 2)):
                    mt[t][i] = m2(V, t, i)
                    mt[t][j] = m2(G, t, j)
                    yield
                m2_t[t] = list(mt[t].values())
                if t % 2 == 0 and t != tiles[0]:
                    yield from l1a_out(t // 2 - 1)
            t = tiles[-1]
            sums(t, (1, 3))
            yield
            sums(t, (0, 2))
            for _ in range(5):
                yield
            yield from l1a_out(t // 2)

        qT_ = [c2(4, 256) for _ in range(2)]
        kT_ = [c2(4, 256) for _ in range(2)]
        va = [c2(2, 16, 17) for _ in range(2)]
        Px = [c2(3, 128) for _ in range(4)]
        PTx = [c2(3, 128) for _ in range(4)]
        OxT = [c2(4, 256), view(fwd_, 1024, 4, 256)]
        Ox = view(fwd_, 0, 2, 256)
        OTx = view(fwd_, 512, 2, 256)
        mxx = [c2(4) for _ in range(4)]
        rcx = c2(2, 16)
        t_v1 = [G.add(lambda e, s=s: e.memset(va[s][:, :, :, 16:17], 1.0)) for s in range(2)][-1]
        t_ox = [G.add(lambda e, i=i: e.memset(OxT[i], 0.0)) for i in range(2)][-1]
        negx3 = sb("negx3", [128, 3, 128], BF16)
        G.add(lambda e: e.memset(negx3[:, 1, :], 0.0))
        G.add(lambda e: e.tensor_copy(negx3[:, 0, :], negm[:, 0, :]), [got("kb")])
        t_ng = G.add(lambda e: e.tensor_copy(negx3[:, 2, :], negm[:, 0, :]))
        negx = negx3[:, :, :]
        pre = {}
        last_S, last_PV, ox_t, on_t, ot_t = {}, {}, {}, {}, {}
        xP, xT_t, xPT, xPV = {}, {}, {}, {}
        SX = 0.25
        x4_t = {}

        def xbank(b):
            return (2, 3, 4, 5, 6) if b < 3 else (0, 0, 1, 7, 1)

        def l1x_kv(b):
            s = b % 2
            bk = 6
            bs = slice(b * 256, b * 256 + 256)
            w = [last_S[b - 2]] if b >= 2 else []
            toks = []
            for g in range(2):
                for cc in range(2):
                    m = mm(PE, B[bk][:, cc * 256:cc * 256 + 256], xk[:, 2 * g + cc, :], ctxT[0:64, bs], True, True,
                           [got("l")] + free[bk], cc == 1)
                m = acopy(A, kT_[s][:, 2 * g:2 * g + 2, :], B[bk][:, :].rearrange("p (c n) -> p c n", c=2), [m] + w)
                free[bk] = [m]
                toks.append(m)
                yield
            w = [last_PV[b - 2]] if b >= 2 else []
            for c in range(2):
                m = mm(PE, B[bk][:, c * 256:c * 256 + 256], ctxT[0:64, (2 * b + c) * 128:(2 * b + c) * 128 + 128], xv,
                       True, True, [got("m")] + free[bk], c == 1)
            for c in range(2):
                m2 = acopy(A, va[s][:, c, :, 0:16], B[bk][:, c * 256:c * 256 + 256].rearrange("p (h d) -> p h d", d=16),
                           [m, t_v1] + w)
            free[bk] = [m2]
            pre[b] = toks + [m2]
            yield

        def xpair(b, bk, dsts):
            for i, t in enumerate((2 * b, 2 * b + 1)):
                for c in range(2):
                    a = tr(PE, B[bk][:, (2 * c + i) * 128:(2 * c + i) * 128 + 128], xh[:, t, c * 128:(c + 1) * 128],
                           ident[:, :], [xh_t[t]] + free[bk], i == 1 and c == 1)
            src = B[bk][:, :].rearrange("p (c n) -> p c n", c=2)
            r = dsts(src, a)
            free[bk] = r
            return r

        def l1x_pre(b):
            s = b % 2
            bk = xbank(b)[4]
            bs = slice(b * 256, b * 256 + 256)
            yield from lnx((2 * b, 2 * b + 1), [x3_t[2 * b], x3_t[2 * b + 1]])
            a = xpair(b, bk, lambda src, a: [acopy(A, xT[:, :, bs], src, [a])])
            yield
            w = [last_S[b - 2]] if b >= 2 else []
            for g in range(2):
                for cc in range(2):
                    c = 2 * g + cc
                    for k in range(2):
                        m = mm(PE, B[bk][:, cc * 256:cc * 256 + 256], xq[:, k, c, :], xT[:, k, bs],
                               k == 0, k == 1, a + [got("l")] + free[bk], k == 1 and cc == 1)
                m = acopy(A, qT_[s][:, 2 * g:2 * g + 2, :], B[bk][:, :].rearrange("p (c n) -> p c n", c=2), [m] + w)
                free[bk] = [m]
                pre[b].append(m)
                if g == 0:
                    yield
            preq[b] = True
            yield

        preq = {}

        def xs_step(b, h):
            i = b * 16 + h
            s = b % 2
            c, j = divmod(h, 4)
            bk = xbank(b)[i % 2]
            r = slice(32 * j, 32 * j + 32)
            Q = qT_[s][r, c, :]
            Kk = kT_[s][r, c, :]
            mm(PE, B[bk][:, 0:384], identb[:, :], negx, True, False, pre[b] + free[bk] + [t_ng])
            mm(PE, B[bk][:, 0:128], Q[:, 0:128], Kk[:, 0:128], False, True)
            a = mm(PE, B[bk][:, 128:384], Q[:, 128:256], Kk[:, 0:256], False, True, (), True)
            last_S[b] = a
            m = i % 4
            w = [a] + ([xP[i - 4]] if i >= 4 else [])
            red(V, mxx[m][:, 0:1], B[bk][:, 0:128], ALU.max, w)
            a = red(V, mxx[m][:, 1:2], B[bk][:, 128:384], ALU.max)
            a = tsc(V, mxx[m][:, 2:4], mxx[m][:, 0:2], -SX, None, ALU.mult, w=[a])
            w = [a] + ([xT_t[i - 4]] if i >= 4 else [])
            act(A, Px[m][:, 0, :], B[bk][:, 0:128], ACT.Exp, w, bias=mxx[m][:, 2:3], scale=SX)
            a = act(A, Px[m][:, 1:3, :].rearrange("p a b -> p (a b)"), B[bk][:, 128:384], ACT.Exp, (),
                    bias=mxx[m][:, 3:4], scale=SX)
            free[bk] = [a]
            xP[i] = a

        def xt_step(b, h):
            i = b * 16 + h
            m = i % 4
            bk = xbank(b)[2]
            for c in range(3):
                a = tr(PE, B[bk][:, c * 128:c * 128 + 128], Px[m][:, c, :], ident[:, :], [xP[i]] + free[bk], c == 2)
            xT_t[i] = a
            w = [a] + ([xPV[i - 4]] if i >= 4 else [])
            a = acopy(A, PTx[m], B[bk][:, 0:384].rearrange("p (c n) -> p c n", c=3), w)
            free[bk] = [a]
            xPT[i] = a

        def xpv_step(b, h):
            i = b * 16 + h
            s = b % 2
            m = i % 4
            c, j = divmod(h, 4)
            bk = xbank(b)[3]
            o = B[bk][32 * j:32 * j + 17, 0:256]
            mm(PE, o, va[s][:, 0, h, :], PTx[m][:, 0:2, :], True, False, [xPT[i]] + free[bk])
            a = mm(PE, o[:, 128:256], va[s][:, 1, h, :], PTx[m][:, 2, :], False, True, (), True)
            xPV[i] = a
            last_PV[b] = a
            for_rows = slice(32 * j, 32 * j + 17)
            a = cp(V, OxT[s][for_rows, c, :], o, [a, t_ox] + ([ox_t[b - 2]] if b >= 2 else []))
            free[bk] = [a]
            ot_t[b] = a

        def x_end(b):
            bk = 6 if b < 2 else 1
            for qc in range(2):
                for c in range(4):
                    m = tr(PE, B[bk][:, c * 128:c * 128 + 128], OxT[b % 2][:, c, qc * 128:qc * 128 + 128], ident[:, :],
                           [ot_t[b]] + free[bk], c == 3)
                if qc == 1:
                    ox_t[b] = m
                src = B[bk][:, :].rearrange("p (h d) -> p h d", d=32)
                a = rec(V, rcx[:, qc, :], src[:, :, 16], [m])
                a = tt(V, Ox[:, qc, :].rearrange("p (h d) -> p h d", d=16), src[:, :, 0:16],
                       rcx[:, qc, :].rearrange("p (h o) -> p h o", o=1).to_broadcast([128, 16, 16]), ALU.mult,
                       [a] + ([on_t[b - 1]] if b - 1 in on_t else []))
                free[bk] = [a]
                yield
            for c in range(2):
                for qc in range(2):
                    m = tr(PE, B[bk][:, c * 256 + qc * 128:c * 256 + qc * 128 + 128], Ox[:, qc, c * 128:c * 128 + 128],
                           ident[:, :], [a] + free[bk], c == 1 and qc == 1)
            on_t[b] = m
            m = acopy(A, OTx, B[bk][:, :].rearrange("p (c n) -> p c n", c=2), [m] + ([x4_pe[b - 1]] if b - 1 in x4_pe else []))
            free[bk] = [m]
            yield
            for qc in range(2):
                for k in range(2):
                    a = mm(PE, B[bk][:, qc * 256:qc * 256 + 256], OTx[:, k, qc * 128:qc * 128 + 128], xo[:, k, :],
                           k == 0, k == 1, [m] + free[bk], k == 1 and qc == 1)
            x4_pe[b] = a
            xv_ = x[:, 2 * b:2 * b + 2, :]
            a = tt(V, xv_, B[bk][:, :].rearrange("p (q n) -> p q n", q=2), xv_, ALU.add, [a])
            free[bk] = [a]
            x4_t[b] = a
            yield

        x4_pe = {}

        def l1x(bs, extra_):
            heads = [(b, h) for b in bs for h in range(16)]

            def extra():
                if extra_ and next(extra_[0], "end") == "end":
                    extra_.pop(0)

            def ask():
                for b in bs:
                    if b not in asked and 2 * b + 1 in x3_t:
                        asked.append(b)
                        extra_.append(l1x_pre(b))

            asked = []
            for i in range(len(heads) + 5):
                if i < len(heads):
                    b = heads[i][0]
                    while b not in preq:
                        ask()
                        extra()
                        yield
                if 2 <= i <= len(heads) + 1:
                    xt_step(*heads[i - 2])
                if i >= 5:
                    xpv_step(*heads[i - 5])
                    b, hd = heads[i - 5]
                    if hd == 15:
                        if b + 2 < 4:
                            extra_.append(l1x_kv(b + 2))
                        extra_.append(x_end(b))
                        extra_.append(router(b))
                if i < len(heads):
                    xs_step(*heads[i])
                    if i % 16 >= 4:
                        ask()
                yield
                if extra_:
                    extra()
                    yield

        xTm = xT
        p30 = [c2(30) for _ in range(2)]
        r30 = [c2(30) for _ in range(2)]
        m8b = [c2(8) for _ in range(2)]
        rr = [c2(4) for _ in range(2)]
        cwr = [c2(28) for _ in range(2)]
        cwp = [sb(f"cwp{i}", [128, 3, 28], BF16) for i in range(2)]
        cwT = [fg[0:84, 3840:4096].bitcast(BF16), fwo_[0:84, 2048:2304].bitcast(BF16)]
        for i in range(2):
            G.add(lambda e, i=i: e.memset(p30[i][:, 28:29], 2.0))
            t_pad = G.add(lambda e, i=i: e.memset(p30[i][:, 29:30], 3.0))
        cw_t, cwc_t, xs_t = {}, {}, {}

        def router(b):
            tl = (2 * b, 2 * b + 1)
            hf, c0 = divmod(b, 2)
            bk = 6 if b < 2 else 1
            hs = slice(c0 * 256, c0 * 256 + 256)
            yield from lnx(tl, [x4_t[b]])

            def parts(src, a):
                f = acopy(A, xT[:, :, b * 256:b * 256 + 256], src, [a])
                h_ = acopy(A, xTh[hf][:, :, hs], src)
                rest.append(tt(G, xTl[hf][:, :, hs], xT[:, :, b * 256:b * 256 + 256], xTh[hf][:, :, hs], ALU.subtract, [h_]))
                rest.append(f)
                return [h_]

            rest = []
            xpair(b, bk, parts)
            xs_t[b] = rest[0:1]
            yield
            a = rest[1:2]
            for s, t in enumerate(tl):
                for k in range(2):
                    m = mm(PE, B[bk][:, s * 32:s * 32 + 28], xT[:, k, t * 128:t * 128 + 128], gt[:, k, :], k == 0, k == 1,
                           a + free[bk], k == 1)
            for s, t in enumerate(tl):
                lg = B[bk][:, s * 32:s * 32 + 28]
                m = V.add(lambda e, s=s, lg=lg: e.tensor_reduce(rr[s][:, 0:1], lg, X, ALU.max, negate=True), [m])
            for s, t in enumerate(tl):
                lg = B[bk][:, s * 32:s * 32 + 28]
                a = act(A, p30[s][:, 0:28], lg, ACT.Exp, [m, t_pad], bias=rr[s][:, 0:1], accum=rr[s][:, 1:2])
            free[bk] = [a]
            yield
            tk = [[a], [a]]
            for f in (lambda s, w: rec(V, rr[s][:, 2:3], rr[s][:, 1:2], w),
                      lambda s, w: tsc(V, p30[s][:, 0:28], p30[s][:, 0:28], rr[s][:, 2:3], None, ALU.mult, w=w),
                      lambda s, w: V.add(lambda e: e.max(m8b[s], p30[s]), w),
                      lambda s, w: V.add(lambda e: e.match_replace(r30[s], m8b[s], p30[s], 0.0), w),
                      lambda s, w: tt(V, r30[s][:, 0:28], p30[s][:, 0:28], r30[s][:, 0:28], ALU.subtract, w),
                      lambda s, w: red(V, rr[s][:, 3:4], r30[s][:, 0:28], ALU.add, w),
                      lambda s, w: tsc(V, rr[s][:, 3:4], rr[s][:, 3:4], 1e-20, None, ALU.add, w=w),
                      lambda s, w: rec(V, rr[s][:, 3:4], rr[s][:, 3:4], w),
                      lambda s, w: tsc(V, cwr[s], r30[s][:, 0:28], rr[s][:, 3:4], None, ALU.mult, w=w),
                      lambda s, w: cp(V, cwp[s][:, 0, :], cwr[s], w + ([cw_t[b - 1]] if b else [])),
                      lambda s, w: tt(V, cwr[s], cwr[s], cwp[s][:, 0, :], ALU.subtract, w),
                      lambda s, w: cp(V, cwp[s][:, 1, :], cwr[s], w),
                      lambda s, w: tt(V, cwr[s], cwr[s], cwp[s][:, 1, :], ALU.subtract, w),
                      lambda s, w: cp(V, cwp[s][:, 2, :], cwr[s], w)):
                for s in range(2):
                    tk[s] = [f(s, tk[s])]
            yield
            pb = B[bk][:, :].bitcast(BF16)
            for s in range(2):
                a = tr(PE, pb[0:84, s * 128:s * 128 + 128], cwp[s][:, :, :].rearrange("p a b -> p (a b)"), identb[:, :],
                       tk[s] + free[bk], True)
            cw_t[b] = a
            a = cp(V, cwT[hf][:, hs], pb[0:84, 0:256], [a])
            free[bk] = [a]
            cwc_t[b] = a
            yield

        NR = 2
        ring = [c2(768) for _ in range(NR)]
        thb = [gb[:, :, :].rearrange('p a b -> p (a b)'), sb('thb', [128, 512])[:, :]]
        rd = [DmaSem(sem(f"ring{i}")) for i in range(NR)]
        steps = [(hf, c) for hf in range(2) for c in range(NCH)]
        ring_t, ring_free = {}, [[] for _ in range(NR)]
        usp, dsp, g_t, h_t, hrd, hp_t, up_pe = {}, {}, {}, {}, {}, {}, {}
        LAG = 2

        def fetch(n):
            if n < len(steps):
                ring_t[n] = rd[n % NR].load(SP, ring[n % NR], D["wmo"][steps[n][1], :, :], ring_free[n % NR])

        def wsplit(n):
            if n < len(steps):
                s, r, d = n % 2, ring[n % NR], n % 4
                w = [ring_t[n]] + ([up_pe[n - 2]] if n >= 2 else [l1_t[7]])
                a = acopy(A, uh_[s][:, :], r[:, 0:512], w)
                b = tt(G, ul_[s][:, :], r[:, 0:512], uh_[s][:, :], ALU.subtract, [a])
                usp[n] = [a, b]
                a = acopy(A, dh_[d][:, :], r[:, 512:768], [hrd[n - 4]] if n >= 4 else [])
                b = tt(G, dl_[d][:, :], r[:, 512:768], dh_[d][:, :], ALU.subtract, [a])
                dsp[n] = [a, b]
                ring_free[n % NR] = [b]
                fetch(n + NR)

        def three(out_, lh, ll, rh, rl, start, stop, w, inc=False):
            mm(PE, out_, lh, rh, start, False, w)
            mm(PE, out_, lh, rl, False, False)
            return mm(PE, out_, ll, rh, False, stop, (), inc)

        def moe_up(n):
            hf, c = steps[n]
            s = n % 2
            Wh = uh_[s][:, :].rearrange("p (j m) -> p j m", m=128)
            Wl = ul_[s][:, :].rearrange("p (j m) -> p j m", m=128)
            bk = [4, 5, 6]
            for u in range(2):
                for k in range(2):
                    a = three(B[bk[u]][:, :], Wh[:, 2 * k + u, :], Wl[:, 2 * k + u, :], xTh[hf][:, k, :], xTl[hf][:, k, :],
                              k == 0, k == 1, usp[n] + xs_t[2 * hf] + xs_t[2 * hf + 1] + free[bk[u]], k == 1)
                if u == 0:
                    w = [a] + ([hp_t[n - 2]] if n >= 2 else [])
                    if hf == 0:
                        t1 = act(A, thb[s], B[4][:, :], ACT.Tanh, w, scale=0.5)
                        t1 = stt(V, thb[s], thb[s], 1.0, B[4][:, :], ALU.add, ALU.mult, [t1])
                    else:
                        t1 = act(A, thb[s], B[4][:, :], ACT.Silu, w)
                    free[bk[0]] = [t1]
                    yield
            up_pe[n] = a
            a = mm(PE, B[bk[2]][:, :], selm[:, c * 128:c * 128 + 128], cwT[hf], True, True,
                   [cwc_t[2 * hf], cwc_t[2 * hf + 1]] + [got("lb")] + free[bk[2]], True)
            gp, up, cb = [B[i][:, :] for i in bk]
            th = thb[s]
            if hf == 0:
                t1 = stt(V, th, th, 0.5, up, ALU.mult, ALU.mult, [t1, a])
            else:
                t1 = tt(V, th, up, th, ALU.mult, [t1, a])
            free[bk[1]] = [t1]
            t1 = tt(V, th, cb, th, ALU.mult, [t1])
            free[bk[2]] = [t1]
            m = n % 3
            w = [t1] + ([hrd[n - 3]] if n >= 3 else [])
            a1 = acopy(A, hh_[m][:, :], th, w)
            a2 = tt(G, hl_[m][:, :], th, hh_[m][:, :], ALU.subtract, [a1])
            hp_t[n] = a2
            h_t[n] = [a1, a2]

        outs = []

        def moe_down(n):
            hf, c = steps[n]
            m = n % 3
            if c == 0:
                for q in range(2):
                    mm(PE, B[2 + q][:, :], zb[0:1, 0:128], zb[0:1, :], True, False, [t_zb] + free[2 + q])
            for q in range(4):
                qs = slice(q * 128, q * 128 + 128)
                a = three(B[2 + q // 2][:, (q % 2) * 256:(q % 2) * 256 + 256], hh_[m][:, qs], hl_[m][:, qs],
                          dh_[n % 4][:, :], dl_[n % 4][:, :], False, c == NCH - 1, h_t[n] + dsp[n], q == 3)
            hrd[n] = a
            if c == NCH - 1:
                for q in range(2):
                    t0 = 4 * hf + 2 * q
                    xv_ = x[:, t0:t0 + 2, :]
                    b = tt(V, xv_, B[2 + q][:, :].rearrange("p (q n) -> p q n", q=2), xv_, ALU.add, [a])
                    free[2 + q] = [b]
                    outs.append(dsems["out"].load(SP, D["outv"][:, t0:t0 + 2, :], xv_, [b]))

        def moe(hf):
            n0 = hf * NCH
            for c in range(NCH + LAG):
                if c < NCH:
                    wsplit(n0 + c + 1)
                    yield from moe_up(n0 + c)
                    yield
                if c >= LAG:
                    moe_down(n0 + c - LAG)
                yield

        dsems["out"] = DmaSem(sem("d_out"))
        for n in range(NR):
            fetch(n)

        def drive(main, side, ratio):
            due = 0.0
            for _ in main:
                due += ratio
                while side is not None and due >= 1.0:
                    due -= 1.0
                    if next(side, "end") == "end":
                        side = None
            return side

        for _ in lnx((2, 3, 4, 5, 6, 7), [a3]):
            pass
        xt_t = {}
        for t in range(8):
            xt_t[t] = xpose(t, [xh_t[t]], 2 + t % 4)
            if t == 1:
                side = l1a_three(range(0, 8))
                next(side)
        kv = [l1x_kv(0), l1x_kv(1)]
        while 1 not in x3_t:
            next(side)
            if kv and next(kv[0], "end") == "end":
                kv.pop(0)
        extra_ = []
        side = drive(l1x((0, 1, 2), extra_), side, 0.95)
        for _ in side or ():
            pass
        while 1 not in cwc_t:
            if next(extra_[0], "end") == "end":
                extra_.pop(0)
        wsplit(0)

        def second():
            yield from l1x((3,), extra_)
            while extra_:
                yield from extra_.pop(0)

        side = drive(moe(0), second(), 0.5)
        for _ in side or ():
            pass
        drive(moe(1), None, 0)
        SP.wait([dsems["out"].all()])
        SP.wait([q.now() for q in (PE, V, A, G)])

        block = ctx.enter_context(nc.Block())

        @block.sync
        def _(e):
            SP.play(e)

        @block.tensor
        def _(e):
            PE.play(e)

        @block.vector
        def _(e):
            V.play(e)

        @block.scalar
        def _(e):
            A.play(e)

        @block.gpsimd
        def _(e):
            G.play(e)


def lay(inp):
    f = np.float32
    i = {k: np.asarray(v) for k, v in inp.items()}
    d = {}

    def kc(w):
        return w.reshape(-1, 128, w.shape[1]).transpose(1, 0, 2)

    def bcast(v):
        return np.broadcast_to(v.reshape(1, -1), (128, v.size))

    d["x"] = i["x"].reshape(8, 128, 256).transpose(1, 0, 2)
    d["ident"] = np.eye(128, dtype=f)
    wk = i["L0_attn_W_DKV_w"].T
    d["wdkv"] = kc(np.concatenate([wk, wk], 1))
    d["wdq"] = kc(i["L0_attn_W_DQ_w"].T)
    cols = np.zeros((128, 8), f)
    cols[:, 0] = np.concatenate([i["L0_attn_W_DKV_b"]] * 2)
    cols[:, 1] = i["L0_attn_W_DQ_b"][0:128]
    cols[0:64, 2] = i["L0_attn_W_DQ_b"][128:192]
    cols[:, 3:5] = i["L0_ffn_ln1_w"].reshape(2, 128).T
    cols[:, 5:7] = i["L0_ffn_ln2_w"].reshape(2, 128).T
    d["cols"] = cols
    d["bkvb"] = bcast(i["L0_attn_W_DKV_b"])
    hd = lambda w: w.reshape(16, 128, -1).transpose(1, 0, 2)
    d["wuq"] = np.concatenate([hd(i["L0_attn_W_UQ_w"]), hd(i["L0_attn_W_UQ_b"])], 2)
    d["wuk"] = np.concatenate([hd(i["L0_attn_W_UK_w"]), hd(i["L0_attn_W_UK_b"])], 2)
    d["wuv"] = hd(i["L0_attn_W_UV_w"])
    d["buv"] = i["L0_attn_W_UV_b"].reshape(16, 128).T
    d["wot"] = hd(i["L0_attn_W_O_w"].T)
    d["bo"] = i["L0_attn_W_O_b"].reshape(1, 256)
    d["ctxT"] = np.concatenate([i["ctx_512"].reshape(1024, 64).T, np.ones((1, 1024), f)], 0)
    d["wk1"] = np.concatenate([i["L0_xattn_W_k"].T, i["L0_xattn_b_k"].reshape(1, 64)], 0)
    d["gb"] = np.stack([bcast(i["L0_xattn_ln_gamma"]), bcast(i["L0_xattn_ln_beta"])], 1)
    d["wrb"] = bcast(i["L0_ffn_w_router"])
    d["utri"] = np.triu(np.ones((128, 128), f))
    d["iota1"] = np.broadcast_to(np.arange(1, 129, dtype=f).reshape(1, 128), (128, 128))
    bf = mybir.dt.np(BF16)
    d["identb"] = np.eye(128, dtype=f).astype(bf)
    neg = np.where(np.tril(np.ones((128, 128), bool)), 0.0, NEG).astype(f)
    d["negm"] = np.broadcast_to(neg.reshape(128, 1, 128), (128, 4, 128)).astype(bf)
    d["bqkv"] = bcast(np.concatenate([i["L0_ffn_bq"], i["L0_ffn_bk"], i["L0_ffn_bv"]]))
    d["wqkv"] = kc(np.concatenate([i["L0_ffn_wq"], i["L0_ffn_wk"], i["L0_ffn_wv"]], 1))
    d["fwo"] = kc(i["L0_ffn_wo"])
    d["fgu"] = kc(np.concatenate([i["L0_ffn_w_gate"], i["L0_ffn_w_up"]], 1))
    d["fwd"] = kc(i["L0_ffn_w_down"])
    inv = (1.0 / np.power(f(10000.0), np.arange(0, 128, 2, dtype=f) / f(128))).astype(f)
    ang = np.arange(256, dtype=f)[:, None] * inv
    d["rope"] = kc(np.concatenate([np.cos(ang), np.sin(ang)], 1).astype(f))
    d["w1q"] = kc(i["L1_attn_w_qkv"].T)
    d["b1q"] = bcast(i["L1_attn_b_qkv"])
    d["w1o"] = kc(i["L1_attn_w_out"].T)
    d["b1o"] = bcast(i["L1_attn_b_out"])

    def pad(w):
        o = np.zeros((w.shape[0], 16, 32), f)
        o[:, :, 0:16] = w.reshape(-1, 16, 16)
        return o.reshape(-1, 4, 128)

    d["xq"] = pad(i["L1_xattn_Wq"].T).reshape(2, 128, 4, 128).transpose(1, 0, 2, 3)
    d["xk"] = pad(i["L1_xattn_Wkv_expand"][0:256].T)
    d["xv"] = i["L1_xattn_Wkv_expand"][256:512].T
    d["xo"] = kc(i["L1_xattn_Wout"].T)
    d["gt"] = kc(i["L1_ffn_gate_weight"].T)
    e = np.zeros((3, 28, NCH * 128), f)
    for k in range(28):
        e[:, k, k * 176:(k + 1) * 176] = 1.0
    d["selm"] = e.reshape(84, NCH * 128).astype(bf)
    w = np.zeros((NCH * 128, 768), f)
    for u, nm in enumerate(("L1_ffn_w_gate", "L1_ffn_w_up")):
        a = i[nm].transpose(0, 2, 1).reshape(4928, 2, 128)
        full = np.zeros((NCH * 128, 2, 128), f)
        full[0:4928] = a
        full = full.reshape(NCH, 128, 2, 128).transpose(0, 3, 2, 1)
        w.reshape(NCH, 128, 6, 128)[:, :, u, :] = full[:, :, 0]
        w.reshape(NCH, 128, 6, 128)[:, :, 2 + u, :] = full[:, :, 1]
    w[0:4928, 512:768] = i["L1_ffn_w_down"].reshape(4928, 256)
    d["wmo"] = w.reshape(NCH, 128, 768)
    return {k: np.ascontiguousarray(v) for k, v in d.items()}


def extra(nc, D, o):
    D["scr"] = nc.dram_tensor("scr", (4, 16, 256, 16), F32).ap()
    D["outv"] = o.rearrange("b (c p) n -> p (b c) n", p=128)


def kernel(**inputs):
    import concourse.bacc as _bacc
    from concourse.bass_utils import run_bass_kernel_spmd as _run

    nc = _bacc.Bacc("TRN2", target_bir_lowering=False, num_devices=1)
    arrays, D = {}, {}
    for name, a in lay(inputs).items():
        arrays[f"in_{name}"] = a
        D[name] = nc.dram_tensor(f"in_{name}", a.shape, mybir.dt.from_np(a.dtype), kind="ExternalInput").ap()
    o = nc.dram_tensor("out_0", (4, 256, 256), F32, kind="ExternalOutput").ap()
    extra(nc, D, o)
    program(nc, D, o)
    r = _run(nc, [arrays], core_ids=[0])
    return r.results[0]["out_0"]
```
